# Optimizing a Trainium2 kernel written in Bass

```python
import numpy as np
import jax
import jax.numpy as jnp

def _softmax(x, axis=-1):
    return jax.nn.softmax(x, axis=axis)

def _gelu(x):
    return jax.nn.gelu(x, approximate=True)

def _silu(x):
    return jax.nn.silu(x)

def _sigmoid(x):
    return jax.nn.sigmoid(x)

def _layernorm(x, axis=-1, eps=1e-05):
    m = jnp.mean(x, axis=axis, keepdims=True)
    v = jnp.var(x, axis=axis, keepdims=True)
    return (x - m) / jnp.sqrt(v + eps)

def _scatter_add(tgt, idx, src, axis=0):
    return tgt.at[idx].add(src)

def _segment_sum(src, seg, n):
    return jax.ops.segment_sum(src, seg, n)
kernel_name = 'mk_seq_preln_d2_jaxref_r4_2d83eb'

def setup_inputs(seed: int=0):
    np.random.seed(seed)
    _w = jnp.asarray

    def _L0_attn_setup():
        import jax, jax.numpy as jnp
        import numpy as np
        D_MODEL = 512
        N_HEADS = 16
        HEAD_DIM = D_MODEL // N_HEADS
        B, T = (2, 512)
        key = jax.random.key(seed)
        ks = jax.random.split(key, 9)
        s = 0.02
        x = jax.random.normal(ks[0], (B, T, D_MODEL), dtype=jnp.float32)
        Wq = jax.random.normal(ks[1], (N_HEADS, D_MODEL, HEAD_DIM), dtype=jnp.float32) * s
        bq = jax.random.normal(ks[2], (N_HEADS, HEAD_DIM), dtype=jnp.float32) * s
        Wk = jax.random.normal(ks[3], (N_HEADS, D_MODEL, HEAD_DIM), dtype=jnp.float32) * s
        bk = jax.random.normal(ks[4], (N_HEADS, HEAD_DIM), dtype=jnp.float32) * s
        Wv = jax.random.normal(ks[5], (N_HEADS, D_MODEL, HEAD_DIM), dtype=jnp.float32) * s
        bv = jax.random.normal(ks[6], (N_HEADS, HEAD_DIM), dtype=jnp.float32) * s
        Wo = jax.random.normal(ks[7], (D_MODEL, D_MODEL), dtype=jnp.float32) * s
        bo = jax.random.normal(ks[8], (D_MODEL,), dtype=jnp.float32) * s
        return {'x': x, 'Wq': Wq, 'bq': bq, 'Wk': Wk, 'bk': bk, 'Wv': Wv, 'bv': bv, 'Wo': Wo, 'bo': bo}
    _L0_attn_in = _L0_attn_setup()

    def _L0_ffn_setup():
        import jax, jax.numpy as jnp
        import numpy as np
        TOP_K = 8

        def _masked_routing(router_logits):
            T, E = router_logits.shape
            sel_w, sel_e = jax.lax.top_k(router_logits, TOP_K)
            sel_w = jax.nn.softmax(sel_w.astype(jnp.float32), axis=1)
            rows = jnp.arange(T)[:, None]
            masked = jnp.zeros((T, E), dtype=jnp.float32).at[rows, sel_e].set(sel_w)
            count = jnp.zeros((E,), dtype=jnp.int32).at[sel_e.reshape(-1)].add(1)
            return (masked, count)
        key = jax.random.key(seed)
        k1, k2, k3, k4, k5 = jax.random.split(key, 5)
        B, S, H, E, I = (1, 512, 512, 32, 192)
        return {'hidden_states': jax.random.normal(k1, (B, S, H), dtype=jnp.float32), 'gate_w': jax.random.normal(k2, (E, H), dtype=jnp.float32) * H ** (-0.5), 'w_gate_proj': jax.random.normal(k3, (E, I, H), dtype=jnp.float32) * H ** (-0.5), 'w_up_proj': jax.random.normal(k4, (E, I, H), dtype=jnp.float32) * H ** (-0.5), 'w_down_proj': jax.random.normal(k5, (E, H, I), dtype=jnp.float32) * I ** (-0.5)}
    _L0_ffn_in = _L0_ffn_setup()

    def _L1_attn_setup():
        import jax, jax.numpy as jnp
        import numpy as np
        D_MODEL = 512
        D_STATE = 64
        D_HEAD = 64
        EXPAND = 2
        CHUNK = 64
        D_INNER = EXPAND * D_MODEL
        N_HEADS = D_INNER // D_HEAD
        PARAM_DIM = 1 + 2 * D_STATE

        def _ssd(a, Bm, Cm, X, Q):
            nb, l = a.shape
            ds = Bm.shape[-1]
            dh = X.shape[-1]
            nc = l // Q
            la = jnp.log(a).reshape(nb, nc, Q)
            cs = jnp.cumsum(la, axis=-1)
            Bc = Bm.reshape(nb, nc, Q, ds)
            Cc = Cm.reshape(nb, nc, Q, ds)
            Xc = X.reshape(nb, nc, Q, dh)
            tri = jnp.tril(jnp.ones((Q, Q), bool))
            L = jnp.where(tri, jnp.exp(cs[..., :, None] - cs[..., None, :]), 0.0)
            scores = jnp.einsum('znid,znjd->znij', Cc, Bc) * L
            y_diag = jnp.einsum('znij,znjh->znih', scores, Xc)
            decay_states = jnp.exp(cs[..., -1:] - cs)
            states = jnp.einsum('znj,znjd,znjh->zndh', decay_states, Bc, Xc)
            A_chunk = jnp.exp(cs[..., -1])

            def step(S, inp):
                Ac, st = inp
                S_prev = S
                return (Ac[:, None, None] * S + st, S_prev)
            S0 = jnp.zeros((nb, ds, dh), a.dtype)
            _, S_prev = jax.lax.scan(step, S0, (A_chunk.T, jnp.moveaxis(states, 1, 0)))
            S_prev = jnp.moveaxis(S_prev, 0, 1)
            y_inter = jnp.einsum('znid,zndh,zni->znih', Cc, S_prev, jnp.exp(cs))
            return (y_diag + y_inter).reshape(nb, l, dh)
        key = jax.random.key(seed)
        k0, k1, k2, k3 = jax.random.split(key, 4)
        x = jax.random.normal(k0, (1, 1024, D_MODEL), jnp.float32)
        w_in = jax.random.normal(k1, (2 * D_INNER, D_MODEL), jnp.float32) * 0.02
        w_param = jax.random.normal(k2, (N_HEADS * PARAM_DIM, D_MODEL), jnp.float32) * 0.02
        w_out = jax.random.normal(k3, (D_MODEL, D_INNER), jnp.float32) * 0.02
        return {'x': x, 'w_in': w_in, 'w_param': w_param, 'w_out': w_out}
    _L1_attn_in = _L1_attn_setup()

    def _L1_ffn_setup():
        import jax, jax.numpy as jnp
        import numpy as np
        HIDDEN = 512
        INTER = 1376
        LUT_SIZE = 16

        def _ghost_linear(x, idx, lut):
            w = lut[idx]
            return jnp.einsum('bsh,oh->bso', x, w)
        key = jax.random.key(seed)
        k_x, k_lut, k_g, k_u, k_d = jax.random.split(key, 5)
        x = jax.random.normal(k_x, (2, 1024, HIDDEN), dtype=jnp.float32)
        lut = jax.random.normal(k_lut, (LUT_SIZE,), dtype=jnp.float32) * 0.02
        gate_idx = jax.random.randint(k_g, (INTER, HIDDEN), 0, LUT_SIZE, dtype=jnp.int32)
        up_idx = jax.random.randint(k_u, (INTER, HIDDEN), 0, LUT_SIZE, dtype=jnp.int32)
        down_idx = jax.random.randint(k_d, (HIDDEN, INTER), 0, LUT_SIZE, dtype=jnp.int32)
        return {'x': x, 'lut': lut, 'gate_idx': gate_idx, 'up_idx': up_idx, 'down_idx': down_idx}
    _L1_ffn_in = _L1_ffn_setup()
    _d = {'L0_attn_x': _L0_attn_in['x'], 'L0_attn_Wq': _L0_attn_in['Wq'], 'L0_attn_bq': _L0_attn_in['bq'], 'L0_attn_Wk': _L0_attn_in['Wk'], 'L0_attn_bk': _L0_attn_in['bk'], 'L0_attn_Wv': _L0_attn_in['Wv'], 'L0_attn_bv': _L0_attn_in['bv'], 'L0_attn_Wo': _L0_attn_in['Wo'], 'L0_attn_bo': _L0_attn_in['bo'], 'L0_ffn_gate_w': _L0_ffn_in['gate_w'], 'L0_ffn_w_gate_proj': _L0_ffn_in['w_gate_proj'], 'L0_ffn_w_up_proj': _L0_ffn_in['w_up_proj'], 'L0_ffn_w_down_proj': _L0_ffn_in['w_down_proj'], 'L1_attn_w_in': _L1_attn_in['w_in'], 'L1_attn_w_param': _L1_attn_in['w_param'], 'L1_attn_w_out': _L1_attn_in['w_out'], 'L1_ffn_lut': _L1_ffn_in['lut'], 'L1_ffn_gate_idx': _L1_ffn_in['gate_idx'], 'L1_ffn_up_idx': _L1_ffn_in['up_idx'], 'L1_ffn_down_idx': _L1_ffn_in['down_idx']}
    _x0 = _d['L0_attn_x']
    _d['L0_attn_x'] = jax.random.normal(jax.random.fold_in(jax.random.key(seed), 1), (2, 1024, 512), dtype=_x0.dtype)
    del _x0
    return _d

def reference(L0_attn_x, L0_attn_Wq, L0_attn_bq, L0_attn_Wk, L0_attn_bk, L0_attn_Wv, L0_attn_bv, L0_attn_Wo, L0_attn_bo, L0_ffn_gate_w, L0_ffn_w_gate_proj, L0_ffn_w_up_proj, L0_ffn_w_down_proj, L1_attn_w_in, L1_attn_w_param, L1_attn_w_out, L1_ffn_lut, L1_ffn_gate_idx, L1_ffn_up_idx, L1_ffn_down_idx):

    def _L0_attn_ref(x, Wq, bq, Wk, bk, Wv, bv, Wo, bo):
        import jax, jax.numpy as jnp
        import numpy as np
        D_MODEL = 512
        N_HEADS = 16
        HEAD_DIM = D_MODEL // N_HEADS
        B, T = (2, 512)
        Bn, Tn, C = x.shape
        H, _, D = Wq.shape
        scale = D ** (-0.5)
        q = jnp.einsum('btc,hcd->bhtd', x, Wq) + bq[None, :, None, :]
        k = jnp.einsum('btc,hcd->bhtd', x, Wk) + bk[None, :, None, :]
        v = jnp.einsum('btc,hcd->bhtd', x, Wv) + bv[None, :, None, :]
        scores = jnp.einsum('bhtd,bhsd->bhts', q, k) * scale
        neg = jnp.finfo(scores.dtype).min
        causal = jnp.triu(jnp.full((Tn, Tn), neg, dtype=scores.dtype), k=1)
        probs = jax.nn.softmax(scores + causal, axis=-1)
        y = jnp.einsum('bhts,bhsd->bhtd', probs, v)
        y = y.transpose(0, 2, 1, 3).reshape(Bn, Tn, H * D)
        return y @ Wo + bo

    def _L0_ffn_ref(hidden_states, gate_w, w_gate_proj, w_up_proj, w_down_proj):
        import jax, jax.numpy as jnp
        import numpy as np
        TOP_K = 8

        def _masked_routing(router_logits):
            T, E = router_logits.shape
            sel_w, sel_e = jax.lax.top_k(router_logits, TOP_K)
            sel_w = jax.nn.softmax(sel_w.astype(jnp.float32), axis=1)
            rows = jnp.arange(T)[:, None]
            masked = jnp.zeros((T, E), dtype=jnp.float32).at[rows, sel_e].set(sel_w)
            count = jnp.zeros((E,), dtype=jnp.int32).at[sel_e.reshape(-1)].add(1)
            return (masked, count)
        B, S, H = hidden_states.shape
        x = hidden_states.reshape(-1, H)
        router_logits = x @ gate_w.T
        masked_w, _count = _masked_routing(router_logits)
        g = jnp.einsum('th,eih->tei', x, w_gate_proj)
        u = jnp.einsum('th,eih->tei', x, w_up_proj)
        h = jax.nn.silu(g) * u
        h = h * masked_w[:, :, None]
        out = jnp.einsum('tei,ehi->th', h, w_down_proj)
        return out.reshape(B, S, H)

    def _L1_attn_ref(x, w_in, w_param, w_out):
        import jax, jax.numpy as jnp
        import numpy as np
        D_MODEL = 512
        D_STATE = 64
        D_HEAD = 64
        EXPAND = 2
        CHUNK = 64
        D_INNER = EXPAND * D_MODEL
        N_HEADS = D_INNER // D_HEAD
        PARAM_DIM = 1 + 2 * D_STATE

        def _ssd(a, Bm, Cm, X, Q):
            nb, l = a.shape
            ds = Bm.shape[-1]
            dh = X.shape[-1]
            nc = l // Q
            la = jnp.log(a).reshape(nb, nc, Q)
            cs = jnp.cumsum(la, axis=-1)
            Bc = Bm.reshape(nb, nc, Q, ds)
            Cc = Cm.reshape(nb, nc, Q, ds)
            Xc = X.reshape(nb, nc, Q, dh)
            tri = jnp.tril(jnp.ones((Q, Q), bool))
            L = jnp.where(tri, jnp.exp(cs[..., :, None] - cs[..., None, :]), 0.0)
            scores = jnp.einsum('znid,znjd->znij', Cc, Bc) * L
            y_diag = jnp.einsum('znij,znjh->znih', scores, Xc)
            decay_states = jnp.exp(cs[..., -1:] - cs)
            states = jnp.einsum('znj,znjd,znjh->zndh', decay_states, Bc, Xc)
            A_chunk = jnp.exp(cs[..., -1])

            def step(S, inp):
                Ac, st = inp
                S_prev = S
                return (Ac[:, None, None] * S + st, S_prev)
            S0 = jnp.zeros((nb, ds, dh), a.dtype)
            _, S_prev = jax.lax.scan(step, S0, (A_chunk.T, jnp.moveaxis(states, 1, 0)))
            S_prev = jnp.moveaxis(S_prev, 0, 1)
            y_inter = jnp.einsum('znid,zndh,zni->znih', Cc, S_prev, jnp.exp(cs))
            return (y_diag + y_inter).reshape(nb, l, dh)
        b, l, _ = x.shape
        xr = x @ w_in.T
        inp, res = (xr[..., :D_INNER], xr[..., D_INNER:])
        params = (x @ w_param.T).reshape(b, l, N_HEADS, PARAM_DIM)
        dt = jax.nn.softplus(params[..., 0])
        a = jnp.exp(-dt)
        Bp = params[..., 1:1 + D_STATE]
        Cp = params[..., 1 + D_STATE:]
        nb = b * N_HEADS
        y = _ssd(a.reshape(nb, l), Bp.reshape(nb, l, D_STATE), Cp.reshape(nb, l, D_STATE), inp.reshape(nb, l, D_HEAD), CHUNK)
        y = y.reshape(b, l, D_INNER)
        out = y * jax.nn.silu(res)
        return out @ w_out.T

    def _L1_ffn_ref(x, lut, gate_idx, up_idx, down_idx):
        import jax, jax.numpy as jnp
        import numpy as np
        HIDDEN = 512
        INTER = 1376
        LUT_SIZE = 16

        def _ghost_linear(x, idx, lut):
            w = lut[idx]
            return jnp.einsum('bsh,oh->bso', x, w)
        gate = _ghost_linear(x, gate_idx, lut)
        up = _ghost_linear(x, up_idx, lut)
        h = jax.nn.silu(gate) * up
        return _ghost_linear(h, down_idx, lut)
    x = L0_attn_x
    x = x + _L0_attn_ref(_layernorm(x, axis=-1), L0_attn_Wq, L0_attn_bq, L0_attn_Wk, L0_attn_bk, L0_attn_Wv, L0_attn_bv, L0_attn_Wo, L0_attn_bo)
    x = x + _L0_ffn_ref(_layernorm(x, axis=-1), L0_ffn_gate_w, L0_ffn_w_gate_proj, L0_ffn_w_up_proj, L0_ffn_w_down_proj)
    x = x + _L1_attn_ref(_layernorm(x, axis=-1), L1_attn_w_in, L1_attn_w_param, L1_attn_w_out)
    x = x + _L1_ffn_ref(_layernorm(x, axis=-1), L1_ffn_lut, L1_ffn_gate_idx, L1_ffn_up_idx, L1_ffn_down_idx)
    return x

_drawn_inputs = setup_inputs


def setup_inputs(seed=0):
    import zlib

    import numpy as np

    out = dict(_drawn_inputs(seed))
    spreads = {}
    factors = {'L0_attn_Wq': 7.226,
     'L0_attn_bq': 8.0,
     'L0_attn_Wk': 7.872,
     'L0_attn_bk': 8.0,
     'L0_attn_bv': 3.985}
    for name, (base, spread) in spreads.items():
        noise = np.random.default_rng([zlib.crc32(name.encode()), seed]).standard_normal(out[name].shape)
        drawn = base * np.exp(spread * noise) if base else spread * noise
        out[name] = jnp.asarray(drawn.astype(out[name].dtype))
    for name, factor in factors.items():
        out[name] = (out[name] * factor).astype(out[name].dtype)
    return out
```

```python
import concourse.bass as bass
from concourse import mybir
from contextlib import ExitStack

STAGES = '1234'

F32 = mybir.dt.float32
I32 = mybir.dt.int32
ALU = mybir.AluOpType
ACT = mybir.ActivationFunctionType
AX = mybir.AxisListType

P = 128
N_TOK = 2048
D = 512
KD = D // P
TILES = N_TOK // P
GROUP = 512
GROUPS = N_TOK // GROUP
LN_EPS = 1e-5
INTER = 1376
JT = -(-INTER // P)
LUT = 16
F32R = mybir.dt.float32r
BF16 = mybir.dt.bfloat16
HEADS = 16
DH = D // HEADS
BATCH = 2
T = N_TOK // BATCH
TB = T // P
SCALE = DH ** -0.5
NEG = -1.0e30


def semaphores(ctx, nc):
    taken = []

    def clear():
        nc.clear_and_free_semaphores(taken)
        with nc.Block():
            pass
    ctx.callback(clear)

    def sem(name):
        taken.append(nc.alloc_semaphore(name))
        return taken[-1]
    return sem


def load_tokens(nc, x_in, x_res, ident):
    with ExitStack() as ctx:
        x_loaded = ctx.enter_context(nc.semaphore("x_loaded"))
        ident_zeroed = ctx.enter_context(nc.semaphore("ident_zeroed"))
        block = ctx.enter_context(nc.Block())

        @block.sync
        def _(sp):
            sp.dma_start(x_res[:, :, :], x_in.rearrange("(n p) d -> p n d", p=P)).then_inc(x_loaded, 16)
            sp.wait_ge(x_loaded, 16)

        @block.gpsimd
        def _(pool):
            pool.memset(ident[:, :], 0.0).then_inc(ident_zeroed, 1)
            pool.wait_ge(ident_zeroed, 1)
            pool.affine_select(out=ident[:, :], in_=ident[:, :], compare_op=ALU.not_equal, fill=1.0,
                               base=0, pattern=[[-1, P]], channel_multiplier=1)


def store_tokens(nc, x_res, out):
    with ExitStack() as ctx:
        stored = ctx.enter_context(nc.semaphore("out_stored"))
        block = ctx.enter_context(nc.Block())

        @block.sync
        def _(sp):
            sp.dma_start(out.rearrange("(n p) d -> p n d", p=P), x_res[:, :, :]).then_inc(stored, 16)
            sp.wait_ge(stored, 16)


def layernorm_transposed(nc, name, x_res, x_hi, x_lo, ident):
    with ExitStack() as ctx:
        stats = ctx.enter_context(nc.sbuf_tensor(name + "_stats", [P, TILES, 6], F32))
        mv = ctx.enter_context(nc.sbuf_tensor(name + "_mv", [P, TILES, 2], F32))
        var_eps = ctx.enter_context(nc.sbuf_tensor(name + "_var_eps", [P, TILES], F32))
        std = ctx.enter_context(nc.sbuf_tensor(name + "_std", [P, TILES], F32))
        rstd = ctx.enter_context(nc.sbuf_tensor(name + "_rstd", [P, TILES], F32))
        xn = ctx.enter_context(nc.sbuf_tensor(name + "_xn", [P, 2, D], F32))
        ps = [ctx.enter_context(nc.psum_tensor(f"{name}_tps{b}", [P, KD, P], F32)) for b in range(2)]
        sem = semaphores(ctx, nc)
        stats_done = sem(name + "_stats_done")
        moments_done = sem(name + "_moments_done")
        std_done = sem(name + "_std_done")
        rstd_done = sem(name + "_rstd_done")
        xn_ready = sem(name + "_xn_ready")
        transposed = sem(name + "_transposed")
        hi_done = sem(name + "_hi_done")
        lo_done = sem(name + "_lo_done")
        block = ctx.enter_context(nc.Block())

        @block.vector
        def _(dve):
            with dve.Fori(0, TILES) as i:
                nc.vector.bn_stats(stats[:, bass.ds(i, 1), :], x_res[:, bass.ds(i, 1), :]).then_inc(stats_done, 1)
            dve.wait_ge(stats_done, TILES)
            for i in range(TILES):
                nc.vector.bn_aggr(mv[:, i, :], stats[:, i, :]).then_inc(moments_done, 1)
            dve.wait_ge(moments_done, TILES)
            nc.vector.tensor_scalar_add(var_eps[:, :], mv[:, :, 1], LN_EPS).then_inc(moments_done, 1)
            dve.wait_ge(std_done, 1)
            nc.vector.reciprocal(rstd[:, :], std[:, :]).then_inc(rstd_done, 1)
            dve.wait_ge(rstd_done, 1)
            dve.sem_inc(lo_done, 2)

            def low_part(i, b):
                dve.wait_ge(hi_done, i + 3)
                toks = bass.ds(i * P, P)
                nc.vector.tensor_tensor(x_lo[:, :, toks], ps[b][:, :, :], x_hi[:, :, toks].bitcast(F32), ALU.subtract).then_inc(lo_done, 1)

            with dve.Fori(0, TILES // 2) as pair:
                for b in range(2):
                    i = pair * 2 + b
                    dve.wait_ge(transposed, i + 1)
                    nc.vector.tensor_scalar(xn[:, b, :], x_res[:, bass.ds(i, 1), :], mv[:, bass.ds(i, 1), 0],
                                            rstd[:, bass.ds(i, 1)], ALU.subtract, ALU.mult).then_inc(xn_ready, 1)
                for b in range(0 if x_lo is None else 2):
                    low_part(pair * 2 + b, b)

        @block.scalar
        def _(act):
            act.sem_inc(hi_done, 2)
            act.wait_ge(moments_done, TILES + 1)
            nc.scalar.activation(std[:, :], var_eps[:, :], ACT.Sqrt).then_inc(std_done, 1)
            with act.Fori(0, TILES // 2) as pair:
                for b in range(2):
                    i = pair * 2 + b
                    act.wait_ge(transposed, i + 3)
                    nc.scalar.copy(x_hi[:, :, bass.ds(i * P, P)], ps[b][:, :, :]).then_inc(hi_done, 1)

        @block.tensor
        def _(pe):
            pe.sem_inc(transposed, 2)
            with pe.Fori(0, TILES // 2) as pair:
                for b in range(2):
                    i = pair * 2 + b
                    pe.wait_ge(xn_ready, i + 1)
                    pe.wait_ge(hi_done if x_lo is None else lo_done, i + 1)
                    for k in range(KD):
                        last = nc.tensor.transpose(ps[b][:, k, :], xn[:, b, k * P:(k + 1) * P], ident[:, :])
                    last.then_inc(transposed, 1)


def split_weights(nc, name, jobs):
    width = max(src.free_size() for src, _, _ in jobs)
    with ExitStack() as ctx:
        stage = [ctx.enter_context(nc.sbuf_tensor(f"{name}_stage{b}", [P, width], F32)) for b in range(2)]
        loaded = [ctx.enter_context(nc.semaphore(f"{name}_loaded{b}")) for b in range(2)]
        hi_done = ctx.enter_context(nc.semaphore(name + "_hi_done"))
        lo_done = ctx.enter_context(nc.semaphore(name + "_lo_done"))
        block = ctx.enter_context(nc.Block())

        def view(n):
            hi = jobs[n][1]
            v = stage[n % 2][:hi.shape[0], :hi.free_size()]
            return v.rearrange("p (a d) -> p a d", a=hi.shape[1]) if len(hi.shape) == 3 else v

        @block.sync
        def _(sp):
            for n, (src, _, _) in enumerate(jobs):
                if n >= 2:
                    sp.wait_ge(lo_done, n - 1)
                sp.dma_start(view(n), src).then_inc(loaded[n % 2], 16)

        @block.scalar
        def _(act):
            for n, (_, hi, _) in enumerate(jobs):
                act.wait_ge(loaded[n % 2], 16 * (n // 2 + 1))
                nc.scalar.copy(hi, view(n)).then_inc(hi_done, 1)

        @block.vector
        def _(dve):
            for n, (_, hi, lo) in enumerate(jobs):
                dve.wait_ge(hi_done, n + 1)
                nc.vector.tensor_tensor(lo, view(n), hi.bitcast(F32), ALU.subtract).then_inc(lo_done, 1)


def attention(nc, x_res, ident, w, b_qkv, wo, bo):
    qk = {n: nc.dram_tensor(f"{n}_parts", (HEADS, 2, DH, N_TOK), F32).ap() for n in "qk"}
    vT = nc.dram_tensor("vT", (HEADS, DH, N_TOK), F32).ap()
    with ExitStack() as ctx:
        x_hi = ctx.enter_context(nc.sbuf_tensor("a_x_hi", [P, KD, N_TOK], F32R))
        x_lo = ctx.enter_context(nc.sbuf_tensor("a_x_lo", [P, KD, N_TOK], F32R))
        w_hi = ctx.enter_context(nc.sbuf_tensor("w_qkv_hi", [P, KD, 3 * D], F32R))
        w_lo = ctx.enter_context(nc.sbuf_tensor("w_qkv_lo", [P, KD, 3 * D], F32R))
        layernorm_transposed(nc, "a_ln", x_res, x_hi, x_lo, ident)
        split_weights(nc, "w_qkv", [(w[k * P:(k + 1) * P, :], w_hi[:, k, :], w_lo[:, k, :]) for k in range(KD)])
        project_qkv(nc, x_hi, x_lo, w_hi, w_lo, b_qkv, qk, vT)
    with ExitStack() as ctx:
        y = ctx.enter_context(nc.sbuf_tensor("att_y", [P, TILES, D], F32))
        attend(nc, y, ident, qk, vT)
        wo_hi = ctx.enter_context(nc.sbuf_tensor("wo_hi", [P, KD, D], F32R))
        wo_lo = ctx.enter_context(nc.sbuf_tensor("wo_lo", [P, KD, D], F32R))
        split_weights(nc, "wo", [(wo.rearrange("(k p) d -> p k d", p=P), wo_hi[:, :, :], wo_lo[:, :, :])])
        output_projection(nc, x_res, y, ident, wo_hi, wo_lo, bo)


def project_qkv(nc, x_hi, x_lo, w_hi, w_lo, b_qkv, qk, vT):
    MT = 3 * D // P
    HT = P // DH
    with ExitStack() as ctx:
        bias = ctx.enter_context(nc.sbuf_tensor("b_qkv_sb", [P, MT], F32))
        hi = ctx.enter_context(nc.sbuf_tensor("qkv_hi", [P, 2, GROUP], F32R))
        lo = ctx.enter_context(nc.sbuf_tensor("qkv_lo", [P, 2, GROUP], F32R))
        v_sb = ctx.enter_context(nc.sbuf_tensor("v_out", [P, 2, GROUP], F32))
        ps = [ctx.enter_context(nc.psum_tensor(f"qkv_ps{i}", [P, GROUP], F32)) for i in range(4)]
        sem = nc.alloc_semaphore
        bias_loaded, product, hi_done, v_done, lo_done = (
            sem("bias_loaded"), sem("product"), sem("hi_done"), sem("v_done"), sem("lo_done"))
        qk_stored = [sem(f"qk_stored{b}") for b in range(2)]
        v_stored = [sem(f"v_stored{b}") for b in range(2)]
        block = ctx.enter_context(nc.Block())
        NQK, NV = 2 * MT // 3, MT // 3

        @block.tensor
        def _(pe):
            with pe.Fori(0, GROUPS) as g:
                for m in range(MT):
                    if m < 4:
                        pe.wait_ge(v_done, g * NV + m + 1)
                    else:
                        pe.wait_ge(lo_done, g * NQK + m - 4 + 1)
                    cols = slice(m * P, (m + 1) * P)
                    toks = bass.ds(g * GROUP, GROUP)
                    terms = [(w_hi, x_hi), (w_lo, x_hi), (w_hi, x_lo)]
                    for n, (k, (a, x)) in enumerate([(k, t) for k in range(KD) for t in terms]):
                        last = nc.tensor.matmul(ps[m % 4][:, :], a[:, k, cols], x[:, k, toks],
                                                start=(n == 0), stop=(n == 3 * KD - 1))
                    last.then_inc(product, 1)

        @block.scalar
        def _(act):
            act.sem_inc(v_done, NV)
            act.sem_inc(qk_stored[0], 32)
            act.sem_inc(qk_stored[1], 32)
            act.sem_inc(v_stored[0], 16)
            act.sem_inc(v_stored[1], 16)
            act.wait_ge(bias_loaded, 16)
            with act.Fori(0, GROUPS) as g:
                for m in range(MT):
                    act.wait_ge(product, g * MT + m + 1)
                    if m < NQK:
                        act.wait_ge(qk_stored[m % 2], (g * (NQK // 2) + m // 2 + 1) * 32)
                        nc.scalar.activation(hi[:, m % 2, :], ps[m % 4][:, :], ACT.Identity,
                                             bias=bias[:, m:m + 1]).then_inc(hi_done, 1)
                    else:
                        act.wait_ge(v_stored[m % 2], (g * (NV // 2) + (m - NQK) // 2 + 1) * 16)
                        nc.scalar.activation(v_sb[:, m % 2, :], ps[m % 4][:, :], ACT.Identity,
                                             bias=bias[:, m:m + 1]).then_inc(v_done, 1)

        @block.vector
        def _(dve):
            with dve.Fori(0, GROUPS) as g:
                for m in range(NQK):
                    dve.wait_ge(hi_done, g * NQK + m + 1)
                    nc.vector.scalar_tensor_tensor(lo[:, m % 2, :], ps[m % 4][:, :], bias[:, m:m + 1],
                                                   hi[:, m % 2, :].bitcast(F32), ALU.add, ALU.subtract).then_inc(lo_done, 1)

        @block.sync
        def _(sp):
            sp.dma_start(bias[:, :], b_qkv).then_inc(bias_loaded, 16)
            with sp.Fori(0, GROUPS) as g:
                toks = bass.ds(g * GROUP, GROUP)
                for m in range(MT):
                    h0 = (m % (MT // 3)) * HT
                    if m < NQK:
                        dst = qk["qk"[m // (MT // 3)]]
                        sp.wait_ge(lo_done, g * NQK + m + 1)
                        for part, buf in ((0, hi), (1, lo)):
                            sp.dma_start(dst[h0:h0 + HT, part, :, toks], buf[:, m % 2, :].bitcast(F32)).then_inc(qk_stored[m % 2], 16)
                    else:
                        sp.wait_ge(v_done, g * NV + m - NQK + 1 + NV)
                        sp.dma_start(vT[h0:h0 + HT, :, toks].rearrange("h d t -> (h d) t"), v_sb[:, m % 2, :]).then_inc(v_stored[m % 2], 16)
            for b in range(2):
                sp.wait_ge(qk_stored[b], 32 * (GROUPS * NQK // 2 + 1))
                sp.wait_ge(v_stored[b], 16 * (GROUPS * NV // 2 + 1))


def attend(nc, y, ident, qk, vT):
    PAIRS = BATCH * HEADS
    ST = 2 * TB
    groups = lambda tb: [(s, min(4, tb + 1 - s)) for s in range(0, tb + 1, 4)]
    with ExitStack() as ctx:
        sb = lambda n, s, dt=F32: ctx.enter_context(nc.sbuf_tensor(n, s, dt))
        q_st, k_st = [sb(f"q_st{b}", [P, T], F32R) for b in range(2)], [sb(f"k_st{b}", [P, T], F32R) for b in range(2)]
        v_st = [sb(f"v_st{b}", [DH, T]) for b in range(2)]
        v_nat = [sb(f"v_nat{b}", [P, TB, DH]) for b in range(2)]
        probs = [sb(f"probs{b}", [P, T]) for b in range(2)]
        pT = [sb(f"probsT{b}", [P, 4, P]) for b in range(4)]
        neg_max, bias, row_sum, inv_sum = sb("neg_max", [P, ST]), sb("exp_bias", [P, ST]), sb("row_sum", [P, ST]), sb("inv_sum", [P, ST])
        scale_col = sb("scale_col", [P, 1])
        ident_bf, mask = sb("ident_bf", [P, P], BF16), sb("causal_mask", [P, P], BF16)
        pb = lambda n, s: ctx.enter_context(nc.psum_tensor(n, s, F32))
        ps_s = [pb(f"ps_s{b}", [P, T]) for b in range(2)]
        ps_t = [pb(f"ps_t{b}", [P, 4, P]) for b in range(2)]
        ps_y = pb("ps_y", [P, 512])[:, :TB * DH].rearrange("p (t d) -> p t d", d=DH)
        ps_v = pb("ps_v", [P, 512])[:, :TB * DH].rearrange("p (t d) -> p t d", d=DH)
        sem = nc.alloc_semaphore
        staged = [sem(f"staged{b}") for b in range(2)]
        loads_begun, v_begun = sem("loads_begun"), sem("v_begun")
        consts, v_transposed, v_ready, scores_done, max_done, bias_ready, exp_done = (
            sem("att_consts"), sem("v_transposed"), sem("v_ready"), sem("scores_done"), sem("max_done"), sem("bias_ready"), sem("exp_done"))
        p_transposed, pT_ready, pv_done, inv_done, y_done = (
            sem("p_transposed"), [sem("pT_ready_act"), sem("pT_ready_dve")], sem("pv_done"), sem("inv_done"), sem("y_done"))
        block = ctx.enter_context(nc.Block())

        GR = [(n, s, c) for n in range(ST) for s, c in groups(n % TB)]
        NG = len(GR)
        assert NG % 4 == 0
        first_group = {n: min(i for i, g in enumerate(GR) if g[0] == n) for n in range(ST)}

        @block.gpsimd
        def _(pool):
            pool.memset(mask[:, :], 0.0).then_inc(consts, 1)
            pool.wait_ge(consts, 1)
            pool.affine_select(out=mask[:, :], in_=mask[:, :], compare_op=ALU.is_ge, fill=NEG,
                               base=0, pattern=[[-1, P]], channel_multiplier=1).then_inc(consts, 1)
            nc.gpsimd.tensor_copy(ident_bf[:, :], ident[:, :]).then_inc(consts, 1)
            pool.memset(scale_col[:, :], SCALE).then_inc(consts, 1)
            pool.wait_ge(consts, 4)
            with pool.Fori(0, PAIRS // 2) as it:
                for n in range(ST):
                    pool.wait_ge(max_done, it * ST + n + 1)
                    nc.gpsimd.tensor_tensor(bias[:, n:n + 1], neg_max[:, n:n + 1], scale_col[:, :], ALU.mult).then_inc(bias_ready, 1)

        @block.sync
        def _(sp):
            with sp.Fori(0, PAIRS // 2) as it:
                for e in range(2):
                    pair = it * 2 + e
                    sp.wait_ge(scores_done, it * ST + (e + 1) * TB)
                    sp.sem_inc(loads_begun, 1)
                    toks = slice(e * T, (e + 1) * T)
                    parts = lambda n, a, b: qk[n][bass.ds(it, 1), a:b, :, toks].rearrange("h a d t -> (h a d) t")
                    for half in range(2):
                        sp.dma_start(q_st[e][half * 64:(half + 1) * 64, :].bitcast(F32), parts("q", 0, 2)).then_inc(staged[e], 16)
                    sp.dma_start(k_st[e][0:64, :].bitcast(F32), parts("k", 0, 2)).then_inc(staged[e], 16)
                    sp.dma_start(k_st[e][64:96, :].bitcast(F32), parts("k", 1, 2)).then_inc(staged[e], 16)
                    sp.dma_start(k_st[e][96:128, :].bitcast(F32), parts("k", 0, 1)).then_inc(staged[e], 16)
                    sp.dma_start(v_st[e][:, :], vT[bass.ds(it, 1), :, toks].rearrange("h d t -> (h d) t")).then_inc(staged[e], 16)

        @block.tensor
        def _(pe):
            pe.sem_inc(scores_done, ST)
            pe.sem_inc(p_transposed, 1)
            pe.sem_inc(pv_done, 1)
            pe.wait_ge(consts, 3)
            with pe.Fori(0, PAIRS // 2) as it:
                def scores(n):
                    e, tb = divmod(n, TB)
                    if tb == 0:
                        pe.wait_ge(staged[e], (it + 1) * 96)
                        pe.wait_ge(v_ready, it * 2 + e + 1)
                        pe.sem_inc(v_begun, 1)
                        for i in range(TB):
                            last = nc.tensor.transpose(ps_v[:, i, :], v_st[e][:, i * P:(i + 1) * P], ident[:DH, :DH])
                        last.then_inc(v_transposed, 1)
                    pe.wait_ge(exp_done, it * ST + n + 1)
                    width = (tb + 1) * P
                    for c in range(0, width, 512):
                        n_c = min(512, width - c)
                        diagonal = c + n_c == width
                        last = nc.tensor.matmul(ps_s[n % 2][:, c:c + n_c], q_st[e][:, tb * P:(tb + 1) * P], k_st[e][:, c:c + n_c],
                                                start=True, stop=not diagonal)
                    last = nc.tensor.matmul(ps_s[n % 2][:, tb * P:width], ident_bf[:, :], mask[:, :], start=False, stop=True)
                    last.then_inc(scores_done, 1)

                scores(0)
                for n in range(ST):
                    e, tb = divmod(n, TB)
                    if n + 1 < ST:
                        scores(n + 1)
                    pe.wait_ge(exp_done, it * ST + n + 3)
                    mine = [i for i, g in enumerate(GR) if g[0] == n]
                    for i in mine:
                        _, s0, c = GR[i]
                        pe.wait_ge(pT_ready[i % 2], it * (NG // 2) + i // 2 + 1)
                        for s in range(c):
                            last = nc.tensor.transpose(ps_t[i % 2][:, s, :], probs[n % 2][:, (s0 + s) * P:(s0 + s + 1) * P], ident[:, :])
                        last.then_inc(p_transposed, 1)
                    if tb == 0:
                        pe.wait_ge(y_done, it * 2 + e + 1)
                        pe.wait_ge(v_ready, it * 2 + e + 2)
                    for i in mine:
                        _, s0, c = GR[i]
                        pe.wait_ge(pT_ready[i % 2], it * (NG // 2) + i // 2 + 2)
                        for s in range(c):
                            last = nc.tensor.matmul(ps_y[:, tb, :], pT[i % 4][:, s, :], v_nat[e][:, s0 + s, :],
                                                    start=(s0 + s == 0), stop=(s0 + s == tb))
                    last.then_inc(pv_done, 1)

        def evacuate(eng, nc_copy, it, i):
            n, s0, c = GR[i]
            eng.wait_ge(p_transposed, it * NG + i + 2)
            if i >= 4:
                eng.wait_ge(pv_done, it * ST + GR[i - 4][0] + 2)
            else:
                eng.wait_ge(pv_done, it * ST + 1)
            nc_copy(pT[i % 4][:, :c, :], ps_t[i % 2][:, :c, :]).then_inc(pT_ready[i % 2], 1)

        @block.scalar
        def _(act):
            act.sem_inc(exp_done, 2)
            act.sem_inc(pT_ready[0], 1)
            act.sem_inc(v_ready, 1)
            with act.Fori(0, PAIRS // 2) as it:
                def step(n):
                    e, tb = divmod(n, TB)
                    if tb == 0:
                        act.wait_ge(v_transposed, it * 2 + e + 1)
                        act.wait_ge(pv_done, it * ST + max(0, n - TB) + 1)
                        nc.scalar.copy(v_nat[e][:, :, :], ps_v[:, :, :]).then_inc(v_ready, 1)
                    width = (tb + 1) * P
                    act.wait_ge(bias_ready, it * ST + n + 1)
                    act.wait_ge(p_transposed, it * NG + (first_group[n - 1] if n > 0 else 0) + 1)
                    nc.scalar.activation(probs[n % 2][:, :width], ps_s[n % 2][:, :width], ACT.Exp, bias=bias[:, n:n + 1], scale=SCALE,
                                         accum_out=row_sum[:, n:n + 1]).then_inc(exp_done, 1)
                step(0)
                for n in range(ST):
                    if n + 1 < ST:
                        step(n + 1)
                    for i, g in enumerate(GR):
                        if g[0] == n and i % 2 == 0:
                            evacuate(act, nc.scalar.copy, it, i)

        @block.vector
        def _(dve):
            dve.sem_inc(pT_ready[1], 1)
            dve.sem_inc(y_done, 1)
            with dve.Fori(0, PAIRS // 2) as it:
                def step(n):
                    dve.wait_ge(scores_done, it * ST + n + 1 + ST)
                    width = (n % TB + 1) * P
                    nc.vector.tensor_reduce(neg_max[:, n:n + 1], ps_s[n % 2][:, :width], AX.X, ALU.max, negate=True).then_inc(max_done, 1)
                step(0)
                for n in range(ST):
                    if n + 1 < ST:
                        step(n + 1)
                    for i, g in enumerate(GR):
                        if g[0] == n and i % 2 == 1:
                            evacuate(dve, nc.vector.tensor_copy, it, i)
                    if n % TB == TB - 1:
                        e = n // TB
                        cols = slice(e * TB, (e + 1) * TB)
                        dve.wait_ge(exp_done, it * ST + n + 3)
                        nc.vector.reciprocal(inv_sum[:, cols], row_sum[:, cols]).then_inc(inv_done, 1)
                        dve.wait_ge(inv_done, it * 2 + e + 1)
                        dve.wait_ge(pv_done, it * ST + n + 2)
                        nc.vector.tensor_tensor(y[:, e * TB:(e + 1) * TB, bass.ds(it * DH, DH)], ps_y[:, :, :],
                                                inv_sum[:, cols].unsqueeze(2).to_broadcast([P, TB, DH]), ALU.mult).then_inc(y_done, 1)


def output_projection(nc, x_res, y, ident, wo_hi, wo_lo, bo):
    with ExitStack() as ctx:
        sb = lambda n, s, dt=F32: ctx.enter_context(nc.sbuf_tensor(n, s, dt))
        y_hi, y_lo = [sb(f"y_hi{b}", [P, KD, P], F32R) for b in range(2)], [sb(f"y_lo{b}", [P, KD, P], F32R) for b in range(2)]
        bo_all = sb("bo_all", [P, D])
        y_st = [sb(f"y_st{b}", [P, D]) for b in range(2)]
        ps_t = [ctx.enter_context(nc.psum_tensor(f"o_ps_t{b}", [P, KD, P], F32)) for b in range(2)]
        ps_o = [ctx.enter_context(nc.psum_tensor(f"o_ps_o{b}", [P, D], F32)) for b in range(2)]
        sem = nc.alloc_semaphore
        bo_loaded, bo_added, transposed, hi_done, lo_done, product, added, staged = (
            sem("bo_loaded"), sem("bo_added"), sem("o_transposed"), sem("o_hi_done"), sem("o_lo_done"), sem("o_product"), sem("o_added"), sem("o_staged"))
        block = ctx.enter_context(nc.Block())

        @block.sync
        def _(sp):
            sp.dma_start(bo_all[:, :], bo.partition_broadcast(P)).then_inc(bo_loaded, 16)

        @block.gpsimd
        def _(pool):
            pool.wait_ge(bo_loaded, 16)
            with pool.Fori(0, TILES) as i:
                nc.gpsimd.tensor_tensor(x_res[:, bass.ds(i, 1), :], x_res[:, bass.ds(i, 1), :], bo_all[:, :], ALU.add).then_inc(bo_added, 1)

        @block.tensor
        def _(pe):
            pe.sem_inc(transposed, 2)
            with pe.Fori(0, TILES // 2) as pair:
                for b in range(2):
                    i = pair * 2 + b
                    pe.wait_ge(staged, i + 1)
                    pe.wait_ge(lo_done, i + 1)
                    for k in range(KD):
                        last = nc.tensor.transpose(ps_t[b][:, k, :], y_st[b][:, k * P:(k + 1) * P], ident[:, :])
                    last.then_inc(transposed, 1)
                    pe.wait_ge(lo_done, i + 3)
                    pe.wait_ge(added, i + 1)
                    terms = [(y_hi[b], wo_hi), (y_lo[b], wo_hi), (y_hi[b], wo_lo)]
                    for n, (k, (yt, w)) in enumerate([(k, t) for k in range(KD) for t in terms]):
                        last = nc.tensor.matmul(ps_o[b][:, :], yt[:, k, :], w[:, k, :], start=(n == 0), stop=(n == 3 * KD - 1))
                    last.then_inc(product, 1)

        @block.scalar
        def _(act):
            act.sem_inc(product, 2)
            with act.Fori(0, TILES // 2) as pair:
                for b in range(2):
                    i = pair * 2 + b
                    act.wait_ge(transposed, i + 3)
                    act.wait_ge(product, i + 1)
                    nc.scalar.copy(y_hi[b][:, :, :], ps_t[b][:, :, :]).then_inc(hi_done, 1)

        @block.vector
        def _(dve):
            dve.sem_inc(lo_done, 2)
            dve.sem_inc(added, 2)
            with dve.Fori(0, TILES // 2) as pair:
                for b in range(2):
                    i = pair * 2 + b
                    dve.wait_ge(transposed, i + 1)
                    nc.vector.tensor_copy(y_st[b][:, :], y[:, bass.ds(i, 1), :]).then_inc(staged, 1)
                    dve.wait_ge(hi_done, i + 1)
                    nc.vector.tensor_tensor(y_lo[b][:, :, :], ps_t[b][:, :, :], y_hi[b][:, :, :].bitcast(F32), ALU.subtract).then_inc(lo_done, 1)
                    dve.wait_ge(product, i + 3)
                    dve.wait_ge(bo_added, i + 1)
                    row = x_res[:, bass.ds(i, 1), :]
                    nc.vector.tensor_tensor(row, ps_o[b][:, :], row, ALU.add).then_inc(added, 1)


EXPERTS = 32
TOP_K = 8
INTER_E = 192
REST_E = INTER_E - P


def mixture_of_experts(nc, x_res, ident, gate_wT, w_gu, w_dn):
    with ExitStack() as ctx:
        x_hi = ctx.enter_context(nc.sbuf_tensor("m_x_hi", [P, KD, N_TOK], F32R))
        x_lo = ctx.enter_context(nc.sbuf_tensor("m_x_lo", [P, KD, N_TOK], F32R))
        routing = ctx.enter_context(nc.sbuf_tensor("routing", [P, TILES, EXPERTS], F32))
        layernorm_transposed(nc, "m_ln", x_res, x_hi, x_lo, ident)
        with ExitStack() as inner:
            gw_hi = inner.enter_context(nc.sbuf_tensor("gw_hi", [P, KD, EXPERTS], F32R))
            gw_lo = inner.enter_context(nc.sbuf_tensor("gw_lo", [P, KD, EXPERTS], F32R))
            split_weights(nc, "gw", [(gate_wT.rearrange("(k p) e -> p k e", p=P), gw_hi[:, :, :], gw_lo[:, :, :])])
            route(nc, x_hi, x_lo, gw_hi, gw_lo, routing)
        experts(nc, x_res, x_hi, x_lo, routing, w_gu, w_dn)


def route(nc, x_hi, x_lo, gw_hi, gw_lo, routing):
    TAKEN = -3.0e38
    with ExitStack() as ctx:
        sb = lambda n, s: ctx.enter_context(nc.sbuf_tensor(n, s, F32))
        logits, shifted, weight = sb("logits", [P, TILES, EXPERTS]), sb("shifted", [P, TILES, EXPERTS]), sb("weight", [P, TILES, EXPERTS])
        rest, chosen = sb("rest", [P, TILES, EXPERTS]), sb("chosen", [P, TILES, EXPERTS])
        top, total, inv = sb("top", [P, TILES, TOP_K]), sb("total", [P, TILES]), sb("inv_total", [P, TILES])
        ps = ctx.enter_context(nc.psum_tensor("ps_logits", [P, TILES, EXPERTS], F32))
        sem = nc.alloc_semaphore
        product, copied, exp_done, step = sem("logits_done"), sem("logits_copied"), sem("r_exp_done"), sem("route_step")
        block = ctx.enter_context(nc.Block())

        @block.tensor
        def _(pe):
            for i in range(TILES):
                toks = slice(i * P, (i + 1) * P)
                terms = [(x_hi, gw_hi), (x_lo, gw_hi), (x_hi, gw_lo)]
                for n, (k, (x, w)) in enumerate([(k, t) for k in range(KD) for t in terms]):
                    last = nc.tensor.matmul(ps[:, i, :], x[:, k, toks], w[:, k, :], start=(n == 0), stop=(n == 3 * KD - 1))
            last.then_inc(product, 1)

        @block.scalar
        def _(act):
            act.wait_ge(product, 1)
            nc.scalar.copy(logits[:, :, :], ps[:, :, :]).then_inc(copied, 1)
            act.wait_ge(step, TILES + 1)
            nc.scalar.activation(weight[:, :, :], shifted[:, :, :], ACT.Exp).then_inc(exp_done, 1)

        @block.vector
        def _(dve):
            dve.wait_ge(copied, 1)
            for i in range(TILES):
                nc.vector.max(top[:, i, :], logits[:, i, :]).then_inc(step, 1)
            dve.wait_ge(step, TILES)
            nc.vector.tensor_tensor(shifted[:, :, :], logits[:, :, :], top[:, :, 0:1].to_broadcast([P, TILES, EXPERTS]), ALU.subtract).then_inc(step, 1)
            for i in range(TILES):
                nc.vector.match_replace(rest[:, i, :], top[:, i, :], logits[:, i, :], TAKEN).then_inc(step, 1)
            dve.wait_ge(step, 2 * TILES + 1)
            nc.vector.tensor_single_scalar(chosen[:, :, :], rest[:, :, :], TAKEN, ALU.is_equal).then_inc(step, 1)
            dve.wait_ge(step, 2 * TILES + 2)
            dve.wait_ge(exp_done, 1)
            nc.vector.tensor_tensor(routing[:, :, :], weight[:, :, :], chosen[:, :, :], ALU.mult).then_inc(step, 1)
            dve.wait_ge(step, 2 * TILES + 3)
            nc.vector.reduce_sum(total[:, :], routing[:, :, :], AX.X).then_inc(step, 1)
            dve.wait_ge(step, 2 * TILES + 4)
            nc.vector.reciprocal(inv[:, :], total[:, :]).then_inc(step, 1)
            dve.wait_ge(step, 2 * TILES + 5)
            nc.vector.tensor_tensor(routing[:, :, :], routing[:, :, :], inv[:, :].unsqueeze(2).to_broadcast([P, TILES, EXPERTS]), ALU.mult)


def experts(nc, x_res, x_hi, x_lo, routing, w_gu, w_dn):
    RUNS = 2 * GROUPS
    SUB = GROUP // P
    BODIES = EXPERTS // 2
    with ExitStack() as ctx:
        sb = lambda n, s, dt=F32: ctx.enter_context(nc.sbuf_tensor(n, s, dt))
        raw_gu, raw_dn = [sb(f"raw_gu{b}", [P, KD, 2 * INTER_E]) for b in range(2)], [sb(f"raw_dn{b}", [P, 2, D]) for b in range(2)]
        gu_hi, gu_lo = [sb(f"gu_hi{b}", [P, KD, 2 * INTER_E], F32R) for b in range(2)], [sb(f"gu_lo{b}", [P, KD, 2 * INTER_E], F32R) for b in range(2)]
        dn_hi, dn_lo = [sb(f"dn_hi{b}", [P, 2, D], F32R) for b in range(2)], [sb(f"dn_lo{b}", [P, 2, D], F32R) for b in range(2)]
        silu = sb("m_silu", [P, 2, GROUP])
        h = [sb(f"m_h{b}", [P, 2, GROUP]) for b in range(2)]
        h_hi, h_lo = [sb(f"m_h_hi{b}", [P, 2, GROUP], F32R) for b in range(2)], [sb(f"m_h_lo{b}", [P, 2, GROUP], F32R) for b in range(2)]
        pb = lambda n: ctx.enter_context(nc.psum_tensor(n, [P, 512], F32))
        ps_g, ps_u, ps_r, ps_o = [[pb(f"m_ps_{c}{b}") for b in range(2)] for c in "guro"]
        sem = nc.alloc_semaphore
        loaded = [sem(f"m_loaded{b}") for b in range(2)]
        w_hi_done, w_lo_done, up_done, silu_done, h_done, hi_done, lo_done, down_done, added = [
            sem("m_" + n) for n in ("w_hi_done", "w_lo_done", "up_done", "silu_done", "h_done", "hi_done", "lo_done", "down_done", "added")]
        block = ctx.enter_context(nc.Block())
        rows = [P, REST_E]

        @block.sync
        def _(sp):
            with sp.Fori(0, BODIES) as it:
                for b in range(2):
                    e = it * 2 + b
                    sp.wait_ge(w_lo_done, e + 1)
                    sp.dma_start(raw_gu[b][:, :, :], w_gu[bass.ds(e, 1), :, :].rearrange("e (k p) i -> p (e k) i", p=P)).then_inc(loaded[b], 16)
                    sp.dma_start(raw_dn[b][:, 0, :], w_dn[bass.ds(e, 1), 0:P, :].rearrange("e i d -> i (e d)")).then_inc(loaded[b], 16)
                    sp.dma_start(raw_dn[b][:REST_E, 1, :], w_dn[bass.ds(e, 1), P:INTER_E, :].rearrange("e i d -> i (e d)")).then_inc(loaded[b], 16)

        @block.tensor
        def _(pe):
            pe.sem_inc(down_done, 2 * SUB)

            def up(it, r):
                n, b, g, r2 = it * RUNS + r, (r // GROUPS) % 2, r % GROUPS, r % 2
                if g == 0:
                    pe.wait_ge(w_lo_done, it * 2 + r // GROUPS + 3)
                pe.wait_ge(h_done, n + 1)
                for ps, c0 in ((ps_g, 0), (ps_u, P), (ps_r, 2 * P)):
                    terms = [(gu_hi[b], x_hi), (gu_lo[b], x_hi), (gu_hi[b], x_lo)]
                    for m, (k, (w, x)) in enumerate([(k, t) for k in range(KD) for t in terms]):
                        last = nc.tensor.matmul(ps[r2][:, :], w[:, k, c0:c0 + P], x[:, k, g * GROUP:(g + 1) * GROUP],
                                                start=(m == 0), stop=(m == 3 * KD - 1))
                last.then_inc(up_done, 1)

            def down(it, r):
                n, b, r2 = it * RUNS + r, r // GROUPS, r % 2
                pe.wait_ge(lo_done, n + 1)
                for s in range(SUB):
                    pe.wait_ge(added, n * SUB + s + 1)
                    toks = slice(s * P, (s + 1) * P)
                    terms = [(h_hi[r2], dn_hi[b]), (h_lo[r2], dn_hi[b]), (h_hi[r2], dn_lo[b])]
                    for m, (k, (a, w)) in enumerate([(k, t) for k in range(2) for t in terms]):
                        last = nc.tensor.matmul(ps_o[s % 2][:, :], a[:rows[k], k, toks], w[:rows[k], k, :], start=(m == 0), stop=(m == 5))
                    last.then_inc(down_done, 1)

            def body(it, final):
                for r in range(RUNS):
                    if not (final and r == RUNS - 1):
                        up(it, r + 1)
                    down(it, r)

            up(0, 0)
            with pe.Fori(0, BODIES - 1) as it:
                body(it, False)
            body(BODIES - 1, True)

        @block.scalar
        def _(act):
            act.sem_inc(silu_done, 1)

            def split_hi(loads, used, b):
                act.wait_ge(loaded[b], loads * 48)
                if used is not None:
                    act.wait_ge(down_done, used * SUB + 2 * SUB)
                nc.scalar.copy(gu_hi[b][:, :, :], raw_gu[b][:, :, :])
                nc.scalar.copy(dn_hi[b][:, 0, :], raw_dn[b][:, 0, :])
                nc.scalar.copy(dn_hi[b][:REST_E, 1, :], raw_dn[b][:REST_E, 1, :]).then_inc(w_hi_done, 1)

            def body(it, final):
                for r in range(RUNS):
                    n, r2 = it * RUNS + r, r % 2
                    act.wait_ge(up_done, n + 1)
                    act.wait_ge(h_done, n + 2)
                    nc.scalar.activation(silu[:, 0, :], ps_g[r2][:, :], ACT.Silu)
                    nc.scalar.activation(silu[P - REST_E:, 1, :], ps_r[r2][:REST_E, :], ACT.Silu).then_inc(silu_done, 1)
                    act.wait_ge(h_done, n + 3)
                    act.wait_ge(down_done, n * SUB + SUB)
                    nc.scalar.copy(h_hi[r2][:, 0, :], h[r2][:, 0, :])
                    nc.scalar.copy(h_hi[r2][:REST_E, 1, :], h[r2][:REST_E, 1, :]).then_inc(hi_done, 1)
                    if r == 0:
                        split_hi(it + 1, it * RUNS, 1)
                    if r == GROUPS and not final:
                        split_hi(it + 2, it * RUNS + GROUPS, 0)

            split_hi(1, None, 0)
            with act.Fori(0, BODIES - 1) as it:
                body(it, False)
            body(BODIES - 1, True)

        @block.vector
        def _(dve):
            dve.sem_inc(h_done, 2)
            dve.sem_inc(added, 2)
            dve.sem_inc(w_lo_done, 2)

            def split_lo(e, b):
                dve.wait_ge(w_hi_done, e + 1)
                nc.vector.tensor_tensor(gu_lo[b][:, :, :], raw_gu[b][:, :, :], gu_hi[b][:, :, :].bitcast(F32), ALU.subtract)
                nc.vector.tensor_tensor(dn_lo[b][:, 0, :], raw_dn[b][:, 0, :], dn_hi[b][:, 0, :].bitcast(F32), ALU.subtract)
                nc.vector.tensor_tensor(dn_lo[b][:REST_E, 1, :], raw_dn[b][:REST_E, 1, :], dn_hi[b][:REST_E, 1, :].bitcast(F32),
                                        ALU.subtract).then_inc(w_lo_done, 1)

            def add_run(it, r):
                n = it * RUNS + r
                for s in range(SUB):
                    i = (r % GROUPS) * SUB + s
                    dve.wait_ge(down_done, n * SUB + s + 1 + 2 * SUB)
                    nc.vector.scalar_tensor_tensor(x_res[:, i, :], ps_o[s % 2][:, :], routing[:, i, bass.ds(it * 2 + r // GROUPS, 1)],
                                                   x_res[:, i, :], ALU.mult, ALU.add).then_inc(added, 1)

            def body(it, final):
                for r in range(RUNS):
                    n, r2 = it * RUNS + r, r % 2
                    dve.wait_ge(silu_done, n + 2)
                    nc.vector.tensor_tensor(h[r2][:, 0, :], ps_u[r2][:, :], silu[:, 0, :], ALU.mult)
                    nc.vector.tensor_tensor(h[r2][:REST_E, 1, :], ps_r[r2][P - REST_E:, :], silu[P - REST_E:, 1, :], ALU.mult).then_inc(h_done, 1)
                    dve.wait_ge(hi_done, n + 1)
                    nc.vector.tensor_tensor(h_lo[r2][:, 0, :], h[r2][:, 0, :], h_hi[r2][:, 0, :].bitcast(F32), ALU.subtract)
                    nc.vector.tensor_tensor(h_lo[r2][:REST_E, 1, :], h[r2][:REST_E, 1, :], h_hi[r2][:REST_E, 1, :].bitcast(F32),
                                            ALU.subtract).then_inc(lo_done, 1)
                    if r > 0:
                        add_run(it, r - 1)
                    if r == 0:
                        split_lo(it * 2 + 1, 1)
                    if r == GROUPS and not final:
                        split_lo(it * 2 + 2, 0)
                add_run(it, RUNS - 1)

            split_lo(0, 0)
            with dve.Fori(0, BODIES - 1) as it:
                body(it, False)
            body(BODIES - 1, True)


STATE = 64
DHEAD = 64
S_HEADS = 16
D_INNER = S_HEADS * DHEAD
M_TILES = S_HEADS + S_HEADS // 2 + D_INNER // P
CHUNK_TOK = P // S_HEADS
CHUNKS = N_TOK // CHUNK_TOK
SEQ_TOK = N_TOK // 2 // S_HEADS
STEPS = SEQ_TOK // CHUNK_TOK
SEQS = 4
S_TOK = SEQS * SEQ_TOK
S_GROUPS = N_TOK // S_TOK


def state_space(nc, x_res, ident, w_proj, w_dt, w_out):
    proj = nc.dram_tensor("proj", (M_TILES, P, N_TOK), F32).ap()
    z_dram = nc.dram_tensor("z_dt", (N_TOK, S_HEADS), F32).ap()
    cs_dram = nc.dram_tensor("log_decay", (CHUNKS, P), F32).ap()
    with ExitStack() as ctx:
        x_hi = ctx.enter_context(nc.sbuf_tensor("s_x_hi", [P, KD, N_TOK], F32R))
        x_lo = ctx.enter_context(nc.sbuf_tensor("s_x_lo", [P, KD, N_TOK], F32R))
        layernorm_transposed(nc, "s_ln", x_res, x_hi, x_lo, ident)
        with ExitStack() as inner:
            dt_hi = inner.enter_context(nc.sbuf_tensor("dt_hi", [P, KD, S_HEADS], F32R))
            dt_lo = inner.enter_context(nc.sbuf_tensor("dt_lo", [P, KD, S_HEADS], F32R))
            split_weights(nc, "dt", [(w_dt.rearrange("(k p) h -> p k h", p=P), dt_hi[:, :, :], dt_lo[:, :, :])])
            project_dt(nc, x_hi, x_lo, dt_hi, dt_lo, z_dram)
        project_tiles(nc, x_hi, x_lo, w_proj, proj)
    with ExitStack() as ctx:
        csT = ctx.enter_context(nc.sbuf_tensor("csT", [P, CHUNKS], F32))
        decay = ctx.enter_context(nc.sbuf_tensor("decay", [P, CHUNKS], F32))
        a_chunk = ctx.enter_context(nc.sbuf_tensor("a_chunk", [P, CHUNKS], F32))
        mask = ctx.enter_context(nc.sbuf_tensor("scan_mask", [P, P], F32))
        scan_mask(nc, ident, mask)
        log_decays(nc, ident, z_dram, cs_dram, csT, decay, a_chunk)
        scan(nc, x_res, ident, proj, cs_dram, csT, decay, a_chunk, mask, w_out)


def project_dt(nc, x_hi, x_lo, dt_hi, dt_lo, z_dram):
    with ExitStack() as ctx:
        z = ctx.enter_context(nc.sbuf_tensor("z_sb", [P, TILES, S_HEADS], F32))
        ps = ctx.enter_context(nc.psum_tensor("ps_z", [P, TILES, S_HEADS], F32))
        sem = nc.alloc_semaphore
        product, copied, stored = sem("z_product"), sem("z_copied"), sem("z_stored")
        block = ctx.enter_context(nc.Block())

        @block.tensor
        def _(pe):
            for i in range(TILES):
                toks = slice(i * P, (i + 1) * P)
                terms = [(x_hi, dt_hi), (x_lo, dt_hi), (x_hi, dt_lo)]
                for n, (k, (x, w)) in enumerate([(k, t) for k in range(KD) for t in terms]):
                    last = nc.tensor.matmul(ps[:, i, :], x[:, k, toks], w[:, k, :], start=(n == 0), stop=(n == 3 * KD - 1))
            last.then_inc(product, 1)

        @block.scalar
        def _(act):
            act.wait_ge(product, 1)
            nc.scalar.copy(z[:, :, :], ps[:, :, :]).then_inc(copied, 1)

        @block.sync
        def _(sp):
            sp.wait_ge(copied, 1)
            sp.dma_start(z_dram.rearrange("(n p) h -> p n h", p=P), z[:, :, :]).then_inc(stored, 16)
            sp.wait_ge(stored, 16)


def project_tiles(nc, x_hi, x_lo, w_proj, proj):
    with ExitStack() as ctx:
        sb = lambda n, s, dt=F32: ctx.enter_context(nc.sbuf_tensor(n, s, dt))
        raw = [sb(f"s_raw{b}", [P, KD, P]) for b in range(2)]
        w_hi, w_lo = [sb(f"s_w_hi{b}", [P, KD, P], F32R) for b in range(2)], [sb(f"s_w_lo{b}", [P, KD, P], F32R) for b in range(2)]
        out = [sb(f"s_out{b}", [P, N_TOK]) for b in range(2)]
        ps = [[ctx.enter_context(nc.psum_tensor(f"s_ps{b}{g}", [P, GROUP], F32)) for g in range(GROUPS)] for b in range(2)]
        sem = nc.alloc_semaphore
        loaded, stored = [sem(f"s_loaded{b}") for b in range(2)], [sem(f"s_stored{b}") for b in range(2)]
        hi_done, lo_done, product, even_out, odd_out = sem("s_hi_done"), sem("s_lo_done"), sem("s_product"), sem("s_even_out"), sem("s_odd_out")
        HALF = GROUPS // 2
        stores_begun, splits_begun = sem("s_stores_begun"), sem("s_splits_begun")
        block = ctx.enter_context(nc.Block())

        @block.sync
        def _(sp):
            def load(m, b):
                sp.dma_start(raw[b][:, :, :], w_proj[bass.ds(m, 1), :, :].rearrange("m (k p) c -> p (m k) c", p=P)).then_inc(loaded[b], 16)

            def store(m, b):
                sp.dma_start(proj[bass.ds(m, 1), :, :].rearrange("m p t -> p (m t)"), out[b][:, :]).then_inc(stored[b], 16)

            def body(it, final):
                for b in range(2):
                    m = it * 2 + b
                    if not final:
                        sp.wait_ge(lo_done, m + 1)
                        load(m + 2, b)
                    sp.wait_ge(even_out, (m + 3) * HALF)
                    sp.sem_inc(stores_begun, 1)
                    sp.wait_ge(odd_out, (m + 3) * HALF)
                    store(m, b)

            for b in range(2):
                load(b, b)
            with sp.Fori(0, M_TILES // 2 - 1) as it:
                body(it, False)
            body(M_TILES // 2 - 1, True)
            for b in range(2):
                sp.wait_ge(stored[b], 16 * (M_TILES // 2 + 1))

        @block.gpsimd
        def _(pool):
            with pool.Fori(0, M_TILES // 2) as it:
                for b in range(2):
                    m = it * 2 + b
                    pool.wait_ge(loaded[b], it * 16 + 16)
                    pool.sem_inc(splits_begun, 1)
                    pool.wait_ge(product, m * GROUPS + GROUPS)
                    pool.sem_inc(splits_begun, 1)
                    nc.gpsimd.tensor_copy(w_hi[b][:, :, :], raw[b][:, :, :]).then_inc(hi_done, 1)
                    pool.wait_ge(hi_done, m + 1)
                    nc.gpsimd.tensor_tensor(w_lo[b][:, :, :], raw[b][:, :, :], w_hi[b][:, :, :].bitcast(F32), ALU.subtract).then_inc(lo_done, 1)

        @block.tensor
        def _(pe):
            pe.sem_inc(product, 2 * GROUPS)
            with pe.Fori(0, M_TILES // 2) as it:
                for b in range(2):
                    m = it * 2 + b
                    pe.wait_ge(lo_done, m + 1)
                    for g in range(GROUPS):
                        pe.wait_ge(even_out if g % 2 == 0 else odd_out, m * HALF + g // 2 + 1)
                        terms = [(w_hi[b], x_hi), (w_lo[b], x_hi), (w_hi[b], x_lo)]
                        for n, (k, (w, x)) in enumerate([(k, t) for k in range(KD) for t in terms]):
                            last = nc.tensor.matmul(ps[b][g][:, :], w[:, k, :], x[:, k, g * GROUP:(g + 1) * GROUP],
                                                    start=(n == 0), stop=(n == 3 * KD - 1))
                        last.then_inc(product, 1)

        @block.scalar
        def _(act):
            for b in range(2):
                act.sem_inc(stored[b], 16)
            act.sem_inc(even_out, 2 * HALF)
            with act.Fori(0, M_TILES // 2) as it:
                for b in range(2):
                    m = it * 2 + b
                    act.wait_ge(stored[b], it * 16 + 16)
                    for g in range(0, GROUPS, 2):
                        act.wait_ge(product, m * GROUPS + g + 1 + 2 * GROUPS)
                        nc.scalar.copy(out[b][:, g * GROUP:(g + 1) * GROUP], ps[b][g][:, :]).then_inc(even_out, 1)

        @block.vector
        def _(dve):
            dve.sem_inc(odd_out, 2 * HALF)
            with dve.Fori(0, M_TILES // 2) as it:
                for b in range(2):
                    m = it * 2 + b
                    dve.wait_ge(stored[b], it * 16 + 16)
                    for g in range(1, GROUPS, 2):
                        dve.wait_ge(product, m * GROUPS + g + 1 + 2 * GROUPS)
                        nc.vector.tensor_copy(out[b][:, g * GROUP:(g + 1) * GROUP], ps[b][g][:, :]).then_inc(odd_out, 1)


def scan_mask(nc, ident, mask):
    with ExitStack() as ctx:
        order_int = ctx.enter_context(nc.sbuf_tensor("order_int", [P, P], I32))
        order = ctx.enter_context(nc.sbuf_tensor("order", [P, P], F32))
        order_col = ctx.enter_context(nc.sbuf_tensor("order_col", [P, 1], F32))
        ps = ctx.enter_context(nc.psum_tensor("order_ps", [P, 512], F32))
        numbered, step, turned = [ctx.enter_context(nc.semaphore(n)) for n in ("numbered", "order_step", "order_turned")]
        block = ctx.enter_context(nc.Block())

        @block.gpsimd
        def _(pool):
            pool.iota(order_int[:, :], pattern=[[1, S_HEADS], [S_HEADS, CHUNK_TOK]], base=0, channel_multiplier=0).then_inc(numbered, 1)

        @block.vector
        def _(dve):
            dve.wait_ge(numbered, 1)
            nc.vector.tensor_copy(order[:, :], order_int[:, :]).then_inc(step, 1)
            dve.wait_ge(turned, 1)
            nc.vector.tensor_copy(order_col[:, :], ps[:, 0:1]).then_inc(step, 1)
            dve.wait_ge(step, 2)
            nc.vector.tensor_scalar(mask[:, :], order[:, :], order_col[:, :], NEG, ALU.is_lt, ALU.mult)

        @block.tensor
        def _(pe):
            pe.wait_ge(step, 1)
            nc.tensor.transpose(ps[:, 0:P], order[:, :], ident[:, :]).then_inc(turned, 1)


def log_decays(nc, ident, z_dram, cs_dram, csT, decay, a_chunk):
    H = CHUNKS // P
    with ExitStack() as ctx:
        sb = lambda n, s: ctx.enter_context(nc.sbuf_tensor(n, s, F32))
        z, neg_abs, e, l, pos, la, cs, ones = [sb("ld_" + n, [P, H, P]) for n in ("z", "neg_abs", "e", "l", "pos", "la", "cs", "ones")]
        cs_p = sb("ld_cs_p", [P, H, P])
        diff = sb("ld_diff", [P, H, P])
        ps_t = ctx.enter_context(nc.psum_tensor("ld_ps_t", [P, 512], F32))
        ps_l = ctx.enter_context(nc.psum_tensor("ld_ps_l", [P, 512], F32))
        sem = nc.alloc_semaphore
        loaded, step, act_step, pe_step, stored = sem("ld_loaded"), sem("ld_step"), sem("ld_act_step"), sem("ld_pe_step"), sem("ld_stored")
        block = ctx.enter_context(nc.Block())

        @block.sync
        def _(sp):
            sp.dma_start(z[:, :, :], z_dram.rearrange("(a c t) h -> c a (t h)", a=H, t=CHUNK_TOK)).then_inc(loaded, 16)
            sp.wait_ge(step, 7)
            sp.dma_start(cs_dram.rearrange("(a c) i -> c a i", a=H), cs_p[:, :, :]).then_inc(stored, 16)
            sp.wait_ge(stored, 16)

        @block.vector
        def _(dve):
            nc.vector.memset(ones[:, :, :], 1.0).then_inc(step, 1)
            dve.wait_ge(loaded, 16)
            nc.vector.scalar_tensor_tensor(neg_abs[:, :, :], z[:, :, :], -1.0, z[:, :, :], ALU.mult, ALU.min).then_inc(step, 1)
            nc.vector.tensor_scalar_max(pos[:, :, :], z[:, :, :], 0.0).then_inc(step, 1)
            dve.wait_ge(act_step, 2)
            dve.wait_ge(step, 3)
            nc.vector.scalar_tensor_tensor(la[:, :, :], pos[:, :, :], -1.0, l[:, :, :], ALU.mult, ALU.subtract).then_inc(step, 1)
            dve.wait_ge(step, 4)
            for a in range(H):
                nc.vector.tensor_tensor_scan(cs[:, a, :], ones[:, a, :], la[:, a, :], 0.0, ALU.mult, ALU.add).then_inc(step, 1)
            dve.wait_ge(step, 6)
            nc.vector.tensor_copy(cs_p[:, :, :].rearrange("c a (h t) -> c a h t", t=CHUNK_TOK),
                                  cs[:, :, :].rearrange("c a (t h) -> c a h t", t=CHUNK_TOK)).then_inc(step, 1)
            dve.wait_ge(pe_step, 2)
            nc.vector.tensor_copy(csT[:, :], ps_t[:, :CHUNKS]).then_inc(step, 1)
            dve.wait_ge(step, 8)
            nc.vector.tensor_tensor(decay[:, :], ps_l[:, :CHUNKS], csT[:, :], ALU.subtract).then_inc(step, 1)

        @block.scalar
        def _(act):
            act.wait_ge(step, 2)
            nc.scalar.activation(e[:, :, :], neg_abs[:, :, :], ACT.Exp).then_inc(act_step, 1)
            act.wait_ge(act_step, 1)
            nc.scalar.activation(l[:, :, :], e[:, :, :], ACT.Ln, bias=1.0).then_inc(act_step, 1)
            act.wait_ge(step, 9)
            nc.scalar.activation(a_chunk[:, :], ps_l[:, :CHUNKS], ACT.Exp)
            nc.scalar.activation(decay[:, :], decay[:, :], ACT.Exp)

        @block.tensor
        def _(pe):
            pe.wait_ge(step, 7)
            for a in range(H):
                last = nc.tensor.transpose(ps_t[:, a * P:(a + 1) * P], cs_p[:, a, :], ident[:, :])
            last.then_inc(pe_step, 1)
            for a in range(H):
                last = nc.tensor.matmul(ps_l[:, a * P:(a + 1) * P], cs_p[:, a, P - 1:P].to_broadcast([P, P]), ident[:, :], start=True, stop=True)
            last.then_inc(pe_step, 1)


def scan(nc, x_res, ident, proj, cs_dram, csT, decay, a_chunk, mask, w_out):
    N_POS = S_TOK * S_HEADS
    TT = S_TOK // P
    KO = D_INNER // P
    NC = SEQS * STEPS
    PAIRS = S_HEADS // 2
    with ExitStack() as ctx:
        sb = lambda n, s: ctx.enter_context(nc.sbuf_tensor(n, s, F32))
        bx_raw = sb("bx_raw", [P, S_HEADS, S_TOK])
        bx = [sb(f"bx{b}", [P, N_POS]) for b in range(2)]
        c_st = [sb(f"c_st{b}", [STATE, S_HEADS, S_TOK]) for b in range(2)]
        gate = [sb(f"gate{b}", [P, KO, S_TOK]) for b in range(2)]
        cs_all = sb("cs_all", [P, N_POS])
        c_dec = sb("c_dec", [STATE, N_POS])
        expo = [sb(f"expo{b}", [P, SEQS, P]) for b in range(2)]
        att = [sb(f"s_att{b}", [P, SEQS, P]) for b in range(2)]
        b_dec = [sb(f"b_dec{b}", [P, SEQS, STATE]) for b in range(2)]
        x_nat = [sb(f"x_nat{b}", [P, SEQS, DHEAD]) for b in range(2)]
        state = [sb(f"state{b}", [STATE, SEQS, DHEAD]) for b in range(2)]
        state_dec = sb("state_dec", [STATE, SEQS, DHEAD])
        gated = sb("gated", [P, KO, S_TOK])
        w_o = sb("s_w_out_sb", [P, KO, D])
        pb = lambda n: ctx.enter_context(nc.psum_tensor(n, [P, 512], F32))
        ps_sc, ps_bx, ps_o = [[pb(f"s_ps_{c}{b}") for b in range(2)] for c in ("sc", "bx", "o")]
        ps_st, ps_y = pb("s_ps_st"), pb("s_ps_y")
        sem = nc.alloc_semaphore
        w_loaded, cs_loaded = sem("s_w_loaded"), sem("cs_loaded")
        loads_begun, turns_begun = sem("s_loads_begun"), sem("s_turns_begun")
        bx_loaded, bx_ready = sem("bx_loaded"), sem("bx_ready")
        c_loaded, gate_loaded = [[sem(f"{n}_loaded{b}") for b in range(2)] for n in ("c", "gate")]
        bx_done, sc_done, expo_done, exp_done, cdec_exp, cdec_done, silu_done = [
            sem(n) for n in ("bx_done", "sc_done", "expo_done", "s_exp_done", "cdec_exp", "cdec_done", "gate_silu_done")]
        x_out, b_out, att_done, st_done, dec_done, state_done, y_done, gated_done, o_done, o_added = [
            sem(n) for n in ("x_out", "b_out", "att_done", "st_done", "dec_done", "state_done", "y_mm_done", "gated_done", "o_done", "o_added_s")]
        block = ctx.enter_context(nc.Block())

        def chunk(buf, s, k):
            t0 = s * SEQ_TOK + k * CHUNK_TOK
            return buf[:, :, t0:t0 + CHUNK_TOK]

        def heads_of(buf, parity):
            return buf.rearrange("p (h two t) -> p h two t", two=2, t=CHUNK_TOK)[:, :, parity, :]

        @block.sync
        def _(sp):
            sp.dma_start(w_o[:, :, :], w_out.rearrange("(k p) d -> p k d", p=P)).then_inc(w_loaded, 16)
            with sp.Fori(0, S_GROUPS // 2) as it:
                for b in range(2):
                    g = it * 2 + b
                    toks = bass.ds(g * S_TOK, S_TOK)
                    sp.wait_ge(bx_ready, g + 1)
                    sp.sem_inc(loads_begun, 1)
                    sp.dma_start(bx_raw[:, :, :], proj[0:S_HEADS, :, toks].rearrange("h p t -> p h t")).then_inc(bx_loaded, 16)
                    sp.wait_ge(sc_done, g * STEPS + STEPS)
                    sp.sem_inc(loads_begun, 1)
                    sp.dma_start(c_st[b][:, :, :], proj[S_HEADS:S_HEADS + PAIRS, :, toks].rearrange("m (two p) t -> p (m two) t", two=2)).then_inc(c_loaded[b], 16)
                    sp.wait_ge(gated_done, g * STEPS + STEPS)
                    sp.sem_inc(loads_begun, 1)
                    sp.dma_start(gate[b][:, :, :], proj[S_HEADS + PAIRS:M_TILES, :, toks].rearrange("m p t -> p m t")).then_inc(gate_loaded[b], 16)
                    sp.wait_ge(expo_done, g * STEPS + 1)
                    sp.sem_inc(loads_begun, 1)
                    sp.wait_ge(cdec_exp, g + 1)
                    sp.sem_inc(loads_begun, 1)
                    rows = cs_dram[bass.ds(g * NC, NC), :].rearrange("c i -> (c i)")
                    sp.dma_start(cs_all[:, :], rows.partition_broadcast(P)).then_inc(cs_loaded, 16)

        @block.gpsimd
        def _(pool):
            pool.sem_inc(bx_ready, 1)
            with pool.Fori(0, S_GROUPS // 2) as it:
                for b in range(2):
                    g = it * 2 + b
                    pool.wait_ge(bx_loaded, g * 16 + 16)
                    pool.sem_inc(turns_begun, 1)
                    pool.wait_ge(sc_done, g * STEPS + STEPS)
                    pool.sem_inc(turns_begun, 1)
                    nc.gpsimd.tensor_copy(bx[b][:, :].rearrange("p (c h t) -> p c h t", h=S_HEADS, t=CHUNK_TOK),
                                          bx_raw[:, :, :].rearrange("p h (c t) -> p c h t", t=CHUNK_TOK)).then_inc(bx_ready, 1)

        @block.tensor
        def _(pe):
            pe.sem_inc(sc_done, 2 * STEPS)
            pe.sem_inc(y_done, 2)
            pe.sem_inc(o_done, 2)
            pe.wait_ge(w_loaded, 16)

            def prepare(it, b, k):
                g = it * 2 + b
                n = g * STEPS + k
                if k == 0:
                    pe.wait_ge(bx_ready, g + 2)
                pe.wait_ge(b_out, n + 1)
                for s in range(SEQS):
                    last = nc.tensor.transpose(ps_bx[k % 2][:, s * P:(s + 1) * P], bx[b][:, (s * STEPS + k) * P:(s * STEPS + k + 1) * P], ident[:, :])
                last.then_inc(bx_done, 1)
                if k == 0:
                    pe.wait_ge(c_loaded[b], it * 16 + 16)
                pe.wait_ge(att_done, n + 1)
                for s in range(SEQS):
                    last = nc.tensor.matmul(ps_sc[k % 2][:, s * P:(s + 1) * P], bx[b][:STATE, (s * STEPS + k) * P:(s * STEPS + k + 1) * P], chunk(c_st[b], s, k), start=True, stop=True)
                last.then_inc(sc_done, 1)

            def new_states(it, b, k):
                g = it * 2 + b
                n = g * STEPS + k
                pe.wait_ge(b_out, n + 3)
                pe.wait_ge(state_done, g * (STEPS - 1) + k + 1)
                for s in range(SEQS):
                    last = nc.tensor.matmul(ps_st[:STATE, s * DHEAD:(s + 1) * DHEAD], b_dec[k % 2][:, s, :], x_nat[k % 2][:, s, :], start=True, stop=True)
                last.then_inc(st_done, 1)

            def outputs(it, b, k):
                g = it * 2 + b
                n = g * STEPS + k
                if k == 1:
                    pe.wait_ge(cdec_done, g + 1)
                if k > 0:
                    pe.wait_ge(state_done, g * (STEPS - 1) + k + 1)
                pe.wait_ge(gated_done, n + 2 * STEPS)
                pe.wait_ge(att_done, n + 3)
                pe.wait_ge(b_out, n + 3)
                for s in range(SEQS):
                    c0 = (s * STEPS + k) * P
                    for parity in range(2):
                        dst = ps_y[parity * DHEAD:(parity + 1) * DHEAD, s * DHEAD:(s + 1) * DHEAD]
                        last = nc.tensor.matmul(dst, x_nat[k % 2][:, s, :], heads_of(att[k % 2][:, s, :], parity), start=True, stop=(k == 0))
                        if k > 0:
                            last = nc.tensor.matmul(dst, state[k % 2][:, s, :], heads_of(c_dec[:, c0:c0 + P], parity), start=False, stop=True)
                last.then_inc(y_done, 1)

            def project_out(it, b):
                g = it * 2 + b
                pe.wait_ge(gated_done, g * STEPS + 3 * STEPS)
                for tt in range(TT):
                    pe.wait_ge(o_added, g * TT + tt + 1)
                    for k in range(KO):
                        last = nc.tensor.matmul(ps_o[tt][:, :], gated[:, k, tt * P:(tt + 1) * P], w_o[:, k, :], start=(k == 0), stop=(k == KO - 1))
                    last.then_inc(o_done, 1)

            with pe.Fori(0, S_GROUPS // 2) as it:
                for b in range(2):
                    prepare(it, b, 0)
                    for k in range(STEPS):
                        if k + 1 < STEPS:
                            prepare(it, b, k + 1)
                            new_states(it, b, k)
                        outputs(it, b, k)
                    project_out(it, b)

        @block.scalar
        def _(act):
            act.sem_inc(cdec_exp, 1)
            act.sem_inc(x_out, 2)
            with act.Fori(0, S_GROUPS // 2) as it:
                for b in range(2):
                    g = it * 2 + b
                    act.wait_ge(cs_loaded, g * 16 + 16)
                    act.wait_ge(y_done, g * STEPS + 2)
                    nc.scalar.activation(c_dec[:, :], cs_all[:STATE, :], ACT.Exp).then_inc(cdec_exp, 1)
                    for k in range(STEPS):
                        n = g * STEPS + k
                        act.wait_ge(bx_done, n + 1)
                        act.wait_ge(y_done, n + 1)
                        nc.scalar.copy(x_nat[k % 2][:, :, :], ps_bx[k % 2][:, :].rearrange("p (s c) -> p s c", s=SEQS)[:, :, STATE:]).then_inc(x_out, 1)
                        act.wait_ge(expo_done, n + 2)
                        nc.scalar.activation(expo[k % 2][:, :, :], expo[k % 2][:, :, :], ACT.Exp).then_inc(exp_done, 1)
                        if k == 0:
                            act.wait_ge(gate_loaded[b], it * 16 + 16)
                            nc.scalar.activation(gate[b][:, :, :], gate[b][:, :, :], ACT.Silu).then_inc(silu_done, 1)

        @block.vector
        def _(dve):
            dve.sem_inc(expo_done, 1)
            dve.sem_inc(b_out, 2)
            dve.sem_inc(att_done, 2)
            dve.sem_inc(state_done, 1)
            dve.sem_inc(gated_done, 2 * STEPS)
            dve.sem_inc(o_added, 2)

            def add_out(it, b):
                g = it * 2 + b
                for tt in range(TT):
                    dve.wait_ge(o_done, g * TT + tt + 3)
                    row = x_res[:, bass.ds(g * TT + tt, 1), :]
                    nc.vector.tensor_tensor(row, ps_o[tt][:, :], row, ALU.add).then_inc(o_added, 1)

            def weigh(it, b, k):
                g = it * 2 + b
                n = g * STEPS + k
                if k == 0:
                    dve.wait_ge(cs_loaded, g * 16 + 16)
                dve.wait_ge(att_done, n + 1)
                for s in range(SEQS):
                    c = s * STEPS + k
                    last = nc.vector.scalar_tensor_tensor(expo[k % 2][:, s, :], cs_all[:, c * P:(c + 1) * P], csT[:, bass.ds(g * NC + c, 1)],
                                                          mask[:, :], ALU.subtract, ALU.add)
                last.then_inc(expo_done, 1)
                dve.wait_ge(x_out, n + 3)
                dve.wait_ge(y_done, n + 1)
                dec = decay[:, bass.ds(g * NC, NC)].rearrange("p (s k) -> p s k", s=SEQS)[:, :, k:k + 1]
                nc.vector.tensor_tensor(b_dec[k % 2][:, :, :], ps_bx[k % 2][:, :].rearrange("p (s c) -> p s c", s=SEQS)[:, :, :STATE],
                                        dec.to_broadcast([P, SEQS, STATE]), ALU.mult).then_inc(b_out, 1)
                dve.wait_ge(sc_done, n + 1 + 2 * STEPS)
                dve.wait_ge(exp_done, n + 1)
                nc.vector.tensor_tensor(att[k % 2][:, :, :], ps_sc[k % 2][:, :].rearrange("p (s c) -> p s c", s=SEQS), expo[k % 2][:, :, :],
                                        ALU.mult).then_inc(att_done, 1)

            def update_state(it, b, k):
                g = it * 2 + b
                n = g * STEPS + k
                new = ps_st[:STATE, :SEQS * DHEAD].rearrange("p (s c) -> p s c", s=SEQS)
                if k > 0:
                    a = a_chunk[:STATE, bass.ds(g * NC, NC)].rearrange("p (s k) -> p s k", s=SEQS)[:, :, k:k + 1]
                    dve.wait_ge(state_done, g * (STEPS - 1) + k + 1)
                    nc.vector.tensor_tensor(state_dec[:, :, :], state[k % 2][:, :, :], a.to_broadcast([STATE, SEQS, DHEAD]), ALU.mult).then_inc(dec_done, 1)
                dve.wait_ge(y_done, n + 2)
                dve.wait_ge(st_done, g * (STEPS - 1) + k + 1)
                if k > 0:
                    dve.wait_ge(dec_done, g * (STEPS - 2) + k)
                    nc.vector.tensor_tensor(state[(k + 1) % 2][:, :, :], new, state_dec[:, :, :], ALU.add).then_inc(state_done, 1)
                else:
                    nc.vector.tensor_copy(state[1][:, :, :], new).then_inc(state_done, 1)

            def gate_outputs(it, b, k):
                g = it * 2 + b
                n = g * STEPS + k
                if k == 0:
                    dve.wait_ge(silu_done, g + 1)
                    dve.wait_ge(o_done, g * TT + 2)
                dve.wait_ge(y_done, n + 3)
                for s in range(SEQS):
                    last = nc.vector.tensor_tensor(chunk(gated, s, k), ps_y[:, s * DHEAD:(s + 1) * DHEAD].rearrange("p (h t) -> p h t", t=CHUNK_TOK),
                                                   chunk(gate[b], s, k), ALU.mult)
                last.then_inc(gated_done, 1)

            with dve.Fori(0, S_GROUPS // 2) as it:
                for b in range(2):
                    g = it * 2 + b
                    weigh(it, b, 0)
                    for k in range(STEPS):
                        if k + 1 < STEPS:
                            weigh(it, b, k + 1)
                            update_state(it, b, k)
                        if k == 0:
                            dve.wait_ge(cdec_exp, g + 2)
                            dve.wait_ge(c_loaded[b], it * 16 + 16)
                            by_head = c_dec[:, :].rearrange("p (c h t) -> p h c t", h=S_HEADS, t=CHUNK_TOK)
                            nc.vector.tensor_tensor(by_head, by_head, c_st[b][:, :, :].rearrange("p h (c t) -> p h c t", t=CHUNK_TOK),
                                                    ALU.mult).then_inc(cdec_done, 1)
                        gate_outputs(it, b, k)
                        if b == 1 and k == 1:
                            add_out(it, 0)
                add_out(it, 1)


def lut_feed_forward(nc, x_res, ident, lut, gate_idxT, up_idxT, down_idxT):
    with ExitStack() as outer:
        def osb(name, shape, dt=F32):
            return outer.enter_context(nc.sbuf_tensor(name, shape, dt))
        w_gate = osb("w_gate", [P, KD, INTER])
        w_up = osb("w_up", [P, KD, INTER])
        w_down = osb("w_down", [P, JT, D])
        dequantise(nc, lut, gate_idxT, up_idxT, down_idxT, w_gate, w_up, w_down)
        xnT = osb("f_xnT", [P, KD, N_TOK])
        layernorm_transposed(nc, "f_ln", x_res, xnT, None, ident)
        with ExitStack() as ctx:
            silu_g = ctx.enter_context(nc.sbuf_tensor("silu_g", [P, 2, GROUP], F32))
            hT = ctx.enter_context(nc.sbuf_tensor("hT", [P, JT, GROUP], F32))
            ps_g = [ctx.enter_context(nc.psum_tensor(f"ps_g{b}", [P, GROUP], F32)) for b in range(2)]
            ps_u = [ctx.enter_context(nc.psum_tensor(f"ps_u{b}", [P, GROUP], F32)) for b in range(2)]
            ps_d = [ctx.enter_context(nc.psum_tensor(f"ps_d{b}", [P, D], F32)) for b in range(2)]
            sem = nc.alloc_semaphore
            gate_done, up_done, silu_done, h_ready = sem("gate_done"), sem("up_done"), sem("silu_done"), sem("h_ready")
            down_done, added = sem("down_done"), sem("added")
            block = ctx.enter_context(nc.Block())
            rows = [min(P, INTER - j * P) for j in range(JT)]
            SUB = GROUP // P

            @block.tensor
            def _(pe):
                pe.sem_inc(down_done, 1)
                with pe.Fori(0, GROUPS // 2) as g2:
                    for gb in range(2):
                        g = g2 * 2 + gb
                        for j in range(JT):
                            b = (gb * JT + j) % 2
                            cols = slice(j * P, j * P + rows[j])
                            pe.wait_ge(silu_done, g * JT + j + 1)
                            for k in range(KD):
                                last = nc.tensor.matmul(ps_g[b][:rows[j], :], w_gate[:, k, cols], xnT[:, k, bass.ds(g * GROUP, GROUP)],
                                                        start=(k == 0), stop=(k == KD - 1))
                            last.then_inc(gate_done, 1)
                            pe.wait_ge(h_ready, g * JT + j + 1)
                            for k in range(KD):
                                last = nc.tensor.matmul(ps_u[b][:rows[j], :], w_up[:, k, cols], xnT[:, k, bass.ds(g * GROUP, GROUP)],
                                                        start=(k == 0), stop=(k == KD - 1))
                            last.then_inc(up_done, 1)
                        for s in range(SUB):
                            pe.wait_ge(added, g * SUB + s + 1)
                            for j in range(JT):
                                pe.wait_ge(h_ready, g * JT + j + 3)
                                last = nc.tensor.matmul(ps_d[s % 2][:, :], hT[:rows[j], j, s * P:(s + 1) * P], w_down[:rows[j], j, :],
                                                        start=(j == 0), stop=(j == JT - 1))
                            last.then_inc(down_done, 1)

            @block.scalar
            def _(act):
                act.sem_inc(silu_done, 2)
                with act.Fori(0, GROUPS // 2) as g2:
                    for gb in range(2):
                        for j in range(JT):
                            b = (gb * JT + j) % 2
                            n = (g2 * 2 + gb) * JT + j
                            act.wait_ge(gate_done, n + 1)
                            act.wait_ge(h_ready, n + 1)
                            nc.scalar.activation(silu_g[:rows[j], b, :], ps_g[b][:rows[j], :], ACT.Silu).then_inc(silu_done, 1)

            @block.vector
            def _(dve):
                dve.sem_inc(h_ready, 2)
                dve.sem_inc(added, 2)
                with dve.Fori(0, GROUPS // 2) as g2:
                    for gb in range(2):
                        g = g2 * 2 + gb
                        for j in range(JT):
                            b = (gb * JT + j) % 2
                            n = g * JT + j
                            dve.wait_ge(silu_done, n + 3)
                            dve.wait_ge(up_done, n + 1)
                            if j == 0:
                                dve.wait_ge(down_done, g * SUB + 1)
                            nc.vector.tensor_tensor(hT[:rows[j], j, :], ps_u[b][:rows[j], :], silu_g[:rows[j], b, :],
                                                    ALU.mult).then_inc(h_ready, 1)
                        for s in range(SUB):
                            dve.wait_ge(down_done, g * SUB + s + 2)
                            row = x_res[:, bass.ds(g * SUB + s, 1), :]
                            nc.vector.tensor_tensor(row, ps_d[s % 2][:, :], row, ALU.add).then_inc(added, 1)


def dequantise(nc, lut, gate_idxT, up_idxT, down_idxT, w_gate, w_up, w_down):
    CH = INTER
    with ExitStack() as ctx:
        lut_all = ctx.enter_context(nc.sbuf_tensor("lut_all", [P, LUT], F32))
        idx = ctx.enter_context(nc.sbuf_tensor("idx", [P, 2, CH], I32))
        term = ctx.enter_context(nc.sbuf_tensor("term", [P, 2, CH], F32))
        sem = nc.alloc_semaphore
        lut_loaded, summed, term_ready = sem("lut_loaded"), sem("summed"), sem("term_ready")
        idx_loaded = [sem(f"idx_loaded{b}") for b in range(2)]
        block = ctx.enter_context(nc.Block())
        chunks = [(gate_idxT[k * P:(k + 1) * P, :], w_gate[:, k, :], P) for k in range(KD)]
        chunks += [(up_idxT[k * P:(k + 1) * P, :], w_up[:, k, :], P) for k in range(KD)]
        for j in range(0, JT - 1, 2):
            chunks.append((down_idxT[j * P:(j + 2) * P, :].rearrange("(j p) d -> p j d", p=P), w_down[:, j:j + 2, :], P))
        chunks.append((down_idxT[(JT - 1) * P:INTER, :], w_down[:INTER - (JT - 1) * P, JT - 1, :], INTER - (JT - 1) * P))

        def view(buf, b, dst, rows):
            v = buf[:rows, b, :dst.free_size()]
            return v.rearrange("p (j d) -> p j d", j=2) if len(dst.shape) == 3 else v

        @block.sync
        def _(sp):
            sp.dma_start(lut_all[:, :], lut.partition_broadcast(P)).then_inc(lut_loaded, 16)
            for n, (src, dst, rows) in enumerate(chunks):
                if n >= 2:
                    sp.wait_ge(term_ready, LUT * (n - 1))
                sp.dma_start(view(idx, n % 2, dst, rows), src).then_inc(idx_loaded[n % 2], 16)

        @block.vector
        def _(dve):
            dve.wait_ge(lut_loaded, 16)
            m = 0
            for n, (src, dst, rows) in enumerate(chunks):
                dve.wait_ge(idx_loaded[n % 2], 16 * (n // 2 + 1))
                for e in range(LUT):
                    if m >= 2:
                        dve.wait_ge(summed, m - 1)
                    nc.vector.tensor_scalar(view(term, m % 2, dst, rows), view(idx, n % 2, dst, rows), float(e),
                                            lut_all[:rows, e:e + 1], ALU.is_equal, ALU.mult).then_inc(term_ready, 1)
                    m += 1

        @block.gpsimd
        def _(pool):
            m = 0
            for n, (src, dst, rows) in enumerate(chunks):
                for e in range(LUT):
                    pool.wait_ge(term_ready, m + 1)
                    if e == 0:
                        nc.gpsimd.tensor_copy(dst, view(term, m % 2, dst, rows)).then_inc(summed, 1)
                    else:
                        pool.wait_ge(summed, m)
                        nc.gpsimd.tensor_tensor(dst, dst, view(term, m % 2, dst, rows), ALU.add).then_inc(summed, 1)
                    m += 1


def build_program(nc, t, out):
    with ExitStack() as ctx:
        x_res = ctx.enter_context(nc.sbuf_tensor("x_res", [P, TILES, D], F32))
        ident = ctx.enter_context(nc.sbuf_tensor("ident", [P, P], F32))
        load_tokens(nc, t["x"], x_res, ident)
        if '1' in STAGES:
            attention(nc, x_res, ident, t["w_qkv"], t["b_qkv"], t["wo"], t["bo"])
        if '2' in STAGES:
            mixture_of_experts(nc, x_res, ident, t["gate_wT"], t["w_gu"], t["w_dn"])
        if '3' in STAGES:
            state_space(nc, x_res, ident, t["w_proj"], t["w_dt"], t["s_w_out"])
        if '4' in STAGES:
            lut_feed_forward(nc, x_res, ident, t["lut"], t["gate_idxT"], t["up_idxT"], t["down_idxT"])
        store_tokens(nc, x_res, out)


def scan_columns(w_in, w_param):
    import numpy as np
    param = w_param.reshape(S_HEADS, 1 + 2 * STATE, D)
    b_x = np.concatenate([param[:, 1:1 + STATE], w_in[:D_INNER].reshape(S_HEADS, DHEAD, D)], axis=1)
    c_pairs = param[:, 1 + STATE:].reshape(S_HEADS // 2, P, D)
    gate = w_in[D_INNER:].reshape(-1, P, D)
    return {
        "w_proj": np.ascontiguousarray(np.concatenate([b_x, c_pairs, gate]).transpose(0, 2, 1)),
        "w_dt": np.ascontiguousarray(param[:, 0].T),
    }


def expert_columns(gate, up):
    import numpy as np
    return np.ascontiguousarray(np.concatenate([gate[:, :P], up[:, :P], gate[:, P:], up[:, P:]], axis=1).transpose(0, 2, 1))


def lay_out(inputs):
    import numpy as np
    c = np.ascontiguousarray
    a = {k: np.asarray(v) for k, v in inputs.items()}
    return {
        "x": c(a["L0_attn_x"].reshape(N_TOK, D)),
        "w_qkv": c(np.concatenate([a["L0_attn_" + n].transpose(1, 0, 2).reshape(D, D) for n in ("Wq", "Wk", "Wv")], axis=1)),
        "b_qkv": c(np.concatenate([a["L0_attn_" + n].reshape(D) for n in ("bq", "bk", "bv")]).reshape(-1, P).T),
        "wo": c(a["L0_attn_Wo"]),
        "bo": c(a["L0_attn_bo"]),
        "gate_wT": c(a["L0_ffn_gate_w"].T),
        "w_gu": expert_columns(a["L0_ffn_w_gate_proj"], a["L0_ffn_w_up_proj"]),
        "w_dn": c(a["L0_ffn_w_down_proj"].transpose(0, 2, 1)),
        **scan_columns(a["L1_attn_w_in"], a["L1_attn_w_param"]),
        "s_w_out": c(a["L1_attn_w_out"].T),
        "lut": c(a["L1_ffn_lut"]),
        "gate_idxT": c(a["L1_ffn_gate_idx"].T),
        "up_idxT": c(a["L1_ffn_up_idx"].T),
        "down_idxT": c(a["L1_ffn_down_idx"].T),
    }


def kernel(**inputs):
    import concourse.bacc as bacc
    from concourse.bass_utils import run_bass_kernel_spmd

    arrays = lay_out(inputs)
    nc = bacc.Bacc("TRN2", target_bir_lowering=False, num_devices=1)
    t = {n: nc.dram_tensor(n, a.shape, mybir.dt.from_np(a.dtype), kind="ExternalInput").ap() for n, a in arrays.items()}
    out = nc.dram_tensor("out", (N_TOK, D), F32, kind="ExternalOutput").ap()
    build_program(nc, t, out)
    r = run_bass_kernel_spmd(nc, [arrays], core_ids=[0])
    return r.results[0]["out"].reshape(2, N_TOK // 2, D)
```

```python
import concourse.bass as bass
from concourse import mybir
from contextlib import ExitStack

STAGES = '1234'

F32 = mybir.dt.float32
I32 = mybir.dt.int32
ALU = mybir.AluOpType
ACT = mybir.ActivationFunctionType
AX = mybir.AxisListType

P = 128
N_TOK = 2048
D = 512
KD = D // P
TILES = N_TOK // P
GROUP = 512
GROUPS = N_TOK // GROUP
LN_EPS = 1e-5
INTER = 1376
JT = -(-INTER // P)
LUT = 16
F32R = mybir.dt.float32r
BF16 = mybir.dt.bfloat16
HEADS = 16
DH = D // HEADS
BATCH = 2
T = N_TOK // BATCH
TB = T // P
SCALE = DH ** -0.5
NEG = -1.0e30


def semaphores(ctx, nc):
    taken = []

    def clear():
        nc.clear_and_free_semaphores(taken)
        with nc.Block():
            pass
    ctx.callback(clear)

    def sem(name):
        taken.append(nc.alloc_semaphore(name))
        return taken[-1]
    return sem


def load_tokens(nc, x_in, x_res, ident):
    with ExitStack() as ctx:
        x_loaded = ctx.enter_context(nc.semaphore("x_loaded"))
        ident_zeroed = ctx.enter_context(nc.semaphore("ident_zeroed"))
        block = ctx.enter_context(nc.Block())

        @block.sync
        def _(sp):
            sp.dma_start(x_res[:, :, :], x_in.rearrange("(n p) d -> p n d", p=P)).then_inc(x_loaded, 16)
            sp.wait_ge(x_loaded, 16)

        @block.gpsimd
        def _(pool):
            pool.memset(ident[:, :], 0.0).then_inc(ident_zeroed, 1)
            pool.wait_ge(ident_zeroed, 1)
            pool.affine_select(out=ident[:, :], in_=ident[:, :], compare_op=ALU.not_equal, fill=1.0,
                               base=0, pattern=[[-1, P]], channel_multiplier=1)


def store_tokens(nc, x_res, out):
    with ExitStack() as ctx:
        stored = ctx.enter_context(nc.semaphore("out_stored"))
        block = ctx.enter_context(nc.Block())

        @block.sync
        def _(sp):
            sp.dma_start(out.rearrange("(n p) d -> p n d", p=P), x_res[:, :, :]).then_inc(stored, 16)
            sp.wait_ge(stored, 16)


def layernorm_transposed(nc, name, x_res, x_hi, x_lo, ident):
    with ExitStack() as ctx:
        stats = ctx.enter_context(nc.sbuf_tensor(name + "_stats", [P, TILES, 6], F32))
        mv = ctx.enter_context(nc.sbuf_tensor(name + "_mv", [P, TILES, 2], F32))
        var_eps = ctx.enter_context(nc.sbuf_tensor(name + "_var_eps", [P, TILES], F32))
        std = ctx.enter_context(nc.sbuf_tensor(name + "_std", [P, TILES], F32))
        rstd = ctx.enter_context(nc.sbuf_tensor(name + "_rstd", [P, TILES], F32))
        xn = ctx.enter_context(nc.sbuf_tensor(name + "_xn", [P, 2, D], F32))
        ps = [ctx.enter_context(nc.psum_tensor(f"{name}_tps{b}", [P, KD, P], F32)) for b in range(2)]
        sem = semaphores(ctx, nc)
        stats_done = sem(name + "_stats_done")
        moments_done = sem(name + "_moments_done")
        std_done = sem(name + "_std_done")
        rstd_done = sem(name + "_rstd_done")
        xn_ready = sem(name + "_xn_ready")
        transposed = sem(name + "_transposed")
        hi_done = sem(name + "_hi_done")
        lo_done = sem(name + "_lo_done")
        block = ctx.enter_context(nc.Block())

        @block.vector
        def _(dve):
            with dve.Fori(0, TILES) as i:
                nc.vector.bn_stats(stats[:, bass.ds(i, 1), :], x_res[:, bass.ds(i, 1), :]).then_inc(stats_done, 1)
            dve.wait_ge(stats_done, TILES)
            for i in range(TILES):
                nc.vector.bn_aggr(mv[:, i, :], stats[:, i, :]).then_inc(moments_done, 1)
            dve.wait_ge(moments_done, TILES)
            nc.vector.tensor_scalar_add(var_eps[:, :], mv[:, :, 1], LN_EPS).then_inc(moments_done, 1)
            dve.wait_ge(std_done, 1)
            nc.vector.reciprocal(rstd[:, :], std[:, :]).then_inc(rstd_done, 1)
            dve.wait_ge(rstd_done, 1)
            dve.sem_inc(lo_done, 2)

            def low_part(i, b):
                dve.wait_ge(hi_done, i + 3)
                toks = bass.ds(i * P, P)
                nc.vector.tensor_tensor(x_lo[:, :, toks], ps[b][:, :, :], x_hi[:, :, toks].bitcast(F32), ALU.subtract).then_inc(lo_done, 1)

            with dve.Fori(0, TILES // 2) as pair:
                for b in range(2):
                    i = pair * 2 + b
                    dve.wait_ge(transposed, i + 1)
                    nc.vector.tensor_scalar(xn[:, b, :], x_res[:, bass.ds(i, 1), :], mv[:, bass.ds(i, 1), 0],
                                            rstd[:, bass.ds(i, 1)], ALU.subtract, ALU.mult).then_inc(xn_ready, 1)
                for b in range(0 if x_lo is None else 2):
                    low_part(pair * 2 + b, b)

        @block.scalar
        def _(act):
            act.sem_inc(hi_done, 2)
            act.wait_ge(moments_done, TILES + 1)
            nc.scalar.activation(std[:, :], var_eps[:, :], ACT.Sqrt).then_inc(std_done, 1)
            with act.Fori(0, TILES // 2) as pair:
                for b in range(2):
                    i = pair * 2 + b
                    act.wait_ge(transposed, i + 3)
                    nc.scalar.copy(x_hi[:, :, bass.ds(i * P, P)], ps[b][:, :, :]).then_inc(hi_done, 1)

        @block.tensor
        def _(pe):
            pe.sem_inc(transposed, 2)
            with pe.Fori(0, TILES // 2) as pair:
                for b in range(2):
                    i = pair * 2 + b
                    pe.wait_ge(xn_ready, i + 1)
                    pe.wait_ge(hi_done if x_lo is None else lo_done, i + 1)
                    for k in range(KD):
                        last = nc.tensor.transpose(ps[b][:, k, :], xn[:, b, k * P:(k + 1) * P], ident[:, :])
                    last.then_inc(transposed, 1)


def split_weights(nc, name, jobs):
    width = max(src.free_size() for src, _, _ in jobs)
    with ExitStack() as ctx:
        stage = [ctx.enter_context(nc.sbuf_tensor(f"{name}_stage{b}", [P, width], F32)) for b in range(2)]
        loaded = [ctx.enter_context(nc.semaphore(f"{name}_loaded{b}")) for b in range(2)]
        hi_done = ctx.enter_context(nc.semaphore(name + "_hi_done"))
        lo_done = ctx.enter_context(nc.semaphore(name + "_lo_done"))
        block = ctx.enter_context(nc.Block())

        def view(n):
            hi = jobs[n][1]
            v = stage[n % 2][:hi.shape[0], :hi.free_size()]
            return v.rearrange("p (a d) -> p a d", a=hi.shape[1]) if len(hi.shape) == 3 else v

        @block.sync
        def _(sp):
            for n, (src, _, _) in enumerate(jobs):
                if n >= 2:
                    sp.wait_ge(lo_done, n - 1)
                sp.dma_start(view(n), src).then_inc(loaded[n % 2], 16)

        @block.scalar
        def _(act):
            for n, (_, hi, _) in enumerate(jobs):
                act.wait_ge(loaded[n % 2], 16 * (n // 2 + 1))
                nc.scalar.copy(hi, view(n)).then_inc(hi_done, 1)

        @block.vector
        def _(dve):
            for n, (_, hi, lo) in enumerate(jobs):
                dve.wait_ge(hi_done, n + 1)
                nc.vector.tensor_tensor(lo, view(n), hi.bitcast(F32), ALU.subtract).then_inc(lo_done, 1)


def attention(nc, x_res, ident, w, b_qk, b_v, wo, bo):
    qk = {n: nc.dram_tensor(f"{n}_parts", (HEADS, 2, DH, N_TOK), F32).ap() for n in "qk"}
    with ExitStack() as ctx:
        inv_sums = nc.dram_tensor("inv_sums", (HEADS, N_TOK), F32).ap()
        v_rows = ctx.enter_context(nc.sbuf_tensor("v_rows", [P, TILES, D], F32))
        yT = nc.dram_tensor("yT_and_sums", (HEADS, DH + 1, N_TOK), F32).ap()
        with ExitStack() as inner:
            x_hi = inner.enter_context(nc.sbuf_tensor("a_x_hi", [P, KD, N_TOK], F32R))
            x_lo = inner.enter_context(nc.sbuf_tensor("a_x_lo", [P, KD, N_TOK], F32R))
            w_hi = inner.enter_context(nc.sbuf_tensor("w_qkv_hi", [P, KD, 3 * D], F32R))
            w_lo = inner.enter_context(nc.sbuf_tensor("w_qkv_lo", [P, KD, 3 * D], F32R))
            layernorm_transposed(nc, "a_ln", x_res, x_hi, x_lo, ident)
            split_weights(nc, "w_qkv", [(w[k * P:(k + 1) * P, :], w_hi[:, k, :], w_lo[:, k, :]) for k in range(KD)])
            project_qkv(nc, x_hi, x_lo, w_hi, w_lo, b_qk, b_v, qk, v_rows)
        attend(nc, qk, v_rows, yT)
        wo_hi = ctx.enter_context(nc.sbuf_tensor("wo_hi", [P, KD, D], F32R))
        wo_lo = ctx.enter_context(nc.sbuf_tensor("wo_lo", [P, KD, D], F32R))
        split_weights(nc, "wo", [(wo.rearrange("(k p) d -> p k d", p=P), wo_hi[:, :, :], wo_lo[:, :, :])])
        output_projection(nc, x_res, yT, inv_sums, wo_hi, wo_lo, bo)


def project_qkv(nc, x_hi, x_lo, w_hi, w_lo, b_qk, b_v, qk, v_rows):
    MT = 2 * D // P
    HT = P // DH
    BUFS = 4
    with ExitStack() as ctx:
        sb = lambda n, s, dt=F32: ctx.enter_context(nc.sbuf_tensor(n, s, dt))
        bias, bias_v = sb("b_qk_sb", [P, MT]), sb("b_v_sb", [P, D])
        hi, lo = sb("qk_hi", [P, 2, GROUP], F32R), sb("qk_lo", [P, 2, GROUP], F32R)
        ps = [ctx.enter_context(nc.psum_tensor(f"qk_ps{i}", [P, GROUP], F32)) for i in range(BUFS)]
        ps_v = [ctx.enter_context(nc.psum_tensor(f"v_ps{i}", [P, D], F32)) for i in range(2)]
        sem = nc.alloc_semaphore
        bias_loaded, product, hi_done, lo_done, v_product, v_added = (
            sem("bias_loaded"), sem("qk_product"), sem("qk_hi_done"), sem("qk_lo_done"), sem("v_product"), sem("v_added"))
        stored = [sem(f"qk_stored{b}") for b in range(2)]
        block = ctx.enter_context(nc.Block())

        @block.tensor
        def _(pe):
            with pe.Fori(0, GROUPS) as g:
                for m in range(MT):
                    pe.wait_ge(lo_done, g * MT + m + 1)
                    toks = bass.ds(g * GROUP, GROUP)
                    terms = [(w_hi, x_hi), (w_lo, x_hi), (w_hi, x_lo)]
                    for n, (k, (a, x)) in enumerate([(k, t) for k in range(KD) for t in terms]):
                        last = nc.tensor.matmul(ps[m % BUFS][:, :], a[:, k, m * P:(m + 1) * P], x[:, k, toks],
                                                start=(n == 0), stop=(n == 3 * KD - 1))
                    last.then_inc(product, 1)
            for i in range(TILES):
                if i >= 2:
                    pe.wait_ge(v_added, i - 1)
                terms = [(x_hi, w_hi), (x_lo, w_hi), (x_hi, w_lo)]
                for n, (k, (x, a)) in enumerate([(k, t) for k in range(KD) for t in terms]):
                    last = nc.tensor.matmul(ps_v[i % 2][:, :], x[:, k, i * P:(i + 1) * P], a[:, k, 2 * D:3 * D],
                                            start=(n == 0), stop=(n == 3 * KD - 1))
                last.then_inc(v_product, 1)

        @block.scalar
        def _(act):
            for b in range(2):
                act.sem_inc(stored[b], 32)
            act.wait_ge(bias_loaded, 32)
            with act.Fori(0, GROUPS) as g:
                for m in range(MT):
                    act.wait_ge(product, g * MT + m + 1)
                    act.wait_ge(stored[m % 2], (g * (MT // 2) + m // 2 + 1) * 32)
                    nc.scalar.activation(hi[:, m % 2, :], ps[m % BUFS][:, :], ACT.Identity, bias=bias[:, m:m + 1]).then_inc(hi_done, 1)

        @block.vector
        def _(dve):
            dve.sem_inc(lo_done, BUFS)
            with dve.Fori(0, GROUPS) as g:
                for m in range(MT):
                    dve.wait_ge(hi_done, g * MT + m + 1)
                    nc.vector.scalar_tensor_tensor(lo[:, m % 2, :], ps[m % BUFS][:, :], bias[:, m:m + 1],
                                                   hi[:, m % 2, :].bitcast(F32), ALU.add, ALU.subtract).then_inc(lo_done, 1)
            for i in range(TILES):
                dve.wait_ge(v_product, i + 1)
                nc.vector.tensor_tensor(v_rows[:, i, :], ps_v[i % 2][:, :], bias_v[:, :], ALU.add).then_inc(v_added, 1)

        @block.sync
        def _(sp):
            sp.dma_start(bias[:, :], b_qk).then_inc(bias_loaded, 16)
            sp.dma_start(bias_v[:, :], b_v.partition_broadcast(P)).then_inc(bias_loaded, 16)
            with sp.Fori(0, GROUPS) as g:
                for m in range(MT):
                    h0 = (m % (MT // 2)) * HT
                    dst = qk["qk"[m // (MT // 2)]]
                    sp.wait_ge(lo_done, g * MT + m + 1 + BUFS)
                    for part, buf in ((0, hi), (1, lo)):
                        sp.dma_start(dst[h0:h0 + HT, part, :, bass.ds(g * GROUP, GROUP)],
                                     buf[:, m % 2, :].bitcast(F32)).then_inc(stored[m % 2], 16)
            for b in range(2):
                sp.wait_ge(stored[b], 32 * (GROUPS * MT // 2 + 1))


def attend(nc, qk, v_rows, yT):
    PAIRS = BATCH * HEADS
    E = 4
    BODIES = PAIRS // E
    CHUNKS_C = [(sb, max(sb * P, t0), t0 + 512 - max(sb * P, t0)) for sb in range(TB) for t0 in range(0, T, 512) if sb * P < t0 + 512]
    NCH = len(CHUNKS_C)
    RING = 4
    LAG = 2
    K_QK = 3 * DH
    CONSTS = 13 + E
    assert NCH % RING == 0
    with ExitStack() as ctx:
        sb = lambda n, s, dt=F32: ctx.enter_context(nc.sbuf_tensor(n, s, dt))
        q_st, k_st = [sb(f"q_st{b}", [P, T], F32R) for b in range(E)], [sb(f"k_st{b}", [P, T], F32R) for b in range(E)]
        v_pair = [sb(f"v_pair{b}", [P, TB, DH + 1]) for b in range(2)]
        probs = [sb(f"probs{b}", [P, 512]) for b in range(RING)]
        y_st = [sb(f"y_st{b}", [DH + 1, T]) for b in range(2)]
        neg_max = sb("neg_max", [P, TB])
        max_cols = sb("max_cols", [P, TB, P], F32R)
        ident, ident_r, ones, zeros = sb("att_ident", [P, P]), sb("ident_r", [P, P], F32R), sb("ones", [P, T]), sb("zeros", [P, TB, P])
        ident_bf, mask, mask_T = sb("ident_bf", [P, P], BF16), sb("causal_mask", [P, P], BF16), sb("causal_mask_T", [P, P], BF16)
        ps_r = [ctx.enter_context(nc.psum_tensor(f"ps_r{b}", [P, T], F32)) for b in range(2)]
        ps_c = [ctx.enter_context(nc.psum_tensor(f"ps_c{b}", [P, 512], F32)) for b in range(2)]
        ps_y = ctx.enter_context(nc.psum_tensor("ps_y", [P, T], F32))
        sem = nc.alloc_semaphore
        staged, y_stored = [sem(f"staged{b}") for b in range(E)], [sem(f"y_stored{b}") for b in range(2)]
        consts, rows_done, max_done, parts_done, turned, shift_ready, cols_done, exp_done, v_ready, pv_done, y_done, turns_begun, loads_begun = [
            sem(n) for n in ("att_consts", "rows_done", "max_done", "max_parts_done", "max_turned", "shift_ready", "cols_done", "exp_done", "v_ready",
                             "pv_done", "y_done", "v_turns_begun", "q_loads_begun")]
        block = ctx.enter_context(nc.Block())
        head = lambda it, e: it * (E // 2) + e // 2
        after = lambda it, e: (it, e + 1) if e + 1 < E else (it + 1, 0)

        @block.gpsimd
        def _(pool):
            for t, value in ((mask, 0.0), (mask_T, 0.0), (ident, 0.0), (ones, 1.0)):
                pool.memset(t[:, :], value).then_inc(consts, 1)
            pool.memset(zeros[:, :, :], 0.0).then_inc(consts, 1)
            for b in range(2):
                pool.memset(v_pair[b][:, :, DH:], 1.0).then_inc(consts, 1)
            pool.wait_ge(consts, 7)
            pool.affine_select(out=mask[:, :], in_=mask[:, :], compare_op=ALU.is_ge, fill=NEG,
                               base=0, pattern=[[-1, P]], channel_multiplier=1).then_inc(consts, 1)
            pool.affine_select(out=mask_T[:, :], in_=mask_T[:, :], compare_op=ALU.is_ge, fill=NEG,
                               base=0, pattern=[[1, P]], channel_multiplier=-1).then_inc(consts, 1)
            pool.affine_select(out=ident[:, :], in_=ident[:, :], compare_op=ALU.not_equal, fill=1.0,
                               base=0, pattern=[[-1, P]], channel_multiplier=1).then_inc(consts, 1)
            with pool.Fori(0, BODIES) as it:
                for e in range(E):
                    p = it * E + e
                    pool.wait_ge(pv_done, (p + 1) * NCH)
                    pool.sem_inc(turns_begun, 1)
                    nc.gpsimd.tensor_copy(v_pair[e % 2][:, :, :DH],
                                          v_rows[:, e % 2 * TB:(e % 2 + 1) * TB, bass.ds(head(it, e) * DH, DH)]).then_inc(v_ready, 1)

        @block.sync
        def _(sp):
            sp.sem_inc(y_stored[0], 16)
            sp.sem_inc(y_stored[1], 16)

            def load(it, e):
                sp.wait_ge(cols_done, (it * E + e + 1) * NCH)
                sp.sem_inc(loads_begun, 1)
                toks = slice(e % 2 * T, (e % 2 + 1) * T)
                parts = lambda n, a, b: qk[n][bass.ds(head(it, e), 1), a:b, :, toks].rearrange("h a d t -> (h a d) t")
                for rows, n, part0, part1 in ((0, "q", 0, 2), (2, "q", 0, 1), (0, "k", 0, 1), (1, "k", 0, 2)):
                    dst = (q_st if n == "q" else k_st)[e][rows * DH:(rows + part1 - part0) * DH, :]
                    sp.dma_start(dst.bitcast(F32), parts(n, part0, part1)).then_inc(staged[e], 16)

            def store(it, e):
                sp.wait_ge(y_done, it * E + e + 2)
                sp.sem_inc(loads_begun, 1)
                sp.dma_start(yT[bass.ds(head(it, e), 1), :, e % 2 * T:(e % 2 + 1) * T].rearrange("h d t -> (h d) t"), y_st[e % 2][:, :]).then_inc(y_stored[e % 2], 16)

            for e in range(E):
                load(0, e)
            with sp.Fori(0, BODIES - 1) as it:
                for e in range(E):
                    store(it, e)
                    load(it + 1, e)
            for e in range(E):
                store(BODIES - 1, e)
            for b in range(2):
                sp.wait_ge(y_stored[b], 16 * (PAIRS // 2 + 1))

        @block.tensor
        def _(pe):
            pe.sem_inc(cols_done, E * NCH)
            pe.sem_inc(pv_done, 2 * NCH)

            def rows(it, e, i):
                p, tb = it * E + e, TB - 1 - i
                if i == 0:
                    pe.wait_ge(staged[e], (it + 1) * 64)
                    if not (isinstance(it, int) and it == 0 and e == 0):
                        pe.wait_ge(shift_ready, p)
                pe.wait_ge(max_done, p * TB + i + 1)
                ps, width = ps_r[i % 2], (tb + 1) * P
                for c in range(0, width, 512):
                    n_c = min(512, width - c)
                    nc.tensor.matmul(ps[:, c:c + n_c], q_st[e][:K_QK, tb * P:(tb + 1) * P], k_st[e][:K_QK, c:c + n_c], start=True, stop=(c + n_c < width))
                nc.tensor.matmul(ps[:, tb * P:width], ident_bf[:, :], mask[:, :], start=False, stop=True).then_inc(rows_done, 1)

            def turn_maxima(it, e):
                pe.wait_ge(parts_done, (it * E + e + 1) * 2)
                for tb in range(TB):
                    last = nc.tensor.matmul(ps_r[0][:, tb * P:(tb + 1) * P], max_cols[:, tb, :], ident_r[:, :], start=True, stop=True)
                last.then_inc(turned, 1)

            def columns(it, e, j):
                s, t0, width = CHUNKS_C[j]
                if j == 0:
                    pe.wait_ge(shift_ready, it * E + e + 1)
                pe.wait_ge(exp_done, (it * E + e) * NCH + j + 1)
                diagonal = t0 == s * P
                last = nc.tensor.matmul(ps_c[j % 2][:, :width], k_st[e][:, s * P:(s + 1) * P], q_st[e][:, t0:t0 + width], start=True, stop=not diagonal)
                if diagonal:
                    last = nc.tensor.matmul(ps_c[j % 2][:, :P], ident_bf[:, :], mask_T[:, :], start=False, stop=True)
                last.then_inc(cols_done, 1)

            def output(it, e, j):
                p = it * E + e
                s, t0, width = CHUNKS_C[j]
                if j == 0:
                    pe.wait_ge(v_ready, p + 1)
                    pe.wait_ge(y_done, p + 1)
                pe.wait_ge(exp_done, p * NCH + j + 3)
                nc.tensor.matmul(ps_y[:DH + 1, t0:t0 + width], v_pair[e % 2][:, s, :], probs[j % RING][:, :width],
                                 start=(s == 0), stop=(t0 + width == (s + 1) * P)).then_inc(pv_done, 1)

            def body(it, final):
                for e in range(E):
                    more = not (final and e == E - 1)
                    for j in range(NCH):
                        columns(it, e, j)
                        if more and j < TB:
                            rows(*after(it, e), j)
                        if more and j == NCH - 1:
                            turn_maxima(*after(it, e))
                        if j >= LAG:
                            output(it, e, j - LAG)
                    for j in range(NCH - LAG, NCH):
                        output(it, e, j)

            pe.wait_ge(consts, CONSTS)
            for i in range(TB):
                rows(0, 0, i)
            turn_maxima(0, 0)
            with pe.Fori(0, BODIES - 1) as it:
                body(it, False)
            body(BODIES - 1, True)

        @block.scalar
        def _(act):
            act.sem_inc(exp_done, 2)
            with act.Fori(0, BODIES) as it:
                for e in range(E):
                    p = it * E + e
                    for j, (_, _, width) in enumerate(CHUNKS_C):
                        act.wait_ge(pv_done, p * NCH + j - RING + 1 + 2 * NCH)
                        act.wait_ge(cols_done, (p + E) * NCH + j + 1)
                        nc.scalar.activation(probs[j % RING][:, :width], ps_c[j % 2][:, :width], ACT.Exp, scale=SCALE).then_inc(exp_done, 1)

        @block.vector
        def _(dve):
            dve.wait_ge(consts, 10)
            nc.vector.tensor_copy(ident_bf[:, :], ident[:, :]).then_inc(consts, 1)
            nc.vector.tensor_copy(ident_r[:, :], ident[:, :]).then_inc(consts, 1)
            nc.vector.tensor_copy(max_cols[:, :, :], zeros[:, :, :]).then_inc(consts, 1)
            for b in range(E):
                nc.vector.tensor_copy(k_st[b][K_QK:, :], ones[K_QK:, :]).then_inc(consts, 1)
            dve.wait_ge(consts, CONSTS)
            dve.sem_inc(max_done, 2)
            dve.sem_inc(y_done, 1)

            def maxima(it, e):
                p = it * E + e
                for i in range(TB):
                    tb = TB - 1 - i
                    dve.wait_ge(rows_done, p * TB + i + 1)
                    nc.vector.tensor_reduce(neg_max[:, tb:tb + 1], ps_r[i % 2][:, :(tb + 1) * P], AX.X, ALU.max, negate=True).then_inc(max_done, 1)
                dve.wait_ge(max_done, p * TB + TB + 2)
                nc.vector.tensor_copy(max_cols[:, :, K_QK], neg_max[:, :]).then_inc(parts_done, 1)
                dve.wait_ge(parts_done, p * 2 + 1)
                nc.vector.tensor_tensor(max_cols[:, :, K_QK + 1], neg_max[:, :], max_cols[:, :, K_QK].bitcast(F32), ALU.subtract).then_inc(parts_done, 1)
                dve.wait_ge(turned, p + 1)
                nc.vector.tensor_copy(q_st[e][K_QK:, :], ps_r[0][K_QK:, :]).then_inc(shift_ready, 1)

            def evacuate(it, e):
                p = it * E + e
                dve.wait_ge(pv_done, (p + 3) * NCH)
                dve.wait_ge(y_stored[e % 2], (it * (E // 2) + e // 2 + 1) * 16)
                nc.vector.tensor_copy(y_st[e % 2][:, :], ps_y[:DH + 1, :]).then_inc(y_done, 1)

            def body(it, final):
                for e in range(E):
                    if not (final and e == E - 1):
                        maxima(*after(it, e))
                    evacuate(it, e)

            maxima(0, 0)
            with dve.Fori(0, BODIES - 1) as it:
                body(it, False)
            body(BODIES - 1, True)


def output_projection(nc, x_res, yT, inv_sums, wo_hi, wo_lo, bo):
    SUB = GROUP // P
    with ExitStack() as ctx:
        sb = lambda n, s, dt=F32: ctx.enter_context(nc.sbuf_tensor(n, s, dt))
        y = [sb(f"o_y{b}", [P, KD, GROUP]) for b in range(2)]
        y_hi, y_lo = [sb(f"y_hi{b}", [P, KD, GROUP], F32R) for b in range(2)], [sb(f"y_lo{b}", [P, KD, GROUP], F32R) for b in range(2)]
        inv = [sb(f"o_inv{b}", [P, KD, GROUP]) for b in range(2)]
        bo_all, sums = sb("bo_all", [P, D]), sb("o_sums", [P, HEADS * N_TOK // P])
        HT = P // DH
        ps_o = [ctx.enter_context(nc.psum_tensor(f"o_ps_o{b}", [P, D], F32)) for b in range(SUB)]
        sem = nc.alloc_semaphore
        loaded = [sem(f"o_loaded{b}") for b in range(2)]
        sums_loaded, inverted, inv_stored, y_ready = sem("sums_loaded"), sem("sums_inverted"), sem("inv_stored"), sem("o_y_ready")
        bo_loaded, bo_added, hi_done, lo_done, product, added = (
            sem("bo_loaded"), sem("bo_added"), sem("o_hi_done"), sem("o_lo_done"), sem("o_product"), sem("o_added"))
        block = ctx.enter_context(nc.Block())

        @block.sync
        def _(sp):
            rows = sums.shape[1]
            for h in range(HEADS):
                per = P // HEADS
                sp.dma_start(sums[h * per:(h + 1) * per, :], yT[h, DH, :].rearrange("(a t) -> a t", t=rows)).then_inc(sums_loaded, 16)
            sp.dma_start(bo_all[:, :], bo.partition_broadcast(P)).then_inc(bo_loaded, 16)
            sp.wait_ge(inverted, 1)
            sp.dma_start(inv_sums.rearrange("h (a t) -> (h a) t", t=rows), sums[:, :]).then_inc(inv_stored, 16)
            sp.wait_ge(inv_stored, 16)
            for g in range(GROUPS):
                toks = slice(g * GROUP, (g + 1) * GROUP)
                if g >= 2:
                    sp.wait_ge(lo_done, g - 1)
                for h in range(HT):
                    rows_h = slice(h * DH, (h + 1) * DH)
                    sp.dma_start(y[g % 2][rows_h, :, :], yT[h::HT, :DH, toks].rearrange("k d t -> d k t")).then_inc(loaded[g % 2], 16)
                    sp.dma_start(inv[g % 2][rows_h, :, :], inv_sums[h::HT, toks].partition_broadcast(DH)).then_inc(loaded[g % 2], 16)

        @block.gpsimd
        def _(pool):
            pool.wait_ge(bo_loaded, 16)
            with pool.Fori(0, TILES) as i:
                nc.gpsimd.tensor_tensor(x_res[:, bass.ds(i, 1), :], x_res[:, bass.ds(i, 1), :], bo_all[:, :], ALU.add).then_inc(bo_added, 1)

        @block.tensor
        def _(pe):
            for g in range(GROUPS):
                b = g % 2
                pe.wait_ge(lo_done, g + 1)
                for s in range(SUB):
                    if g > 0:
                        pe.wait_ge(added, (g - 1) * SUB + s + 1)
                    terms = [(y_hi[b], wo_hi), (y_lo[b], wo_hi), (y_hi[b], wo_lo)]
                    for n, (k, (yt, w)) in enumerate([(k, t) for k in range(KD) for t in terms]):
                        last = nc.tensor.matmul(ps_o[s][:, :], yt[:, k, s * P:(s + 1) * P], w[:, k, :], start=(n == 0), stop=(n == 3 * KD - 1))
                    last.then_inc(product, 1)

        @block.scalar
        def _(act):
            for g in range(GROUPS):
                act.wait_ge(y_ready, g + 1)
                if g >= 2:
                    act.wait_ge(product, (g - 1) * SUB)
                nc.scalar.copy(y_hi[g % 2][:, :, :], y[g % 2][:, :, :]).then_inc(hi_done, 1)

        @block.vector
        def _(dve):
            def add(g):
                for s in range(SUB):
                    i = g * SUB + s
                    dve.wait_ge(product, i + 1)
                    dve.wait_ge(bo_added, i + 1)
                    nc.vector.tensor_tensor(x_res[:, i, :], ps_o[s][:, :], x_res[:, i, :], ALU.add).then_inc(added, 1)

            dve.wait_ge(sums_loaded, 16 * HEADS)
            nc.vector.reciprocal(sums[:, :], sums[:, :]).then_inc(inverted, 1)
            for g in range(GROUPS):
                dve.wait_ge(loaded[g % 2], 32 * HT * (g // 2 + 1))
                nc.vector.tensor_tensor(y[g % 2][:, :, :], y[g % 2][:, :, :], inv[g % 2][:, :, :], ALU.mult).then_inc(y_ready, 1)
                dve.wait_ge(hi_done, g + 1)
                nc.vector.tensor_tensor(y_lo[g % 2][:, :, :], y[g % 2][:, :, :], y_hi[g % 2][:, :, :].bitcast(F32), ALU.subtract).then_inc(lo_done, 1)
                if g > 0:
                    add(g - 1)
            add(GROUPS - 1)


LOOKUP = 258
LOOKUPS = 3 * INTER * D // P // LOOKUP
EXPERTS = 32
TOP_K = 8
INTER_E = 192
REST_E = INTER_E - P


def mixture_of_experts(nc, x_res, ident, gate_wT, w_gu, w_dn, lut, idx, w_ffn):
    with ExitStack() as ctx:
        x_hi = ctx.enter_context(nc.sbuf_tensor("m_x_hi", [P, KD, N_TOK], F32R))
        x_lo = ctx.enter_context(nc.sbuf_tensor("m_x_lo", [P, KD, N_TOK], F32R))
        routing = ctx.enter_context(nc.sbuf_tensor("routing", [P, TILES, EXPERTS], F32))
        layernorm_transposed(nc, "m_ln", x_res, x_hi, x_lo, ident)
        with ExitStack() as inner:
            gw_hi = inner.enter_context(nc.sbuf_tensor("gw_hi", [P, KD, EXPERTS], F32R))
            gw_lo = inner.enter_context(nc.sbuf_tensor("gw_lo", [P, KD, EXPERTS], F32R))
            split_weights(nc, "gw", [(gate_wT.rearrange("(k p) e -> p k e", p=P), gw_hi[:, :, :], gw_lo[:, :, :])])
            route(nc, x_hi, x_lo, gw_hi, gw_lo, routing)
        experts(nc, x_res, x_hi, x_lo, routing, w_gu, w_dn, lut, idx, w_ffn)


def route(nc, x_hi, x_lo, gw_hi, gw_lo, routing):
    TAKEN = -3.0e38
    with ExitStack() as ctx:
        sb = lambda n, s: ctx.enter_context(nc.sbuf_tensor(n, s, F32))
        logits, shifted, weight = sb("logits", [P, TILES, EXPERTS]), sb("shifted", [P, TILES, EXPERTS]), sb("weight", [P, TILES, EXPERTS])
        rest, chosen = sb("rest", [P, TILES, EXPERTS]), sb("chosen", [P, TILES, EXPERTS])
        top, total, inv = sb("top", [P, TILES, TOP_K]), sb("total", [P, TILES]), sb("inv_total", [P, TILES])
        ps = ctx.enter_context(nc.psum_tensor("ps_logits", [P, TILES, EXPERTS], F32))
        sem = nc.alloc_semaphore
        product, copied, exp_done, step = sem("logits_done"), sem("logits_copied"), sem("r_exp_done"), sem("route_step")
        block = ctx.enter_context(nc.Block())

        @block.tensor
        def _(pe):
            for i in range(TILES):
                toks = slice(i * P, (i + 1) * P)
                terms = [(x_hi, gw_hi), (x_lo, gw_hi), (x_hi, gw_lo)]
                for n, (k, (x, w)) in enumerate([(k, t) for k in range(KD) for t in terms]):
                    last = nc.tensor.matmul(ps[:, i, :], x[:, k, toks], w[:, k, :], start=(n == 0), stop=(n == 3 * KD - 1))
            last.then_inc(product, 1)

        @block.scalar
        def _(act):
            act.wait_ge(product, 1)
            nc.scalar.copy(logits[:, :, :], ps[:, :, :]).then_inc(copied, 1)
            act.wait_ge(step, TILES + 1)
            nc.scalar.activation(weight[:, :, :], shifted[:, :, :], ACT.Exp).then_inc(exp_done, 1)

        @block.vector
        def _(dve):
            dve.wait_ge(copied, 1)
            for i in range(TILES):
                nc.vector.max(top[:, i, :], logits[:, i, :]).then_inc(step, 1)
            dve.wait_ge(step, TILES)
            nc.vector.tensor_tensor(shifted[:, :, :], logits[:, :, :], top[:, :, 0:1].to_broadcast([P, TILES, EXPERTS]), ALU.subtract).then_inc(step, 1)
            for i in range(TILES):
                nc.vector.match_replace(rest[:, i, :], top[:, i, :], logits[:, i, :], TAKEN).then_inc(step, 1)
            dve.wait_ge(step, 2 * TILES + 1)
            nc.vector.tensor_single_scalar(chosen[:, :, :], rest[:, :, :], TAKEN, ALU.is_equal).then_inc(step, 1)
            dve.wait_ge(step, 2 * TILES + 2)
            dve.wait_ge(exp_done, 1)
            nc.vector.tensor_tensor(routing[:, :, :], weight[:, :, :], chosen[:, :, :], ALU.mult).then_inc(step, 1)
            dve.wait_ge(step, 2 * TILES + 3)
            nc.vector.reduce_sum(total[:, :], routing[:, :, :], AX.X).then_inc(step, 1)
            dve.wait_ge(step, 2 * TILES + 4)
            nc.vector.reciprocal(inv[:, :], total[:, :]).then_inc(step, 1)
            dve.wait_ge(step, 2 * TILES + 5)
            nc.vector.tensor_tensor(routing[:, :, :], routing[:, :, :], inv[:, :].unsqueeze(2).to_broadcast([P, TILES, EXPERTS]), ALU.mult)


def experts(nc, x_res, x_hi, x_lo, routing, w_gu, w_dn, lut, idx, w_ffn):
    RUNS = 2 * GROUPS
    SUB = GROUP // P
    TERMS = LUT // 2
    PARTS = 3
    BODIES = EXPERTS // 2
    with ExitStack() as ctx:
        sb = lambda n, s, dt=F32: ctx.enter_context(nc.sbuf_tensor(n, s, dt))
        raw_gu, raw_dn = [sb(f"raw_gu{b}", [P, KD, 2 * INTER_E]) for b in range(2)], [sb(f"raw_dn{b}", [P, 2, D]) for b in range(2)]
        gu_hi, gu_lo = [sb(f"gu_hi{b}", [P, KD, 2 * INTER_E], F32R) for b in range(2)], [sb(f"gu_lo{b}", [P, KD, 2 * INTER_E], F32R) for b in range(2)]
        dn_hi, dn_lo = [sb(f"dn_hi{b}", [P, 2, D], F32R) for b in range(2)], [sb(f"dn_lo{b}", [P, 2, D], F32R) for b in range(2)]
        silu = sb("m_silu", [P, 2, GROUP])
        h = sb("m_h", [P, 2, GROUP])
        lut_all, entry = sb("lut_all", [P, LUT]), sb("lut_entry", [P, TERMS, LOOKUP])
        idx_st, looked_up = [sb(f"idx_st{b}", [P, LOOKUP], mybir.dt.int32) for b in range(2)], sb("looked_up", [P, LOOKUP])
        h_hi, h_lo = [sb(f"m_h_hi{b}", [P, 2, GROUP], F32R) for b in range(2)], [sb(f"m_h_lo{b}", [P, 1, GROUP], F32R) for b in range(2)]
        pb = lambda n: ctx.enter_context(nc.psum_tensor(n, [P, 512], F32))
        ps_g, ps_u, ps_r, ps_o = [[pb(f"m_ps_{c}{b}") for b in range(2)] for c in "guro"]
        sem = nc.alloc_semaphore
        loaded = [sem(f"m_loaded{b}") for b in range(2)]
        w_hi_done, w_lo_done, up_done, silu_done, h_done, hi_done, lo_done, down_done, added = [
            sem("m_" + n) for n in ("w_hi_done", "w_lo_done", "up_done", "silu_done", "h_done", "hi_done", "lo_done", "down_done", "added")]
        idx_loaded = [sem(f"idx_loaded{b}") for b in range(2)]
        lut_loaded, terms_ready, summed, w_stored, lookups_begun = [
            sem(n) for n in ("lut_loaded", "lut_terms_ready", "lut_terms_summed", "w_ffn_stored", "lookups_begun")]
        assert EXPERTS * GROUPS == 2 * LOOKUPS
        block = ctx.enter_context(nc.Block())

        @block.gpsimd
        def _(pool):
            pool.dma_start(lut_all[:, :], lut.partition_broadcast(P)).then_inc(lut_loaded, 16)
            pool.sem_inc(summed, 1)

            def load_idx(c, b):
                pool.dma_start(idx_st[b][:, :], idx[bass.ds(c, 1), :, :].rearrange("c p j -> p (c j)")).then_inc(idx_loaded[b], 16)

            def sum_up(it, b, first, final):
                c = it * 2 + b
                if not (first and b == 0):
                    pool.wait_ge(w_stored, c * 16)
                    pool.sem_inc(lookups_begun, 1)
                for e in range(1, LUT):
                    if e in (1, TERMS):
                        pool.wait_ge(terms_ready, c * 2 + e // TERMS + 1)
                        pool.sem_inc(lookups_begun, 1)
                    so_far = entry[:, 0, :]
                    if e > 1:
                        so_far = looked_up[:, :]
                        pool.wait_ge(summed, c * (LUT - 1) + e)
                    nc.gpsimd.tensor_tensor(looked_up[:, :], so_far, entry[:, e % TERMS, :], ALU.add).then_inc(summed, 1)
                pool.wait_ge(summed, (c + 1) * (LUT - 1) + 1)
                pool.sem_inc(lookups_begun, 1)
                pool.dma_start(w_ffn[bass.ds(c, 1), :, :].rearrange("c p j -> p (c j)"), looked_up[:, :]).then_inc(w_stored, 16)
                if not final:
                    load_idx(c + 2, b)

            for b in range(2):
                load_idx(b, b)
            for b in range(2):
                sum_up(0, b, True, False)
            with pool.Fori(1, LOOKUPS // 2 - 1) as it:
                for b in range(2):
                    sum_up(it, b, False, False)
            for b in range(2):
                sum_up(LOOKUPS // 2 - 1, b, False, True)
            pool.wait_ge(w_stored, 16 * LOOKUPS)

        @block.sync
        def _(sp):
            with sp.Fori(0, BODIES) as it:
                for b in range(2):
                    e = it * 2 + b
                    sp.wait_ge(w_lo_done, e + 1)
                    sp.dma_start(raw_gu[b][:, :, :], w_gu[bass.ds(e, 1), :, :].rearrange("e (k p) i -> p (e k) i", p=P)).then_inc(loaded[b], 16)
                    sp.dma_start(raw_dn[b][:, 0, :], w_dn[bass.ds(e, 1), 0:P, :].rearrange("e i d -> i (e d)")).then_inc(loaded[b], 16)
                    for half in range(2):
                        sp.dma_start(raw_dn[b][half * REST_E:(half + 1) * REST_E, 1, :], w_dn[bass.ds(e, 1), P:INTER_E, :].rearrange("e i d -> i (e d)")).then_inc(loaded[b], 16)

        @block.tensor
        def _(pe):
            pe.sem_inc(down_done, 2 * SUB)

            def up(it, r):
                n, b, g, r2 = it * RUNS + r, (r // GROUPS) % 2, r % GROUPS, r % 2
                if g == 0:
                    pe.wait_ge(w_lo_done, it * 2 + r // GROUPS + 3)
                pe.wait_ge(h_done, n + 1)
                for ps, c0 in ((ps_g, 0), (ps_u, P), (ps_r, 2 * P)):
                    terms = [(gu_hi[b], x_hi), (gu_lo[b], x_hi), (gu_hi[b], x_lo)]
                    for m, (k, (w, x)) in enumerate([(k, t) for k in range(KD) for t in terms]):
                        last = nc.tensor.matmul(ps[r2][:, :], w[:, k, c0:c0 + P], x[:, k, g * GROUP:(g + 1) * GROUP],
                                                start=(m == 0), stop=(m == 3 * KD - 1))
                last.then_inc(up_done, 1)

            def down(it, r):
                n, b, r2 = it * RUNS + r, r // GROUPS, r % 2
                pe.wait_ge(lo_done, n + 2)
                for s in range(SUB):
                    pe.wait_ge(added, n * SUB + s + 1)
                    toks = slice(s * P, (s + 1) * P)
                    terms = [(h_hi[r2], dn_hi[b], 0, P), (h_lo[r2], dn_hi[b], 0, P), (h_hi[r2], dn_lo[b], 0, P),
                             (h_hi[r2], dn_hi[b], 1, P), (h_hi[r2], dn_lo[b], 1, REST_E)]
                    for m, (a, w, k, rows) in enumerate(terms):
                        last = nc.tensor.matmul(ps_o[s % 2][:, :], a[:rows, k, toks], w[:rows, k, :], start=(m == 0), stop=(m == len(terms) - 1))
                    last.then_inc(down_done, 1)

            def body(it, final):
                for r in range(RUNS):
                    if not (final and r == RUNS - 1):
                        up(it, r + 1)
                    down(it, r)

            up(0, 0)
            with pe.Fori(0, BODIES - 1) as it:
                body(it, False)
            body(BODIES - 1, True)

        @block.scalar
        def _(act):
            act.sem_inc(silu_done, 1)

            def split_hi(loads, used, b, part):
                if part == 0:
                    act.wait_ge(loaded[b], loads * 64)
                    if used is not None:
                        act.wait_ge(down_done, used * SUB + 2 * SUB)
                if part < 2:
                    nc.scalar.copy(gu_hi[b][:, 2 * part:2 * part + 2, :], raw_gu[b][:, 2 * part:2 * part + 2, :]).then_inc(w_hi_done, 1)
                else:
                    nc.scalar.copy(dn_hi[b][:, :, :], raw_dn[b][:, :, :]).then_inc(w_hi_done, 1)

            def body(it, final):
                for r in range(RUNS):
                    n, r2 = it * RUNS + r, r % 2
                    act.wait_ge(up_done, n + 1)
                    act.wait_ge(h_done, n + 2)
                    nc.scalar.activation(silu[:, 0, :], ps_g[r2][:, :], ACT.Silu)
                    nc.scalar.activation(silu[P - REST_E:, 1, :], ps_r[r2][:REST_E, :], ACT.Silu).then_inc(silu_done, 1)
                    act.wait_ge(h_done, n + 3)
                    act.wait_ge(down_done, n * SUB + SUB)
                    nc.scalar.copy(h_hi[r2][:, 0, :], h[:, 0, :])
                    nc.scalar.copy(h_hi[r2][:REST_E, 1, :], h[:REST_E, 1, :]).then_inc(hi_done, 1)
                    if r % GROUPS < PARTS and not (final and r >= GROUPS):
                        split_hi(it + 1 + r // GROUPS, it * RUNS + r // GROUPS * GROUPS, 1 - r // GROUPS, r % GROUPS)

            for part in range(PARTS):
                split_hi(1, None, 0, part)
            with act.Fori(0, BODIES - 1) as it:
                body(it, False)
            body(BODIES - 1, True)

        @block.vector
        def _(dve):
            dve.sem_inc(h_done, 2)
            dve.sem_inc(added, 2)
            dve.sem_inc(w_lo_done, 2)
            dve.sem_inc(lo_done, 1)
            dve.wait_ge(lut_loaded, 16)

            def split_lo(e, b, part):
                dve.wait_ge(w_hi_done, e * PARTS + part + 1)
                if part < 2:
                    ks = slice(2 * part, 2 * part + 2)
                    nc.vector.tensor_tensor(gu_lo[b][:, ks, :], raw_gu[b][:, ks, :], gu_hi[b][:, ks, :].bitcast(F32), ALU.subtract)
                else:
                    nc.vector.tensor_tensor(dn_lo[b][:, :, :], raw_dn[b][:, :, :], dn_hi[b][:, :, :].bitcast(F32), ALU.subtract).then_inc(w_lo_done, 1)

            def add_run(it, r):
                n = it * RUNS + r
                for s in range(SUB):
                    i = (r % GROUPS) * SUB + s
                    dve.wait_ge(down_done, n * SUB + s + 1 + 2 * SUB)
                    nc.vector.scalar_tensor_tensor(x_res[:, i, :], ps_o[s % 2][:, :], routing[:, i, bass.ds(it * 2 + r // GROUPS, 1)],
                                                   x_res[:, i, :], ALU.mult, ALU.add).then_inc(added, 1)

            def lookup_terms(it, r):
                c, half = it * (RUNS // 2) + r // 2, r % 2
                if half == 0:
                    dve.wait_ge(idx_loaded[r // 2 % 2], (it * (RUNS // 4) + r // 4 + 1) * 16)
                dve.wait_ge(summed, c * (LUT - 1) + half * (TERMS - 1) + 1)
                for q in range(TERMS):
                    e = half * TERMS + q
                    last = nc.vector.tensor_scalar(entry[:, q, :], idx_st[r // 2 % 2][:, :], float(e), lut_all[:, e:e + 1], ALU.is_equal, ALU.mult)
                last.then_inc(terms_ready, 1)

            def body(it, final):
                for r in range(RUNS):
                    n, r2 = it * RUNS + r, r % 2
                    if r > 0:
                        add_run(it, r - 1)
                    dve.wait_ge(silu_done, n + 2)
                    dve.wait_ge(lo_done, n + 1)
                    nc.vector.tensor_tensor(h[:, 0, :], ps_u[r2][:, :], silu[:, 0, :], ALU.mult)
                    nc.vector.tensor_tensor(h[:REST_E, 1, :], ps_r[r2][P - REST_E:, :], silu[P - REST_E:, 1, :], ALU.mult).then_inc(h_done, 1)
                    dve.wait_ge(hi_done, n + 1)
                    nc.vector.tensor_tensor(h_lo[r2][:, 0, :], h[:, 0, :], h_hi[r2][:, 0, :].bitcast(F32), ALU.subtract)
                    nc.vector.tensor_tensor(h_hi[r2][P - REST_E:, 1, :], h[:REST_E, 1, :], h_hi[r2][:REST_E, 1, :].bitcast(F32),
                                            ALU.subtract).then_inc(lo_done, 1)
                    if r % GROUPS < PARTS and not (final and r >= GROUPS):
                        split_lo(it * 2 + 1 + r // GROUPS, 1 - r // GROUPS, r % GROUPS)
                    lookup_terms(it, r)
                add_run(it, RUNS - 1)

            for part in range(PARTS):
                split_lo(0, 0, part)
            with dve.Fori(0, BODIES - 1) as it:
                body(it, False)
            body(BODIES - 1, True)


STATE = 64
DHEAD = 64
S_HEADS = 16
D_INNER = S_HEADS * DHEAD
M_TILES = S_HEADS + S_HEADS // 2 + D_INNER // P
CHUNK_TOK = P // S_HEADS
CHUNKS = N_TOK // CHUNK_TOK
SEQ_TOK = N_TOK // 2 // S_HEADS
STEPS = SEQ_TOK // CHUNK_TOK
SEQS = 4
S_TOK = SEQS * SEQ_TOK
S_GROUPS = N_TOK // S_TOK


def state_space(nc, x_res, ident, w_proj, w_dt, w_out):
    proj = nc.dram_tensor("proj", (M_TILES, P, N_TOK), F32).ap()
    z_dram = nc.dram_tensor("z_dt", (N_TOK, S_HEADS), F32).ap()
    cs_dram = nc.dram_tensor("log_decay", (CHUNKS, P), F32).ap()
    with ExitStack() as ctx:
        x_hi = ctx.enter_context(nc.sbuf_tensor("s_x_hi", [P, KD, N_TOK], F32R))
        x_lo = ctx.enter_context(nc.sbuf_tensor("s_x_lo", [P, KD, N_TOK], F32R))
        layernorm_transposed(nc, "s_ln", x_res, x_hi, x_lo, ident)
        with ExitStack() as inner:
            dt_hi = inner.enter_context(nc.sbuf_tensor("dt_hi", [P, KD, S_HEADS], F32R))
            dt_lo = inner.enter_context(nc.sbuf_tensor("dt_lo", [P, KD, S_HEADS], F32R))
            split_weights(nc, "dt", [(w_dt.rearrange("(k p) h -> p k h", p=P), dt_hi[:, :, :], dt_lo[:, :, :])])
            project_dt(nc, x_hi, x_lo, dt_hi, dt_lo, z_dram)
        project_tiles(nc, x_hi, x_lo, w_proj, proj)
    with ExitStack() as ctx:
        csT = ctx.enter_context(nc.sbuf_tensor("csT", [P, CHUNKS], F32))
        decay = ctx.enter_context(nc.sbuf_tensor("decay", [P, CHUNKS], F32))
        a_chunk = ctx.enter_context(nc.sbuf_tensor("a_chunk", [P, CHUNKS], F32))
        mask = ctx.enter_context(nc.sbuf_tensor("scan_mask", [P, P], F32))
        scan_mask(nc, ident, mask)
        log_decays(nc, ident, z_dram, cs_dram, csT, decay, a_chunk)
        scan(nc, x_res, ident, proj, cs_dram, csT, decay, a_chunk, mask, w_out)


def project_dt(nc, x_hi, x_lo, dt_hi, dt_lo, z_dram):
    with ExitStack() as ctx:
        z = ctx.enter_context(nc.sbuf_tensor("z_sb", [P, TILES, S_HEADS], F32))
        ps = ctx.enter_context(nc.psum_tensor("ps_z", [P, TILES, S_HEADS], F32))
        sem = nc.alloc_semaphore
        product, copied, stored = sem("z_product"), sem("z_copied"), sem("z_stored")
        block = ctx.enter_context(nc.Block())

        @block.tensor
        def _(pe):
            for i in range(TILES):
                toks = slice(i * P, (i + 1) * P)
                terms = [(x_hi, dt_hi), (x_lo, dt_hi), (x_hi, dt_lo)]
                for n, (k, (x, w)) in enumerate([(k, t) for k in range(KD) for t in terms]):
                    last = nc.tensor.matmul(ps[:, i, :], x[:, k, toks], w[:, k, :], start=(n == 0), stop=(n == 3 * KD - 1))
            last.then_inc(product, 1)

        @block.scalar
        def _(act):
            act.wait_ge(product, 1)
            nc.scalar.copy(z[:, :, :], ps[:, :, :]).then_inc(copied, 1)

        @block.sync
        def _(sp):
            sp.wait_ge(copied, 1)
            sp.dma_start(z_dram.rearrange("(n p) h -> p n h", p=P), z[:, :, :]).then_inc(stored, 16)
            sp.wait_ge(stored, 16)


def project_tiles(nc, x_hi, x_lo, w_proj, proj):
    with ExitStack() as ctx:
        sb = lambda n, s, dt=F32: ctx.enter_context(nc.sbuf_tensor(n, s, dt))
        raw = [sb(f"s_raw{b}", [P, KD, P]) for b in range(2)]
        w_hi, w_lo = [sb(f"s_w_hi{b}", [P, KD, P], F32R) for b in range(2)], [sb(f"s_w_lo{b}", [P, KD, P], F32R) for b in range(2)]
        out = [sb(f"s_out{b}", [P, N_TOK]) for b in range(2)]
        ps = [[ctx.enter_context(nc.psum_tensor(f"s_ps{b}{g}", [P, GROUP], F32)) for g in range(GROUPS)] for b in range(2)]
        sem = nc.alloc_semaphore
        loaded, stored = [sem(f"s_loaded{b}") for b in range(2)], [sem(f"s_stored{b}") for b in range(2)]
        hi_done, lo_done, product, even_out, odd_out = sem("s_hi_done"), sem("s_lo_done"), sem("s_product"), sem("s_even_out"), sem("s_odd_out")
        HALF = GROUPS // 2
        stores_begun, splits_begun = sem("s_stores_begun"), sem("s_splits_begun")
        block = ctx.enter_context(nc.Block())

        @block.sync
        def _(sp):
            def load(m, b):
                sp.dma_start(raw[b][:, :, :], w_proj[bass.ds(m, 1), :, :].rearrange("m (k p) c -> p (m k) c", p=P)).then_inc(loaded[b], 16)

            def store(m, b):
                sp.dma_start(proj[bass.ds(m, 1), :, :].rearrange("m p t -> p (m t)"), out[b][:, :]).then_inc(stored[b], 16)

            def body(it, final):
                for b in range(2):
                    m = it * 2 + b
                    if not final:
                        sp.wait_ge(lo_done, m + 1)
                        load(m + 2, b)
                    sp.wait_ge(even_out, (m + 3) * HALF)
                    sp.sem_inc(stores_begun, 1)
                    sp.wait_ge(odd_out, (m + 3) * HALF)
                    store(m, b)

            for b in range(2):
                load(b, b)
            with sp.Fori(0, M_TILES // 2 - 1) as it:
                body(it, False)
            body(M_TILES // 2 - 1, True)
            for b in range(2):
                sp.wait_ge(stored[b], 16 * (M_TILES // 2 + 1))

        @block.gpsimd
        def _(pool):
            with pool.Fori(0, M_TILES // 2) as it:
                for b in range(2):
                    m = it * 2 + b
                    pool.wait_ge(loaded[b], it * 16 + 16)
                    pool.sem_inc(splits_begun, 1)
                    pool.wait_ge(product, m * GROUPS + GROUPS)
                    pool.sem_inc(splits_begun, 1)
                    nc.gpsimd.tensor_copy(w_hi[b][:, :, :], raw[b][:, :, :]).then_inc(hi_done, 1)
                    pool.wait_ge(hi_done, m + 1)
                    nc.gpsimd.tensor_tensor(w_lo[b][:, :, :], raw[b][:, :, :], w_hi[b][:, :, :].bitcast(F32), ALU.subtract).then_inc(lo_done, 1)

        @block.tensor
        def _(pe):
            pe.sem_inc(product, 2 * GROUPS)
            with pe.Fori(0, M_TILES // 2) as it:
                for b in range(2):
                    m = it * 2 + b
                    pe.wait_ge(lo_done, m + 1)
                    for g in range(GROUPS):
                        pe.wait_ge(even_out if g % 2 == 0 else odd_out, m * HALF + g // 2 + 1)
                        terms = [(w_hi[b], x_hi), (w_lo[b], x_hi), (w_hi[b], x_lo)]
                        for n, (k, (w, x)) in enumerate([(k, t) for k in range(KD) for t in terms]):
                            last = nc.tensor.matmul(ps[b][g][:, :], w[:, k, :], x[:, k, g * GROUP:(g + 1) * GROUP],
                                                    start=(n == 0), stop=(n == 3 * KD - 1))
                        last.then_inc(product, 1)

        @block.scalar
        def _(act):
            for b in range(2):
                act.sem_inc(stored[b], 16)
            act.sem_inc(even_out, 2 * HALF)
            with act.Fori(0, M_TILES // 2) as it:
                for b in range(2):
                    m = it * 2 + b
                    act.wait_ge(stored[b], it * 16 + 16)
                    for g in range(0, GROUPS, 2):
                        act.wait_ge(product, m * GROUPS + g + 1 + 2 * GROUPS)
                        nc.scalar.copy(out[b][:, g * GROUP:(g + 1) * GROUP], ps[b][g][:, :]).then_inc(even_out, 1)

        @block.vector
        def _(dve):
            dve.sem_inc(odd_out, 2 * HALF)
            with dve.Fori(0, M_TILES // 2) as it:
                for b in range(2):
                    m = it * 2 + b
                    dve.wait_ge(stored[b], it * 16 + 16)
                    for g in range(1, GROUPS, 2):
                        dve.wait_ge(product, m * GROUPS + g + 1 + 2 * GROUPS)
                        nc.vector.tensor_copy(out[b][:, g * GROUP:(g + 1) * GROUP], ps[b][g][:, :]).then_inc(odd_out, 1)


def scan_mask(nc, ident, mask):
    with ExitStack() as ctx:
        order_int = ctx.enter_context(nc.sbuf_tensor("order_int", [P, P], I32))
        order = ctx.enter_context(nc.sbuf_tensor("order", [P, P], F32))
        order_col = ctx.enter_context(nc.sbuf_tensor("order_col", [P, 1], F32))
        ps = ctx.enter_context(nc.psum_tensor("order_ps", [P, 512], F32))
        numbered, step, turned = [ctx.enter_context(nc.semaphore(n)) for n in ("numbered", "order_step", "order_turned")]
        block = ctx.enter_context(nc.Block())

        @block.gpsimd
        def _(pool):
            pool.iota(order_int[:, :], pattern=[[1, S_HEADS], [S_HEADS, CHUNK_TOK]], base=0, channel_multiplier=0).then_inc(numbered, 1)

        @block.vector
        def _(dve):
            dve.wait_ge(numbered, 1)
            nc.vector.tensor_copy(order[:, :], order_int[:, :]).then_inc(step, 1)
            dve.wait_ge(turned, 1)
            nc.vector.tensor_copy(order_col[:, :], ps[:, 0:1]).then_inc(step, 1)
            dve.wait_ge(step, 2)
            nc.vector.tensor_scalar(mask[:, :], order[:, :], order_col[:, :], NEG, ALU.is_lt, ALU.mult)

        @block.tensor
        def _(pe):
            pe.wait_ge(step, 1)
            nc.tensor.transpose(ps[:, 0:P], order[:, :], ident[:, :]).then_inc(turned, 1)


def log_decays(nc, ident, z_dram, cs_dram, csT, decay, a_chunk):
    H = CHUNKS // P
    with ExitStack() as ctx:
        sb = lambda n, s: ctx.enter_context(nc.sbuf_tensor(n, s, F32))
        z, neg_abs, e, l, pos, la, cs, ones = [sb("ld_" + n, [P, H, P]) for n in ("z", "neg_abs", "e", "l", "pos", "la", "cs", "ones")]
        cs_p = sb("ld_cs_p", [P, H, P])
        diff = sb("ld_diff", [P, H, P])
        ps_t = ctx.enter_context(nc.psum_tensor("ld_ps_t", [P, 512], F32))
        ps_l = ctx.enter_context(nc.psum_tensor("ld_ps_l", [P, 512], F32))
        sem = nc.alloc_semaphore
        loaded, step, act_step, pe_step, stored = sem("ld_loaded"), sem("ld_step"), sem("ld_act_step"), sem("ld_pe_step"), sem("ld_stored")
        block = ctx.enter_context(nc.Block())

        @block.sync
        def _(sp):
            sp.dma_start(z[:, :, :], z_dram.rearrange("(a c t) h -> c a (t h)", a=H, t=CHUNK_TOK)).then_inc(loaded, 16)
            sp.wait_ge(step, 7)
            sp.dma_start(cs_dram.rearrange("(a c) i -> c a i", a=H), cs_p[:, :, :]).then_inc(stored, 16)
            sp.wait_ge(stored, 16)

        @block.vector
        def _(dve):
            nc.vector.memset(ones[:, :, :], 1.0).then_inc(step, 1)
            dve.wait_ge(loaded, 16)
            nc.vector.scalar_tensor_tensor(neg_abs[:, :, :], z[:, :, :], -1.0, z[:, :, :], ALU.mult, ALU.min).then_inc(step, 1)
            nc.vector.tensor_scalar_max(pos[:, :, :], z[:, :, :], 0.0).then_inc(step, 1)
            dve.wait_ge(act_step, 2)
            dve.wait_ge(step, 3)
            nc.vector.scalar_tensor_tensor(la[:, :, :], pos[:, :, :], -1.0, l[:, :, :], ALU.mult, ALU.subtract).then_inc(step, 1)
            dve.wait_ge(step, 4)
            for a in range(H):
                nc.vector.tensor_tensor_scan(cs[:, a, :], ones[:, a, :], la[:, a, :], 0.0, ALU.mult, ALU.add).then_inc(step, 1)
            dve.wait_ge(step, 6)
            nc.vector.tensor_copy(cs_p[:, :, :].rearrange("c a (h t) -> c a h t", t=CHUNK_TOK),
                                  cs[:, :, :].rearrange("c a (t h) -> c a h t", t=CHUNK_TOK)).then_inc(step, 1)
            dve.wait_ge(pe_step, 2)
            nc.vector.tensor_copy(csT[:, :], ps_t[:, :CHUNKS]).then_inc(step, 1)
            dve.wait_ge(step, 8)
            nc.vector.tensor_tensor(decay[:, :], ps_l[:, :CHUNKS], csT[:, :], ALU.subtract).then_inc(step, 1)

        @block.scalar
        def _(act):
            act.wait_ge(step, 2)
            nc.scalar.activation(e[:, :, :], neg_abs[:, :, :], ACT.Exp).then_inc(act_step, 1)
            act.wait_ge(act_step, 1)
            nc.scalar.activation(l[:, :, :], e[:, :, :], ACT.Ln, bias=1.0).then_inc(act_step, 1)
            act.wait_ge(step, 9)
            nc.scalar.activation(a_chunk[:, :], ps_l[:, :CHUNKS], ACT.Exp)
            nc.scalar.activation(decay[:, :], decay[:, :], ACT.Exp)

        @block.tensor
        def _(pe):
            pe.wait_ge(step, 7)
            for a in range(H):
                last = nc.tensor.transpose(ps_t[:, a * P:(a + 1) * P], cs_p[:, a, :], ident[:, :])
            last.then_inc(pe_step, 1)
            for a in range(H):
                last = nc.tensor.matmul(ps_l[:, a * P:(a + 1) * P], cs_p[:, a, P - 1:P].to_broadcast([P, P]), ident[:, :], start=True, stop=True)
            last.then_inc(pe_step, 1)


def scan(nc, x_res, ident, proj, cs_dram, csT, decay, a_chunk, mask, w_out):
    N_POS = S_TOK * S_HEADS
    TT = S_TOK // P
    KO = D_INNER // P
    NC = SEQS * STEPS
    PAIRS = S_HEADS // 2
    with ExitStack() as ctx:
        sb = lambda n, s: ctx.enter_context(nc.sbuf_tensor(n, s, F32))
        bx_raw = sb("bx_raw", [P, S_HEADS, S_TOK])
        bx = [sb(f"bx{b}", [P, N_POS]) for b in range(2)]
        c_st = [sb(f"c_st{b}", [STATE, S_HEADS, S_TOK]) for b in range(2)]
        gate = [sb(f"gate{b}", [P, KO, S_TOK]) for b in range(2)]
        cs_all = sb("cs_all", [P, N_POS])
        c_dec = sb("c_dec", [STATE, N_POS])
        expo = [sb(f"expo{b}", [P, SEQS, P]) for b in range(2)]
        att = [sb(f"s_att{b}", [P, SEQS, P]) for b in range(2)]
        b_dec = [sb(f"b_dec{b}", [P, SEQS, STATE]) for b in range(2)]
        x_nat = [sb(f"x_nat{b}", [P, SEQS, DHEAD]) for b in range(2)]
        state = [sb(f"state{b}", [STATE, SEQS, DHEAD]) for b in range(2)]
        state_dec = sb("state_dec", [STATE, SEQS, DHEAD])
        gated = sb("gated", [P, KO, S_TOK])
        w_o = sb("s_w_out_sb", [P, KO, D])
        pb = lambda n: ctx.enter_context(nc.psum_tensor(n, [P, 512], F32))
        ps_sc, ps_bx, ps_o = [[pb(f"s_ps_{c}{b}") for b in range(2)] for c in ("sc", "bx", "o")]
        ps_st, ps_y = pb("s_ps_st"), pb("s_ps_y")
        sem = nc.alloc_semaphore
        w_loaded, cs_loaded = sem("s_w_loaded"), sem("cs_loaded")
        loads_begun, turns_begun = sem("s_loads_begun"), sem("s_turns_begun")
        bx_loaded, bx_ready = sem("bx_loaded"), sem("bx_ready")
        c_loaded, gate_loaded = [[sem(f"{n}_loaded{b}") for b in range(2)] for n in ("c", "gate")]
        bx_done, sc_done, expo_done, exp_done, cdec_exp, cdec_done, silu_done = [
            sem(n) for n in ("bx_done", "sc_done", "expo_done", "s_exp_done", "cdec_exp", "cdec_done", "gate_silu_done")]
        x_out, b_out, att_done, st_done, dec_done, state_done, y_done, gated_done, o_done, o_added = [
            sem(n) for n in ("x_out", "b_out", "att_done", "st_done", "dec_done", "state_done", "y_mm_done", "gated_done", "o_done", "o_added_s")]
        block = ctx.enter_context(nc.Block())

        def chunk(buf, s, k):
            t0 = s * SEQ_TOK + k * CHUNK_TOK
            return buf[:, :, t0:t0 + CHUNK_TOK]

        def heads_of(buf, parity):
            return buf.rearrange("p (h two t) -> p h two t", two=2, t=CHUNK_TOK)[:, :, parity, :]

        @block.sync
        def _(sp):
            sp.dma_start(w_o[:, :, :], w_out.rearrange("(k p) d -> p k d", p=P)).then_inc(w_loaded, 16)
            with sp.Fori(0, S_GROUPS // 2) as it:
                for b in range(2):
                    g = it * 2 + b
                    toks = bass.ds(g * S_TOK, S_TOK)
                    sp.wait_ge(bx_ready, g + 1)
                    sp.sem_inc(loads_begun, 1)
                    sp.dma_start(bx_raw[:, :, :], proj[0:S_HEADS, :, toks].rearrange("h p t -> p h t")).then_inc(bx_loaded, 16)
                    sp.wait_ge(sc_done, g * STEPS + STEPS)
                    sp.sem_inc(loads_begun, 1)
                    sp.dma_start(c_st[b][:, :, :], proj[S_HEADS:S_HEADS + PAIRS, :, toks].rearrange("m (two p) t -> p (m two) t", two=2)).then_inc(c_loaded[b], 16)
                    sp.wait_ge(gated_done, g * STEPS + STEPS)
                    sp.sem_inc(loads_begun, 1)
                    sp.dma_start(gate[b][:, :, :], proj[S_HEADS + PAIRS:M_TILES, :, toks].rearrange("m p t -> p m t")).then_inc(gate_loaded[b], 16)
                    sp.wait_ge(expo_done, g * STEPS + 1)
                    sp.sem_inc(loads_begun, 1)
                    sp.wait_ge(cdec_exp, g + 1)
                    sp.sem_inc(loads_begun, 1)
                    rows = cs_dram[bass.ds(g * NC, NC), :].rearrange("c i -> (c i)")
                    sp.dma_start(cs_all[:, :], rows.partition_broadcast(P)).then_inc(cs_loaded, 16)

        @block.gpsimd
        def _(pool):
            pool.sem_inc(bx_ready, 1)
            with pool.Fori(0, S_GROUPS // 2) as it:
                for b in range(2):
                    g = it * 2 + b
                    pool.wait_ge(bx_loaded, g * 16 + 16)
                    pool.sem_inc(turns_begun, 1)
                    pool.wait_ge(sc_done, g * STEPS + STEPS)
                    pool.sem_inc(turns_begun, 1)
                    nc.gpsimd.tensor_copy(bx[b][:, :].rearrange("p (c h t) -> p c h t", h=S_HEADS, t=CHUNK_TOK),
                                          bx_raw[:, :, :].rearrange("p h (c t) -> p c h t", t=CHUNK_TOK)).then_inc(bx_ready, 1)

        @block.tensor
        def _(pe):
            pe.sem_inc(sc_done, 2 * STEPS)
            pe.sem_inc(y_done, 2)
            pe.sem_inc(o_done, 2)
            pe.wait_ge(w_loaded, 16)

            def prepare(it, b, k):
                g = it * 2 + b
                n = g * STEPS + k
                if k == 0:
                    pe.wait_ge(bx_ready, g + 2)
                pe.wait_ge(b_out, n + 1)
                for s in range(SEQS):
                    last = nc.tensor.transpose(ps_bx[k % 2][:, s * P:(s + 1) * P], bx[b][:, (s * STEPS + k) * P:(s * STEPS + k + 1) * P], ident[:, :])
                last.then_inc(bx_done, 1)
                if k == 0:
                    pe.wait_ge(c_loaded[b], it * 16 + 16)
                pe.wait_ge(att_done, n + 1)
                for s in range(SEQS):
                    last = nc.tensor.matmul(ps_sc[k % 2][:, s * P:(s + 1) * P], bx[b][:STATE, (s * STEPS + k) * P:(s * STEPS + k + 1) * P], chunk(c_st[b], s, k), start=True, stop=True)
                last.then_inc(sc_done, 1)

            def new_states(it, b, k):
                g = it * 2 + b
                n = g * STEPS + k
                pe.wait_ge(b_out, n + 3)
                pe.wait_ge(state_done, g * (STEPS - 1) + k + 1)
                for s in range(SEQS):
                    last = nc.tensor.matmul(ps_st[:STATE, s * DHEAD:(s + 1) * DHEAD], b_dec[k % 2][:, s, :], x_nat[k % 2][:, s, :], start=True, stop=True)
                last.then_inc(st_done, 1)

            def outputs(it, b, k):
                g = it * 2 + b
                n = g * STEPS + k
                if k == 1:
                    pe.wait_ge(cdec_done, g + 1)
                if k > 0:
                    pe.wait_ge(state_done, g * (STEPS - 1) + k + 1)
                pe.wait_ge(gated_done, n + 2 * STEPS)
                pe.wait_ge(att_done, n + 3)
                pe.wait_ge(b_out, n + 3)
                for s in range(SEQS):
                    c0 = (s * STEPS + k) * P
                    for parity in range(2):
                        dst = ps_y[parity * DHEAD:(parity + 1) * DHEAD, s * DHEAD:(s + 1) * DHEAD]
                        last = nc.tensor.matmul(dst, x_nat[k % 2][:, s, :], heads_of(att[k % 2][:, s, :], parity), start=True, stop=(k == 0))
                        if k > 0:
                            last = nc.tensor.matmul(dst, state[k % 2][:, s, :], heads_of(c_dec[:, c0:c0 + P], parity), start=False, stop=True)
                last.then_inc(y_done, 1)

            def project_out(it, b):
                g = it * 2 + b
                pe.wait_ge(gated_done, g * STEPS + 3 * STEPS)
                for tt in range(TT):
                    pe.wait_ge(o_added, g * TT + tt + 1)
                    for k in range(KO):
                        last = nc.tensor.matmul(ps_o[tt][:, :], gated[:, k, tt * P:(tt + 1) * P], w_o[:, k, :], start=(k == 0), stop=(k == KO - 1))
                    last.then_inc(o_done, 1)

            with pe.Fori(0, S_GROUPS // 2) as it:
                for b in range(2):
                    prepare(it, b, 0)
                    for k in range(STEPS):
                        if k + 1 < STEPS:
                            prepare(it, b, k + 1)
                            new_states(it, b, k)
                        outputs(it, b, k)
                    project_out(it, b)

        @block.scalar
        def _(act):
            act.sem_inc(cdec_exp, 1)
            act.sem_inc(x_out, 2)
            with act.Fori(0, S_GROUPS // 2) as it:
                for b in range(2):
                    g = it * 2 + b
                    act.wait_ge(cs_loaded, g * 16 + 16)
                    act.wait_ge(y_done, g * STEPS + 2)
                    nc.scalar.activation(c_dec[:, :], cs_all[:STATE, :], ACT.Exp).then_inc(cdec_exp, 1)
                    for k in range(STEPS):
                        n = g * STEPS + k
                        act.wait_ge(bx_done, n + 1)
                        act.wait_ge(y_done, n + 1)
                        nc.scalar.copy(x_nat[k % 2][:, :, :], ps_bx[k % 2][:, :].rearrange("p (s c) -> p s c", s=SEQS)[:, :, STATE:]).then_inc(x_out, 1)
                        act.wait_ge(expo_done, n + 2)
                        nc.scalar.activation(expo[k % 2][:, :, :], expo[k % 2][:, :, :], ACT.Exp).then_inc(exp_done, 1)
                        if k == 0:
                            act.wait_ge(gate_loaded[b], it * 16 + 16)
                            nc.scalar.activation(gate[b][:, :, :], gate[b][:, :, :], ACT.Silu).then_inc(silu_done, 1)

        @block.vector
        def _(dve):
            dve.sem_inc(expo_done, 1)
            dve.sem_inc(b_out, 2)
            dve.sem_inc(att_done, 2)
            dve.sem_inc(state_done, 1)
            dve.sem_inc(gated_done, 2 * STEPS)
            dve.sem_inc(o_added, 2)

            def add_out(it, b):
                g = it * 2 + b
                for tt in range(TT):
                    dve.wait_ge(o_done, g * TT + tt + 3)
                    row = x_res[:, bass.ds(g * TT + tt, 1), :]
                    nc.vector.tensor_tensor(row, ps_o[tt][:, :], row, ALU.add).then_inc(o_added, 1)

            def weigh(it, b, k):
                g = it * 2 + b
                n = g * STEPS + k
                if k == 0:
                    dve.wait_ge(cs_loaded, g * 16 + 16)
                dve.wait_ge(att_done, n + 1)
                for s in range(SEQS):
                    c = s * STEPS + k
                    last = nc.vector.scalar_tensor_tensor(expo[k % 2][:, s, :], cs_all[:, c * P:(c + 1) * P], csT[:, bass.ds(g * NC + c, 1)],
                                                          mask[:, :], ALU.subtract, ALU.add)
                last.then_inc(expo_done, 1)
                dve.wait_ge(x_out, n + 3)
                dve.wait_ge(y_done, n + 1)
                dec = decay[:, bass.ds(g * NC, NC)].rearrange("p (s k) -> p s k", s=SEQS)[:, :, k:k + 1]
                nc.vector.tensor_tensor(b_dec[k % 2][:, :, :], ps_bx[k % 2][:, :].rearrange("p (s c) -> p s c", s=SEQS)[:, :, :STATE],
                                        dec.to_broadcast([P, SEQS, STATE]), ALU.mult).then_inc(b_out, 1)
                dve.wait_ge(sc_done, n + 1 + 2 * STEPS)
                dve.wait_ge(exp_done, n + 1)
                nc.vector.tensor_tensor(att[k % 2][:, :, :], ps_sc[k % 2][:, :].rearrange("p (s c) -> p s c", s=SEQS), expo[k % 2][:, :, :],
                                        ALU.mult).then_inc(att_done, 1)

            def update_state(it, b, k):
                g = it * 2 + b
                n = g * STEPS + k
                new = ps_st[:STATE, :SEQS * DHEAD].rearrange("p (s c) -> p s c", s=SEQS)
                if k > 0:
                    a = a_chunk[:STATE, bass.ds(g * NC, NC)].rearrange("p (s k) -> p s k", s=SEQS)[:, :, k:k + 1]
                    dve.wait_ge(state_done, g * (STEPS - 1) + k + 1)
                    nc.vector.tensor_tensor(state_dec[:, :, :], state[k % 2][:, :, :], a.to_broadcast([STATE, SEQS, DHEAD]), ALU.mult).then_inc(dec_done, 1)
                dve.wait_ge(y_done, n + 2)
                dve.wait_ge(st_done, g * (STEPS - 1) + k + 1)
                if k > 0:
                    dve.wait_ge(dec_done, g * (STEPS - 2) + k)
                    nc.vector.tensor_tensor(state[(k + 1) % 2][:, :, :], new, state_dec[:, :, :], ALU.add).then_inc(state_done, 1)
                else:
                    nc.vector.tensor_copy(state[1][:, :, :], new).then_inc(state_done, 1)

            def gate_outputs(it, b, k):
                g = it * 2 + b
                n = g * STEPS + k
                if k == 0:
                    dve.wait_ge(silu_done, g + 1)
                    dve.wait_ge(o_done, g * TT + 2)
                dve.wait_ge(y_done, n + 3)
                for s in range(SEQS):
                    last = nc.vector.tensor_tensor(chunk(gated, s, k), ps_y[:, s * DHEAD:(s + 1) * DHEAD].rearrange("p (h t) -> p h t", t=CHUNK_TOK),
                                                   chunk(gate[b], s, k), ALU.mult)
                last.then_inc(gated_done, 1)

            with dve.Fori(0, S_GROUPS // 2) as it:
                for b in range(2):
                    g = it * 2 + b
                    weigh(it, b, 0)
                    for k in range(STEPS):
                        if k + 1 < STEPS:
                            weigh(it, b, k + 1)
                            update_state(it, b, k)
                        if k == 0:
                            dve.wait_ge(cdec_exp, g + 2)
                            dve.wait_ge(c_loaded[b], it * 16 + 16)
                            by_head = c_dec[:, :].rearrange("p (c h t) -> p h c t", h=S_HEADS, t=CHUNK_TOK)
                            nc.vector.tensor_tensor(by_head, by_head, c_st[b][:, :, :].rearrange("p h (c t) -> p h c t", t=CHUNK_TOK),
                                                    ALU.mult).then_inc(cdec_done, 1)
                        gate_outputs(it, b, k)
                        if b == 1 and k == 1:
                            add_out(it, 0)
                add_out(it, 1)


def lut_feed_forward(nc, x_res, ident, w_ffn):
    with ExitStack() as outer:
        def osb(name, shape, dt=F32):
            return outer.enter_context(nc.sbuf_tensor(name, shape, dt))
        w_gate = osb("w_gate", [P, KD, INTER])
        w_up = osb("w_up", [P, KD, INTER])
        w_down = osb("w_down", [P, JT, D])
        w_loaded = nc.alloc_semaphore("w_ffn_loaded")
        with nc.Block() as block:
            flat = w_ffn.rearrange("c p j -> (c p j)")
            size = D * INTER
            FULL = JT - 1
            down = flat[2 * size:3 * size].rearrange("(i d) -> i d", d=D)

            @block.sync
            def _(sp):
                for n, w in enumerate((w_gate, w_up)):
                    sp.dma_start(w[:, :, :], flat[n * size:(n + 1) * size].rearrange("(k p i) -> p k i", p=P, i=INTER)).then_inc(w_loaded, 16)
                sp.dma_start(w_down[:, :FULL, :], down[:FULL * P, :].rearrange("(j p) d -> p j d", p=P)).then_inc(w_loaded, 16)
                sp.dma_start(w_down[:INTER - FULL * P, FULL, :], down[FULL * P:, :]).then_inc(w_loaded, 16)
        xnT = osb("f_xnT", [P, KD, N_TOK])
        layernorm_transposed(nc, "f_ln", x_res, xnT, None, ident)
        with ExitStack() as ctx:
            silu_g = ctx.enter_context(nc.sbuf_tensor("silu_g", [P, 2, GROUP], F32))
            hT = ctx.enter_context(nc.sbuf_tensor("hT", [P, JT, GROUP], F32))
            ps_g = [ctx.enter_context(nc.psum_tensor(f"ps_g{b}", [P, GROUP], F32)) for b in range(2)]
            ps_u = [ctx.enter_context(nc.psum_tensor(f"ps_u{b}", [P, GROUP], F32)) for b in range(2)]
            ps_d = [ctx.enter_context(nc.psum_tensor(f"ps_d{b}", [P, D], F32)) for b in range(2)]
            sem = nc.alloc_semaphore
            gate_done, up_done, silu_done, h_ready = sem("gate_done"), sem("up_done"), sem("silu_done"), sem("h_ready")
            down_done, added = sem("down_done"), sem("added")
            block = ctx.enter_context(nc.Block())
            rows = [min(P, INTER - j * P) for j in range(JT)]
            SUB = GROUP // P

            @block.tensor
            def _(pe):
                pe.sem_inc(down_done, 1)
                pe.wait_ge(w_loaded, 64)
                with pe.Fori(0, GROUPS // 2) as g2:
                    for gb in range(2):
                        g = g2 * 2 + gb
                        for j in range(JT):
                            b = (gb * JT + j) % 2
                            cols = slice(j * P, j * P + rows[j])
                            pe.wait_ge(silu_done, g * JT + j + 1)
                            for k in range(KD):
                                last = nc.tensor.matmul(ps_g[b][:rows[j], :], w_gate[:, k, cols], xnT[:, k, bass.ds(g * GROUP, GROUP)],
                                                        start=(k == 0), stop=(k == KD - 1))
                            last.then_inc(gate_done, 1)
                            pe.wait_ge(h_ready, g * JT + j + 1)
                            for k in range(KD):
                                last = nc.tensor.matmul(ps_u[b][:rows[j], :], w_up[:, k, cols], xnT[:, k, bass.ds(g * GROUP, GROUP)],
                                                        start=(k == 0), stop=(k == KD - 1))
                            last.then_inc(up_done, 1)
                        for s in range(SUB):
                            pe.wait_ge(added, g * SUB + s + 1)
                            for j in range(JT):
                                pe.wait_ge(h_ready, g * JT + j + 3)
                                last = nc.tensor.matmul(ps_d[s % 2][:, :], hT[:rows[j], j, s * P:(s + 1) * P], w_down[:rows[j], j, :],
                                                        start=(j == 0), stop=(j == JT - 1))
                            last.then_inc(down_done, 1)

            @block.scalar
            def _(act):
                act.sem_inc(silu_done, 2)
                with act.Fori(0, GROUPS // 2) as g2:
                    for gb in range(2):
                        for j in range(JT):
                            b = (gb * JT + j) % 2
                            n = (g2 * 2 + gb) * JT + j
                            act.wait_ge(gate_done, n + 1)
                            act.wait_ge(h_ready, n + 1)
                            nc.scalar.activation(silu_g[:rows[j], b, :], ps_g[b][:rows[j], :], ACT.Silu).then_inc(silu_done, 1)

            @block.vector
            def _(dve):
                dve.sem_inc(h_ready, 2)
                dve.sem_inc(added, 2)
                with dve.Fori(0, GROUPS // 2) as g2:
                    for gb in range(2):
                        g = g2 * 2 + gb
                        for j in range(JT):
                            b = (gb * JT + j) % 2
                            n = g * JT + j
                            dve.wait_ge(silu_done, n + 3)
                            dve.wait_ge(up_done, n + 1)
                            if j == 0:
                                dve.wait_ge(down_done, g * SUB + 1)
                            nc.vector.tensor_tensor(hT[:rows[j], j, :], ps_u[b][:rows[j], :], silu_g[:rows[j], b, :],
                                                    ALU.mult).then_inc(h_ready, 1)
                        for s in range(SUB):
                            dve.wait_ge(down_done, g * SUB + s + 2)
                            row = x_res[:, bass.ds(g * SUB + s, 1), :]
                            nc.vector.tensor_tensor(row, ps_d[s % 2][:, :], row, ALU.add).then_inc(added, 1)


def build_program(nc, t, out):
    with ExitStack() as ctx:
        x_res = ctx.enter_context(nc.sbuf_tensor("x_res", [P, TILES, D], F32))
        ident = ctx.enter_context(nc.sbuf_tensor("ident", [P, P], F32))
        w_ffn = nc.dram_tensor("w_ffn", (LOOKUPS, P, LOOKUP), F32).ap()
        load_tokens(nc, t["x"], x_res, ident)
        if '1' in STAGES:
            attention(nc, x_res, ident, t["w_qkv"], t["b_qk"], t["b_v"], t["wo"], t["bo"])
        if '2' in STAGES:
            mixture_of_experts(nc, x_res, ident, t["gate_wT"], t["w_gu"], t["w_dn"], t["lut"], t["idx"], w_ffn)
        if '3' in STAGES:
            state_space(nc, x_res, ident, t["w_proj"], t["w_dt"], t["s_w_out"])
        if '4' in STAGES:
            lut_feed_forward(nc, x_res, ident, w_ffn)
        store_tokens(nc, x_res, out)


def scan_columns(w_in, w_param):
    import numpy as np
    param = w_param.reshape(S_HEADS, 1 + 2 * STATE, D)
    b_x = np.concatenate([param[:, 1:1 + STATE], w_in[:D_INNER].reshape(S_HEADS, DHEAD, D)], axis=1)
    c_pairs = param[:, 1 + STATE:].reshape(S_HEADS // 2, P, D)
    gate = w_in[D_INNER:].reshape(-1, P, D)
    return {
        "w_proj": np.ascontiguousarray(np.concatenate([b_x, c_pairs, gate]).transpose(0, 2, 1)),
        "w_dt": np.ascontiguousarray(param[:, 0].T),
    }


def expert_columns(gate, up):
    import numpy as np
    return np.ascontiguousarray(np.concatenate([gate[:, :P], up[:, :P], gate[:, P:], up[:, P:]], axis=1).transpose(0, 2, 1))


def lay_out(inputs):
    import numpy as np
    c = np.ascontiguousarray
    a = {k: np.asarray(v) for k, v in inputs.items()}
    return {
        "x": c(a["L0_attn_x"].reshape(N_TOK, D)),
        "w_qkv": c(np.concatenate([a["L0_attn_" + n].transpose(1, 0, 2).reshape(D, D) for n in ("Wq", "Wk", "Wv")], axis=1)),
        "b_qk": c(np.concatenate([a["L0_attn_" + n].reshape(D) for n in ("bq", "bk")]).reshape(-1, P).T),
        "b_v": c(a["L0_attn_bv"].reshape(D)),
        "wo": c(a["L0_attn_Wo"]),
        "bo": c(a["L0_attn_bo"]),
        "gate_wT": c(a["L0_ffn_gate_w"].T),
        "w_gu": expert_columns(a["L0_ffn_w_gate_proj"], a["L0_ffn_w_up_proj"]),
        "w_dn": c(a["L0_ffn_w_down_proj"].transpose(0, 2, 1)),
        **scan_columns(a["L1_attn_w_in"], a["L1_attn_w_param"]),
        "s_w_out": c(a["L1_attn_w_out"].T),
        "lut": c(a["L1_ffn_lut"]),
        "idx": c(np.concatenate([a["L1_ffn_" + n].T.reshape(-1) for n in ("gate_idx", "up_idx", "down_idx")]).reshape(LOOKUPS, P, LOOKUP)),
    }


def kernel(**inputs):
    import concourse.bacc as bacc
    from concourse.bass_utils import run_bass_kernel_spmd

    arrays = lay_out(inputs)
    nc = bacc.Bacc("TRN2", target_bir_lowering=False, num_devices=1)
    t = {n: nc.dram_tensor(n, a.shape, mybir.dt.from_np(a.dtype), kind="ExternalInput").ap() for n, a in arrays.items()}
    out = nc.dram_tensor("out", (N_TOK, D), F32, kind="ExternalOutput").ap()
    build_program(nc, t, out)
    r = run_bass_kernel_spmd(nc, [arrays], core_ids=[0])
    return r.results[0]["out"].reshape(2, N_TOK // 2, D)
```

```python
import concourse.bass as bass
from concourse import mybir
from contextlib import ExitStack

STAGES = '1234'

F32 = mybir.dt.float32
I32 = mybir.dt.int32
ALU = mybir.AluOpType
ACT = mybir.ActivationFunctionType
AX = mybir.AxisListType

P = 128
N_TOK = 2048
D = 512
KD = D // P
TILES = N_TOK // P
GROUP = 512
GROUPS = N_TOK // GROUP
LN_EPS = 1e-5
INTER = 1376
JT = -(-INTER // P)
LUT = 16
F32R = mybir.dt.float32r
BF16 = mybir.dt.bfloat16
HEADS = 16
DH = D // HEADS
BATCH = 2
T = N_TOK // BATCH
TB = T // P
SCALE = DH ** -0.5
NEG = -1.0e30


def semaphores(ctx, nc):
    taken = []

    def clear():
        nc.clear_and_free_semaphores(taken)
        with nc.Block():
            pass
    ctx.callback(clear)

    def sem(name):
        taken.append(nc.alloc_semaphore(name))
        return taken[-1]
    return sem


def load_tokens(nc, x_in, x_res, ident):
    with ExitStack() as ctx:
        x_loaded = ctx.enter_context(nc.semaphore("x_loaded"))
        ident_zeroed = ctx.enter_context(nc.semaphore("ident_zeroed"))
        block = ctx.enter_context(nc.Block())

        @block.sync
        def _(sp):
            sp.dma_start(x_res[:, :, :], x_in.rearrange("(n p) d -> p n d", p=P)).then_inc(x_loaded, 16)
            sp.wait_ge(x_loaded, 16)

        @block.gpsimd
        def _(pool):
            pool.memset(ident[:, :], 0.0).then_inc(ident_zeroed, 1)
            pool.wait_ge(ident_zeroed, 1)
            pool.affine_select(out=ident[:, :], in_=ident[:, :], compare_op=ALU.not_equal, fill=1.0,
                               base=0, pattern=[[-1, P]], channel_multiplier=1)


def store_tokens(nc, x_res, out):
    with ExitStack() as ctx:
        stored = ctx.enter_context(nc.semaphore("out_stored"))
        block = ctx.enter_context(nc.Block())

        @block.sync
        def _(sp):
            sp.dma_start(out.rearrange("(n p) d -> p n d", p=P), x_res[:, :, :]).then_inc(stored, 16)
            sp.wait_ge(stored, 16)


def layernorm_transposed(nc, name, x_res, x_hi, x_lo, ident):
    with ExitStack() as ctx:
        stats = ctx.enter_context(nc.sbuf_tensor(name + "_stats", [P, TILES, 6], F32))
        mv = ctx.enter_context(nc.sbuf_tensor(name + "_mv", [P, TILES, 2], F32))
        var_eps = ctx.enter_context(nc.sbuf_tensor(name + "_var_eps", [P, TILES], F32))
        std = ctx.enter_context(nc.sbuf_tensor(name + "_std", [P, TILES], F32))
        rstd = ctx.enter_context(nc.sbuf_tensor(name + "_rstd", [P, TILES], F32))
        xn = ctx.enter_context(nc.sbuf_tensor(name + "_xn", [P, 2, D], F32))
        ps = [ctx.enter_context(nc.psum_tensor(f"{name}_tps{b}", [P, KD, P], F32)) for b in range(2)]
        sem = semaphores(ctx, nc)
        stats_done = sem(name + "_stats_done")
        moments_done = sem(name + "_moments_done")
        std_done = sem(name + "_std_done")
        rstd_done = sem(name + "_rstd_done")
        xn_ready = sem(name + "_xn_ready")
        transposed = sem(name + "_transposed")
        hi_done = sem(name + "_hi_done")
        lo_done = sem(name + "_lo_done")
        block = ctx.enter_context(nc.Block())

        @block.vector
        def _(dve):
            with dve.Fori(0, TILES) as i:
                nc.vector.bn_stats(stats[:, bass.ds(i, 1), :], x_res[:, bass.ds(i, 1), :]).then_inc(stats_done, 1)
            dve.wait_ge(stats_done, TILES)
            for i in range(TILES):
                nc.vector.bn_aggr(mv[:, i, :], stats[:, i, :]).then_inc(moments_done, 1)
            dve.wait_ge(moments_done, TILES)
            nc.vector.tensor_scalar_add(var_eps[:, :], mv[:, :, 1], LN_EPS).then_inc(moments_done, 1)
            dve.wait_ge(std_done, 1)
            nc.vector.reciprocal(rstd[:, :], std[:, :]).then_inc(rstd_done, 1)
            dve.wait_ge(rstd_done, 1)
            dve.sem_inc(lo_done, 2)

            def low_part(i, b):
                dve.wait_ge(hi_done, i + 3)
                toks = bass.ds(i * P, P)
                nc.vector.tensor_tensor(x_lo[:, :, toks], ps[b][:, :, :], x_hi[:, :, toks].bitcast(F32), ALU.subtract).then_inc(lo_done, 1)

            with dve.Fori(0, TILES // 2) as pair:
                for b in range(2):
                    i = pair * 2 + b
                    dve.wait_ge(transposed, i + 1)
                    nc.vector.tensor_scalar(xn[:, b, :], x_res[:, bass.ds(i, 1), :], mv[:, bass.ds(i, 1), 0],
                                            rstd[:, bass.ds(i, 1)], ALU.subtract, ALU.mult).then_inc(xn_ready, 1)
                for b in range(0 if x_lo is None else 2):
                    low_part(pair * 2 + b, b)

        @block.scalar
        def _(act):
            act.sem_inc(hi_done, 2)
            act.wait_ge(moments_done, TILES + 1)
            nc.scalar.activation(std[:, :], var_eps[:, :], ACT.Sqrt).then_inc(std_done, 1)
            with act.Fori(0, TILES // 2) as pair:
                for b in range(2):
                    i = pair * 2 + b
                    act.wait_ge(transposed, i + 3)
                    nc.scalar.copy(x_hi[:, :, bass.ds(i * P, P)], ps[b][:, :, :]).then_inc(hi_done, 1)

        @block.tensor
        def _(pe):
            pe.sem_inc(transposed, 2)
            with pe.Fori(0, TILES // 2) as pair:
                for b in range(2):
                    i = pair * 2 + b
                    pe.wait_ge(xn_ready, i + 1)
                    pe.wait_ge(hi_done if x_lo is None else lo_done, i + 1)
                    for k in range(KD):
                        last = nc.tensor.transpose(ps[b][:, k, :], xn[:, b, k * P:(k + 1) * P], ident[:, :])
                    last.then_inc(transposed, 1)


def split_weights(nc, name, jobs):
    width = max(src.free_size() for src, _, _ in jobs)
    with ExitStack() as ctx:
        stage = [ctx.enter_context(nc.sbuf_tensor(f"{name}_stage{b}", [P, width], F32)) for b in range(2)]
        loaded = [ctx.enter_context(nc.semaphore(f"{name}_loaded{b}")) for b in range(2)]
        hi_done = ctx.enter_context(nc.semaphore(name + "_hi_done"))
        lo_done = ctx.enter_context(nc.semaphore(name + "_lo_done"))
        block = ctx.enter_context(nc.Block())

        def view(n):
            hi = jobs[n][1]
            v = stage[n % 2][:hi.shape[0], :hi.free_size()]
            return v.rearrange("p (a d) -> p a d", a=hi.shape[1]) if len(hi.shape) == 3 else v

        @block.sync
        def _(sp):
            for n, (src, _, _) in enumerate(jobs):
                if n >= 2:
                    sp.wait_ge(lo_done, n - 1)
                sp.dma_start(view(n), src).then_inc(loaded[n % 2], 16)

        @block.scalar
        def _(act):
            for n, (_, hi, _) in enumerate(jobs):
                act.wait_ge(loaded[n % 2], 16 * (n // 2 + 1))
                nc.scalar.copy(hi, view(n)).then_inc(hi_done, 1)

        @block.vector
        def _(dve):
            for n, (_, hi, lo) in enumerate(jobs):
                dve.wait_ge(hi_done, n + 1)
                nc.vector.tensor_tensor(lo, view(n), hi.bitcast(F32), ALU.subtract).then_inc(lo_done, 1)


def attention(nc, x_res, ident, w, b_qk, b_v, wo, bo):
    qk = {n: nc.dram_tensor(f"{n}_parts", (HEADS, 2, DH, N_TOK), F32).ap() for n in "qk"}
    with ExitStack() as ctx:
        inv_sums = nc.dram_tensor("inv_sums", (HEADS, N_TOK), F32).ap()
        v_rows = ctx.enter_context(nc.sbuf_tensor("v_rows", [P, TILES, D], F32))
        yT = nc.dram_tensor("yT_and_sums", (HEADS, DH + 1, N_TOK), F32).ap()
        with ExitStack() as inner:
            x_hi = inner.enter_context(nc.sbuf_tensor("a_x_hi", [P, KD, N_TOK], F32R))
            x_lo = inner.enter_context(nc.sbuf_tensor("a_x_lo", [P, KD, N_TOK], F32R))
            w_hi = inner.enter_context(nc.sbuf_tensor("w_qkv_hi", [P, KD, 3 * D], F32R))
            w_lo = inner.enter_context(nc.sbuf_tensor("w_qkv_lo", [P, KD, 3 * D], F32R))
            layernorm_transposed(nc, "a_ln", x_res, x_hi, x_lo, ident)
            split_weights(nc, "w_qkv", [(w[k * P:(k + 1) * P, :], w_hi[:, k, :], w_lo[:, k, :]) for k in range(KD)])
            project_qkv(nc, x_hi, x_lo, w_hi, w_lo, b_qk, b_v, qk, v_rows)
        attend(nc, qk, v_rows, yT)
        wo_hi = ctx.enter_context(nc.sbuf_tensor("wo_hi", [P, KD, D], F32R))
        wo_lo = ctx.enter_context(nc.sbuf_tensor("wo_lo", [P, KD, D], F32R))
        split_weights(nc, "wo", [(wo.rearrange("(k p) d -> p k d", p=P), wo_hi[:, :, :], wo_lo[:, :, :])])
        output_projection(nc, x_res, yT, inv_sums, wo_hi, wo_lo, bo)


def project_qkv(nc, x_hi, x_lo, w_hi, w_lo, b_qk, b_v, qk, v_rows):
    MT = 2 * D // P
    HT = P // DH
    BUFS = 4
    with ExitStack() as ctx:
        sb = lambda n, s, dt=F32: ctx.enter_context(nc.sbuf_tensor(n, s, dt))
        bias, bias_v = sb("b_qk_sb", [P, MT]), sb("b_v_sb", [P, D])
        hi, lo = sb("qk_hi", [P, 2, GROUP], F32R), sb("qk_lo", [P, 2, GROUP], F32R)
        ps = [ctx.enter_context(nc.psum_tensor(f"qk_ps{i}", [P, GROUP], F32)) for i in range(BUFS)]
        ps_v = [ctx.enter_context(nc.psum_tensor(f"v_ps{i}", [P, D], F32)) for i in range(2)]
        sem = nc.alloc_semaphore
        bias_loaded, product, hi_done, lo_done, v_product, v_added = (
            sem("bias_loaded"), sem("qk_product"), sem("qk_hi_done"), sem("qk_lo_done"), sem("v_product"), sem("v_added"))
        stored = [sem(f"qk_stored{b}") for b in range(2)]
        block = ctx.enter_context(nc.Block())

        @block.tensor
        def _(pe):
            with pe.Fori(0, GROUPS) as g:
                for m in range(MT):
                    pe.wait_ge(lo_done, g * MT + m + 1)
                    toks = bass.ds(g * GROUP, GROUP)
                    terms = [(w_hi, x_hi), (w_lo, x_hi), (w_hi, x_lo)]
                    for n, (k, (a, x)) in enumerate([(k, t) for k in range(KD) for t in terms]):
                        last = nc.tensor.matmul(ps[m % BUFS][:, :], a[:, k, m * P:(m + 1) * P], x[:, k, toks],
                                                start=(n == 0), stop=(n == 3 * KD - 1))
                    last.then_inc(product, 1)
            for i in range(TILES):
                if i >= 2:
                    pe.wait_ge(v_added, i - 1)
                terms = [(x_hi, w_hi), (x_lo, w_hi), (x_hi, w_lo)]
                for n, (k, (x, a)) in enumerate([(k, t) for k in range(KD) for t in terms]):
                    last = nc.tensor.matmul(ps_v[i % 2][:, :], x[:, k, i * P:(i + 1) * P], a[:, k, 2 * D:3 * D],
                                            start=(n == 0), stop=(n == 3 * KD - 1))
                last.then_inc(v_product, 1)

        @block.scalar
        def _(act):
            for b in range(2):
                act.sem_inc(stored[b], 32)
            act.wait_ge(bias_loaded, 32)
            with act.Fori(0, GROUPS) as g:
                for m in range(MT):
                    act.wait_ge(product, g * MT + m + 1)
                    act.wait_ge(stored[m % 2], (g * (MT // 2) + m // 2 + 1) * 32)
                    nc.scalar.activation(hi[:, m % 2, :], ps[m % BUFS][:, :], ACT.Identity, bias=bias[:, m:m + 1]).then_inc(hi_done, 1)

        @block.vector
        def _(dve):
            dve.sem_inc(lo_done, BUFS)
            with dve.Fori(0, GROUPS) as g:
                for m in range(MT):
                    dve.wait_ge(hi_done, g * MT + m + 1)
                    nc.vector.scalar_tensor_tensor(lo[:, m % 2, :], ps[m % BUFS][:, :], bias[:, m:m + 1],
                                                   hi[:, m % 2, :].bitcast(F32), ALU.add, ALU.subtract).then_inc(lo_done, 1)
            for i in range(TILES):
                dve.wait_ge(v_product, i + 1)
                nc.vector.tensor_tensor(v_rows[:, i, :], ps_v[i % 2][:, :], bias_v[:, :], ALU.add).then_inc(v_added, 1)

        @block.sync
        def _(sp):
            sp.dma_start(bias[:, :], b_qk).then_inc(bias_loaded, 16)
            sp.dma_start(bias_v[:, :], b_v.partition_broadcast(P)).then_inc(bias_loaded, 16)
            with sp.Fori(0, GROUPS) as g:
                for m in range(MT):
                    h0 = (m % (MT // 2)) * HT
                    dst = qk["qk"[m // (MT // 2)]]
                    sp.wait_ge(lo_done, g * MT + m + 1 + BUFS)
                    for part, buf in ((0, hi), (1, lo)):
                        sp.dma_start(dst[h0:h0 + HT, part, :, bass.ds(g * GROUP, GROUP)],
                                     buf[:, m % 2, :].bitcast(F32)).then_inc(stored[m % 2], 16)
            for b in range(2):
                sp.wait_ge(stored[b], 32 * (GROUPS * MT // 2 + 1))


def attend(nc, qk, v_rows, yT):
    PAIRS = BATCH * HEADS
    E = 4
    BODIES = PAIRS // E
    CHUNKS_C = [(sb, max(sb * P, t0), t0 + 512 - max(sb * P, t0)) for sb in range(TB) for t0 in range(0, T, 512) if sb * P < t0 + 512]
    NCH = len(CHUNKS_C)
    RING = 4
    LAG = 2
    K_QK = 3 * DH
    CONSTS = 13 + E
    assert NCH % RING == 0
    with ExitStack() as ctx:
        sb = lambda n, s, dt=F32: ctx.enter_context(nc.sbuf_tensor(n, s, dt))
        q_st, k_st = [sb(f"q_st{b}", [P, T], F32R) for b in range(E)], [sb(f"k_st{b}", [P, T], F32R) for b in range(E)]
        v_pair = [sb(f"v_pair{b}", [P, TB, DH + 1]) for b in range(2)]
        probs = [sb(f"probs{b}", [P, 512]) for b in range(RING)]
        y_st = [sb(f"y_st{b}", [DH + 1, T]) for b in range(2)]
        neg_max = sb("neg_max", [P, TB])
        max_cols = sb("max_cols", [P, TB, P], F32R)
        ident, ident_r, ones, zeros = sb("att_ident", [P, P]), sb("ident_r", [P, P], F32R), sb("ones", [P, T]), sb("zeros", [P, TB, P])
        ident_bf, mask, mask_T = sb("ident_bf", [P, P], BF16), sb("causal_mask", [P, P], BF16), sb("causal_mask_T", [P, P], BF16)
        ps_r = [ctx.enter_context(nc.psum_tensor(f"ps_r{b}", [P, T], F32)) for b in range(2)]
        ps_c = [ctx.enter_context(nc.psum_tensor(f"ps_c{b}", [P, 512], F32)) for b in range(2)]
        ps_y = ctx.enter_context(nc.psum_tensor("ps_y", [P, T], F32))
        sem = nc.alloc_semaphore
        staged, y_stored = [sem(f"staged{b}") for b in range(E)], [sem(f"y_stored{b}") for b in range(2)]
        consts, rows_done, max_done, parts_done, turned, shift_ready, cols_done, exp_done, v_ready, pv_done, y_done, turns_begun, loads_begun = [
            sem(n) for n in ("att_consts", "rows_done", "max_done", "max_parts_done", "max_turned", "shift_ready", "cols_done", "exp_done", "v_ready",
                             "pv_done", "y_done", "v_turns_begun", "q_loads_begun")]
        block = ctx.enter_context(nc.Block())
        head = lambda it, e: it * (E // 2) + e // 2
        after = lambda it, e: (it, e + 1) if e + 1 < E else (it + 1, 0)

        @block.gpsimd
        def _(pool):
            for t, value in ((mask, 0.0), (mask_T, 0.0), (ident, 0.0), (ones, 1.0)):
                pool.memset(t[:, :], value).then_inc(consts, 1)
            pool.memset(zeros[:, :, :], 0.0).then_inc(consts, 1)
            for b in range(2):
                pool.memset(v_pair[b][:, :, DH:], 1.0).then_inc(consts, 1)
            pool.wait_ge(consts, 7)
            pool.affine_select(out=mask[:, :], in_=mask[:, :], compare_op=ALU.is_ge, fill=NEG,
                               base=0, pattern=[[-1, P]], channel_multiplier=1).then_inc(consts, 1)
            pool.affine_select(out=mask_T[:, :], in_=mask_T[:, :], compare_op=ALU.is_ge, fill=NEG,
                               base=0, pattern=[[1, P]], channel_multiplier=-1).then_inc(consts, 1)
            pool.affine_select(out=ident[:, :], in_=ident[:, :], compare_op=ALU.not_equal, fill=1.0,
                               base=0, pattern=[[-1, P]], channel_multiplier=1).then_inc(consts, 1)
            with pool.Fori(0, BODIES) as it:
                for e in range(E):
                    p = it * E + e
                    pool.wait_ge(pv_done, (p + 1) * NCH)
                    pool.sem_inc(turns_begun, 1)
                    nc.gpsimd.tensor_copy(v_pair[e % 2][:, :, :DH],
                                          v_rows[:, e % 2 * TB:(e % 2 + 1) * TB, bass.ds(head(it, e) * DH, DH)]).then_inc(v_ready, 1)

        @block.sync
        def _(sp):
            sp.sem_inc(y_stored[0], 16)
            sp.sem_inc(y_stored[1], 16)

            def load(it, e):
                sp.wait_ge(cols_done, (it * E + e + 1) * NCH)
                sp.sem_inc(loads_begun, 1)
                toks = slice(e % 2 * T, (e % 2 + 1) * T)
                parts = lambda n, a, b: qk[n][bass.ds(head(it, e), 1), a:b, :, toks].rearrange("h a d t -> (h a d) t")
                for rows, n, part0, part1 in ((0, "q", 0, 2), (2, "q", 0, 1), (0, "k", 0, 1), (1, "k", 0, 2)):
                    dst = (q_st if n == "q" else k_st)[e][rows * DH:(rows + part1 - part0) * DH, :]
                    sp.dma_start(dst.bitcast(F32), parts(n, part0, part1)).then_inc(staged[e], 16)

            def store(it, e):
                sp.wait_ge(y_done, it * E + e + 2)
                sp.sem_inc(loads_begun, 1)
                sp.dma_start(yT[bass.ds(head(it, e), 1), :, e % 2 * T:(e % 2 + 1) * T].rearrange("h d t -> (h d) t"), y_st[e % 2][:, :]).then_inc(y_stored[e % 2], 16)

            for e in range(E):
                load(0, e)
            with sp.Fori(0, BODIES - 1) as it:
                for e in range(E):
                    store(it, e)
                    load(it + 1, e)
            for e in range(E):
                store(BODIES - 1, e)
            for b in range(2):
                sp.wait_ge(y_stored[b], 16 * (PAIRS // 2 + 1))

        @block.tensor
        def _(pe):
            pe.sem_inc(cols_done, E * NCH)
            pe.sem_inc(pv_done, 2 * NCH)

            def rows(it, e, i):
                p, tb = it * E + e, TB - 1 - i
                if i == 0:
                    pe.wait_ge(staged[e], (it + 1) * 64)
                    if not (isinstance(it, int) and it == 0 and e == 0):
                        pe.wait_ge(shift_ready, p)
                pe.wait_ge(max_done, p * TB + i + 1)
                ps, width = ps_r[i % 2], (tb + 1) * P
                for c in range(0, width, 512):
                    n_c = min(512, width - c)
                    nc.tensor.matmul(ps[:, c:c + n_c], q_st[e][:K_QK, tb * P:(tb + 1) * P], k_st[e][:K_QK, c:c + n_c], start=True, stop=(c + n_c < width))
                nc.tensor.matmul(ps[:, tb * P:width], ident_bf[:, :], mask[:, :], start=False, stop=True).then_inc(rows_done, 1)

            def turn_maxima(it, e):
                pe.wait_ge(parts_done, (it * E + e + 1) * 2)
                for tb in range(TB):
                    last = nc.tensor.matmul(ps_r[0][:, tb * P:(tb + 1) * P], max_cols[:, tb, :], ident_r[:, :], start=True, stop=True)
                last.then_inc(turned, 1)

            def columns(it, e, j):
                s, t0, width = CHUNKS_C[j]
                if j == 0:
                    pe.wait_ge(shift_ready, it * E + e + 1)
                pe.wait_ge(exp_done, (it * E + e) * NCH + j + 1)
                diagonal = t0 == s * P
                last = nc.tensor.matmul(ps_c[j % 2][:, :width], k_st[e][:, s * P:(s + 1) * P], q_st[e][:, t0:t0 + width], start=True, stop=not diagonal)
                if diagonal:
                    last = nc.tensor.matmul(ps_c[j % 2][:, :P], ident_bf[:, :], mask_T[:, :], start=False, stop=True)
                last.then_inc(cols_done, 1)

            def output(it, e, j):
                p = it * E + e
                s, t0, width = CHUNKS_C[j]
                if j == 0:
                    pe.wait_ge(v_ready, p + 1)
                    pe.wait_ge(y_done, p + 1)
                pe.wait_ge(exp_done, p * NCH + j + 3)
                nc.tensor.matmul(ps_y[:DH + 1, t0:t0 + width], v_pair[e % 2][:, s, :], probs[j % RING][:, :width],
                                 start=(s == 0), stop=(t0 + width == (s + 1) * P)).then_inc(pv_done, 1)

            def body(it, final):
                for e in range(E):
                    more = not (final and e == E - 1)
                    for j in range(NCH):
                        columns(it, e, j)
                        if more and j < TB:
                            rows(*after(it, e), j)
                        if more and j == NCH - 1:
                            turn_maxima(*after(it, e))
                        if j >= LAG:
                            output(it, e, j - LAG)
                    for j in range(NCH - LAG, NCH):
                        output(it, e, j)

            pe.wait_ge(consts, CONSTS)
            for i in range(TB):
                rows(0, 0, i)
            turn_maxima(0, 0)
            with pe.Fori(0, BODIES - 1) as it:
                body(it, False)
            body(BODIES - 1, True)

        @block.scalar
        def _(act):
            act.sem_inc(exp_done, 2)
            with act.Fori(0, BODIES) as it:
                for e in range(E):
                    p = it * E + e
                    for j, (_, _, width) in enumerate(CHUNKS_C):
                        act.wait_ge(pv_done, p * NCH + j - RING + 1 + 2 * NCH)
                        act.wait_ge(cols_done, (p + E) * NCH + j + 1)
                        nc.scalar.activation(probs[j % RING][:, :width], ps_c[j % 2][:, :width], ACT.Exp, scale=SCALE).then_inc(exp_done, 1)

        @block.vector
        def _(dve):
            dve.wait_ge(consts, 10)
            nc.vector.tensor_copy(ident_bf[:, :], ident[:, :]).then_inc(consts, 1)
            nc.vector.tensor_copy(ident_r[:, :], ident[:, :]).then_inc(consts, 1)
            nc.vector.tensor_copy(max_cols[:, :, :], zeros[:, :, :]).then_inc(consts, 1)
            for b in range(E):
                nc.vector.tensor_copy(k_st[b][K_QK:, :], ones[K_QK:, :]).then_inc(consts, 1)
            dve.wait_ge(consts, CONSTS)
            dve.sem_inc(max_done, 2)
            dve.sem_inc(y_done, 1)

            def maxima(it, e):
                p = it * E + e
                for i in range(TB):
                    tb = TB - 1 - i
                    dve.wait_ge(rows_done, p * TB + i + 1)
                    nc.vector.tensor_reduce(neg_max[:, tb:tb + 1], ps_r[i % 2][:, :(tb + 1) * P], AX.X, ALU.max, negate=True).then_inc(max_done, 1)
                dve.wait_ge(max_done, p * TB + TB + 2)
                nc.vector.tensor_copy(max_cols[:, :, K_QK], neg_max[:, :]).then_inc(parts_done, 1)
                dve.wait_ge(parts_done, p * 2 + 1)
                nc.vector.tensor_tensor(max_cols[:, :, K_QK + 1], neg_max[:, :], max_cols[:, :, K_QK].bitcast(F32), ALU.subtract).then_inc(parts_done, 1)
                dve.wait_ge(turned, p + 1)
                nc.vector.tensor_copy(q_st[e][K_QK:, :], ps_r[0][K_QK:, :]).then_inc(shift_ready, 1)

            def evacuate(it, e):
                p = it * E + e
                dve.wait_ge(pv_done, (p + 3) * NCH)
                dve.wait_ge(y_stored[e % 2], (it * (E // 2) + e // 2 + 1) * 16)
                nc.vector.tensor_copy(y_st[e % 2][:, :], ps_y[:DH + 1, :]).then_inc(y_done, 1)

            def body(it, final):
                for e in range(E):
                    if not (final and e == E - 1):
                        maxima(*after(it, e))
                    evacuate(it, e)

            maxima(0, 0)
            with dve.Fori(0, BODIES - 1) as it:
                body(it, False)
            body(BODIES - 1, True)


def output_projection(nc, x_res, yT, inv_sums, wo_hi, wo_lo, bo):
    SUB = GROUP // P
    with ExitStack() as ctx:
        sb = lambda n, s, dt=F32: ctx.enter_context(nc.sbuf_tensor(n, s, dt))
        y = [sb(f"o_y{b}", [P, KD, GROUP]) for b in range(2)]
        y_hi, y_lo = [sb(f"y_hi{b}", [P, KD, GROUP], F32R) for b in range(2)], [sb(f"y_lo{b}", [P, KD, GROUP], F32R) for b in range(2)]
        inv = [sb(f"o_inv{b}", [P, KD, GROUP]) for b in range(2)]
        bo_all, sums = sb("bo_all", [P, D]), sb("o_sums", [P, HEADS * N_TOK // P])
        HT = P // DH
        ps_o = [ctx.enter_context(nc.psum_tensor(f"o_ps_o{b}", [P, D], F32)) for b in range(SUB)]
        sem = nc.alloc_semaphore
        loaded = [sem(f"o_loaded{b}") for b in range(2)]
        sums_loaded, inverted, inv_stored, y_ready = sem("sums_loaded"), sem("sums_inverted"), sem("inv_stored"), sem("o_y_ready")
        bo_loaded, bo_added, hi_done, lo_done, product, added = (
            sem("bo_loaded"), sem("bo_added"), sem("o_hi_done"), sem("o_lo_done"), sem("o_product"), sem("o_added"))
        block = ctx.enter_context(nc.Block())

        @block.sync
        def _(sp):
            rows = sums.shape[1]
            for h in range(HEADS):
                per = P // HEADS
                sp.dma_start(sums[h * per:(h + 1) * per, :], yT[h, DH, :].rearrange("(a t) -> a t", t=rows)).then_inc(sums_loaded, 16)
            sp.dma_start(bo_all[:, :], bo.partition_broadcast(P)).then_inc(bo_loaded, 16)
            sp.wait_ge(inverted, 1)
            sp.dma_start(inv_sums.rearrange("h (a t) -> (h a) t", t=rows), sums[:, :]).then_inc(inv_stored, 16)
            sp.wait_ge(inv_stored, 16)
            for g in range(GROUPS):
                toks = slice(g * GROUP, (g + 1) * GROUP)
                if g >= 2:
                    sp.wait_ge(lo_done, g - 1)
                for h in range(HT):
                    rows_h = slice(h * DH, (h + 1) * DH)
                    sp.dma_start(y[g % 2][rows_h, :, :], yT[h::HT, :DH, toks].rearrange("k d t -> d k t")).then_inc(loaded[g % 2], 16)
                    sp.dma_start(inv[g % 2][rows_h, :, :], inv_sums[h::HT, toks].partition_broadcast(DH)).then_inc(loaded[g % 2], 16)

        @block.gpsimd
        def _(pool):
            pool.wait_ge(bo_loaded, 16)
            with pool.Fori(0, TILES) as i:
                nc.gpsimd.tensor_tensor(x_res[:, bass.ds(i, 1), :], x_res[:, bass.ds(i, 1), :], bo_all[:, :], ALU.add).then_inc(bo_added, 1)

        @block.tensor
        def _(pe):
            for g in range(GROUPS):
                b = g % 2
                pe.wait_ge(lo_done, g + 1)
                for s in range(SUB):
                    if g > 0:
                        pe.wait_ge(added, (g - 1) * SUB + s + 1)
                    terms = [(y_hi[b], wo_hi), (y_lo[b], wo_hi), (y_hi[b], wo_lo)]
                    for n, (k, (yt, w)) in enumerate([(k, t) for k in range(KD) for t in terms]):
                        last = nc.tensor.matmul(ps_o[s][:, :], yt[:, k, s * P:(s + 1) * P], w[:, k, :], start=(n == 0), stop=(n == 3 * KD - 1))
                    last.then_inc(product, 1)

        @block.scalar
        def _(act):
            for g in range(GROUPS):
                act.wait_ge(y_ready, g + 1)
                if g >= 2:
                    act.wait_ge(product, (g - 1) * SUB)
                nc.scalar.copy(y_hi[g % 2][:, :, :], y[g % 2][:, :, :]).then_inc(hi_done, 1)

        @block.vector
        def _(dve):
            def add(g):
                for s in range(SUB):
                    i = g * SUB + s
                    dve.wait_ge(product, i + 1)
                    dve.wait_ge(bo_added, i + 1)
                    nc.vector.tensor_tensor(x_res[:, i, :], ps_o[s][:, :], x_res[:, i, :], ALU.add).then_inc(added, 1)

            dve.wait_ge(sums_loaded, 16 * HEADS)
            nc.vector.reciprocal(sums[:, :], sums[:, :]).then_inc(inverted, 1)
            for g in range(GROUPS):
                dve.wait_ge(loaded[g % 2], 32 * HT * (g // 2 + 1))
                nc.vector.tensor_tensor(y[g % 2][:, :, :], y[g % 2][:, :, :], inv[g % 2][:, :, :], ALU.mult).then_inc(y_ready, 1)
                dve.wait_ge(hi_done, g + 1)
                nc.vector.tensor_tensor(y_lo[g % 2][:, :, :], y[g % 2][:, :, :], y_hi[g % 2][:, :, :].bitcast(F32), ALU.subtract).then_inc(lo_done, 1)
                if g > 0:
                    add(g - 1)
            add(GROUPS - 1)


LOOKUP = 258
LOOKUPS = 3 * INTER * D // P // LOOKUP
EXPERTS = 32
TOP_K = 8
INTER_E = 192
REST_E = INTER_E - P


def mixture_of_experts(nc, x_res, ident, gate_wT, w_gu, w_dn, lut, idx, w_ffn):
    with ExitStack() as ctx:
        x_hi = ctx.enter_context(nc.sbuf_tensor("m_x_hi", [P, KD, N_TOK], F32R))
        x_lo = ctx.enter_context(nc.sbuf_tensor("m_x_lo", [P, KD, N_TOK], F32R))
        routing = ctx.enter_context(nc.sbuf_tensor("routing", [P, TILES, EXPERTS], F32))
        layernorm_transposed(nc, "m_ln", x_res, x_hi, x_lo, ident)
        with ExitStack() as inner:
            gw_hi = inner.enter_context(nc.sbuf_tensor("gw_hi", [P, KD, EXPERTS], F32R))
            gw_lo = inner.enter_context(nc.sbuf_tensor("gw_lo", [P, KD, EXPERTS], F32R))
            split_weights(nc, "gw", [(gate_wT.rearrange("(k p) e -> p k e", p=P), gw_hi[:, :, :], gw_lo[:, :, :])])
            route(nc, x_hi, x_lo, gw_hi, gw_lo, routing)
        experts(nc, x_res, x_hi, x_lo, routing, w_gu, w_dn, lut, idx, w_ffn)


def route(nc, x_hi, x_lo, gw_hi, gw_lo, routing):
    TAKEN = -3.0e38
    with ExitStack() as ctx:
        sb = lambda n, s: ctx.enter_context(nc.sbuf_tensor(n, s, F32))
        logits, shifted, weight = sb("logits", [P, TILES, EXPERTS]), sb("shifted", [P, TILES, EXPERTS]), sb("weight", [P, TILES, EXPERTS])
        rest, chosen = sb("rest", [P, TILES, EXPERTS]), sb("chosen", [P, TILES, EXPERTS])
        top, total, inv = sb("top", [P, TILES, TOP_K]), sb("total", [P, TILES]), sb("inv_total", [P, TILES])
        ps = ctx.enter_context(nc.psum_tensor("ps_logits", [P, TILES, EXPERTS], F32))
        sem = nc.alloc_semaphore
        product, copied, exp_done, step = sem("logits_done"), sem("logits_copied"), sem("r_exp_done"), sem("route_step")
        block = ctx.enter_context(nc.Block())

        @block.tensor
        def _(pe):
            for i in range(TILES):
                toks = slice(i * P, (i + 1) * P)
                terms = [(x_hi, gw_hi), (x_lo, gw_hi), (x_hi, gw_lo)]
                for n, (k, (x, w)) in enumerate([(k, t) for k in range(KD) for t in terms]):
                    last = nc.tensor.matmul(ps[:, i, :], x[:, k, toks], w[:, k, :], start=(n == 0), stop=(n == 3 * KD - 1))
            last.then_inc(product, 1)

        @block.scalar
        def _(act):
            act.wait_ge(product, 1)
            nc.scalar.copy(logits[:, :, :], ps[:, :, :]).then_inc(copied, 1)
            act.wait_ge(step, TILES + 1)
            nc.scalar.activation(weight[:, :, :], shifted[:, :, :], ACT.Exp).then_inc(exp_done, 1)

        @block.vector
        def _(dve):
            dve.wait_ge(copied, 1)
            for i in range(TILES):
                nc.vector.max(top[:, i, :], logits[:, i, :]).then_inc(step, 1)
            dve.wait_ge(step, TILES)
            nc.vector.tensor_tensor(shifted[:, :, :], logits[:, :, :], top[:, :, 0:1].to_broadcast([P, TILES, EXPERTS]), ALU.subtract).then_inc(step, 1)
            for i in range(TILES):
                nc.vector.match_replace(rest[:, i, :], top[:, i, :], logits[:, i, :], TAKEN).then_inc(step, 1)
            dve.wait_ge(step, 2 * TILES + 1)
            nc.vector.tensor_single_scalar(chosen[:, :, :], rest[:, :, :], TAKEN, ALU.is_equal).then_inc(step, 1)
            dve.wait_ge(step, 2 * TILES + 2)
            dve.wait_ge(exp_done, 1)
            nc.vector.tensor_tensor(routing[:, :, :], weight[:, :, :], chosen[:, :, :], ALU.mult).then_inc(step, 1)
            dve.wait_ge(step, 2 * TILES + 3)
            nc.vector.reduce_sum(total[:, :], routing[:, :, :], AX.X).then_inc(step, 1)
            dve.wait_ge(step, 2 * TILES + 4)
            nc.vector.reciprocal(inv[:, :], total[:, :]).then_inc(step, 1)
            dve.wait_ge(step, 2 * TILES + 5)
            nc.vector.tensor_tensor(routing[:, :, :], routing[:, :, :], inv[:, :].unsqueeze(2).to_broadcast([P, TILES, EXPERTS]), ALU.mult)


def experts(nc, x_res, x_hi, x_lo, routing, w_gu, w_dn, lut, idx, w_ffn):
    RUNS = 2 * GROUPS
    SUB = GROUP // P
    TERMS = LUT // 2
    PARTS = 3
    BODIES = EXPERTS // 2
    with ExitStack() as ctx:
        sb = lambda n, s, dt=F32: ctx.enter_context(nc.sbuf_tensor(n, s, dt))
        raw_gu, raw_dn = [sb(f"raw_gu{b}", [P, KD, 2 * INTER_E]) for b in range(2)], [sb(f"raw_dn{b}", [P, 2, D]) for b in range(2)]
        gu_hi, gu_lo = [sb(f"gu_hi{b}", [P, KD, 2 * INTER_E], F32R) for b in range(2)], [sb(f"gu_lo{b}", [P, KD, 2 * INTER_E], F32R) for b in range(2)]
        dn_hi, dn_lo = [sb(f"dn_hi{b}", [P, 2, D], F32R) for b in range(2)], [sb(f"dn_lo{b}", [P, 2, D], F32R) for b in range(2)]
        silu = sb("m_silu", [P, 2, GROUP])
        h = sb("m_h", [P, 2, GROUP])
        lut_all, entry = sb("lut_all", [P, LUT]), sb("lut_entry", [P, TERMS, LOOKUP])
        idx_st, looked_up = [sb(f"idx_st{b}", [P, LOOKUP], mybir.dt.int32) for b in range(2)], sb("looked_up", [P, LOOKUP])
        h_hi, h_lo = [sb(f"m_h_hi{b}", [P, 2, GROUP], F32R) for b in range(2)], [sb(f"m_h_lo{b}", [P, 1, GROUP], F32R) for b in range(2)]
        pb = lambda n: ctx.enter_context(nc.psum_tensor(n, [P, 512], F32))
        ps_g, ps_u, ps_r, ps_o = [[pb(f"m_ps_{c}{b}") for b in range(2)] for c in "guro"]
        sem = nc.alloc_semaphore
        loaded = [sem(f"m_loaded{b}") for b in range(2)]
        w_hi_done, w_lo_done, up_done, silu_done, h_done, hi_done, lo_done, down_done, added = [
            sem("m_" + n) for n in ("w_hi_done", "w_lo_done", "up_done", "silu_done", "h_done", "hi_done", "lo_done", "down_done", "added")]
        idx_loaded = [sem(f"idx_loaded{b}") for b in range(2)]
        lut_loaded, terms_ready, summed, w_stored, lookups_begun = [
            sem(n) for n in ("lut_loaded", "lut_terms_ready", "lut_terms_summed", "w_ffn_stored", "lookups_begun")]
        assert EXPERTS * GROUPS == 2 * LOOKUPS
        block = ctx.enter_context(nc.Block())

        @block.gpsimd
        def _(pool):
            pool.dma_start(lut_all[:, :], lut.partition_broadcast(P)).then_inc(lut_loaded, 16)
            pool.sem_inc(summed, 1)

            def load_idx(c, b):
                pool.dma_start(idx_st[b][:, :], idx[bass.ds(c, 1), :, :].rearrange("c p j -> p (c j)")).then_inc(idx_loaded[b], 16)

            def sum_up(it, b, first, final):
                c = it * 2 + b
                if not (first and b == 0):
                    pool.wait_ge(w_stored, c * 16)
                    pool.sem_inc(lookups_begun, 1)
                for e in range(1, LUT):
                    if e in (1, TERMS):
                        pool.wait_ge(terms_ready, c * 2 + e // TERMS + 1)
                        pool.sem_inc(lookups_begun, 1)
                    so_far = entry[:, 0, :]
                    if e > 1:
                        so_far = looked_up[:, :]
                        pool.wait_ge(summed, c * (LUT - 1) + e)
                    nc.gpsimd.tensor_tensor(looked_up[:, :], so_far, entry[:, e % TERMS, :], ALU.add).then_inc(summed, 1)
                pool.wait_ge(summed, (c + 1) * (LUT - 1) + 1)
                pool.sem_inc(lookups_begun, 1)
                pool.dma_start(w_ffn[bass.ds(c, 1), :, :].rearrange("c p j -> p (c j)"), looked_up[:, :]).then_inc(w_stored, 16)
                if not final:
                    load_idx(c + 2, b)

            for b in range(2):
                load_idx(b, b)
            for b in range(2):
                sum_up(0, b, True, False)
            with pool.Fori(1, LOOKUPS // 2 - 1) as it:
                for b in range(2):
                    sum_up(it, b, False, False)
            for b in range(2):
                sum_up(LOOKUPS // 2 - 1, b, False, True)
            pool.wait_ge(w_stored, 16 * LOOKUPS)

        @block.sync
        def _(sp):
            with sp.Fori(0, BODIES) as it:
                for b in range(2):
                    e = it * 2 + b
                    sp.wait_ge(w_lo_done, e + 1)
                    sp.dma_start(raw_gu[b][:, :, :], w_gu[bass.ds(e, 1), :, :].rearrange("e (k p) i -> p (e k) i", p=P)).then_inc(loaded[b], 16)
                    sp.dma_start(raw_dn[b][:, 0, :], w_dn[bass.ds(e, 1), 0:P, :].rearrange("e i d -> i (e d)")).then_inc(loaded[b], 16)
                    for half in range(2):
                        sp.dma_start(raw_dn[b][half * REST_E:(half + 1) * REST_E, 1, :], w_dn[bass.ds(e, 1), P:INTER_E, :].rearrange("e i d -> i (e d)")).then_inc(loaded[b], 16)

        @block.tensor
        def _(pe):
            pe.sem_inc(down_done, 2 * SUB)

            def up(it, r):
                n, b, g, r2 = it * RUNS + r, (r // GROUPS) % 2, r % GROUPS, r % 2
                if g == 0:
                    pe.wait_ge(w_lo_done, it * 2 + r // GROUPS + 3)
                pe.wait_ge(h_done, n + 1)
                for ps, c0 in ((ps_g, 0), (ps_u, P), (ps_r, 2 * P)):
                    terms = [(gu_hi[b], x_hi), (gu_lo[b], x_hi), (gu_hi[b], x_lo)]
                    for m, (k, (w, x)) in enumerate([(k, t) for k in range(KD) for t in terms]):
                        last = nc.tensor.matmul(ps[r2][:, :], w[:, k, c0:c0 + P], x[:, k, g * GROUP:(g + 1) * GROUP],
                                                start=(m == 0), stop=(m == 3 * KD - 1))
                last.then_inc(up_done, 1)

            def down(it, r):
                n, b, r2 = it * RUNS + r, r // GROUPS, r % 2
                pe.wait_ge(lo_done, n + 2)
                for s in range(SUB):
                    pe.wait_ge(added, n * SUB + s + 1)
                    toks = slice(s * P, (s + 1) * P)
                    terms = [(h_hi[r2], dn_hi[b], 0, P), (h_lo[r2], dn_hi[b], 0, P), (h_hi[r2], dn_lo[b], 0, P),
                             (h_hi[r2], dn_hi[b], 1, P), (h_hi[r2], dn_lo[b], 1, REST_E)]
                    for m, (a, w, k, rows) in enumerate(terms):
                        last = nc.tensor.matmul(ps_o[s % 2][:, :], a[:rows, k, toks], w[:rows, k, :], start=(m == 0), stop=(m == len(terms) - 1))
                    last.then_inc(down_done, 1)

            def body(it, final):
                for r in range(RUNS):
                    if not (final and r == RUNS - 1):
                        up(it, r + 1)
                    down(it, r)

            up(0, 0)
            with pe.Fori(0, BODIES - 1) as it:
                body(it, False)
            body(BODIES - 1, True)

        @block.scalar
        def _(act):
            act.sem_inc(silu_done, 1)

            def split_hi(loads, used, b, part):
                if part == 0:
                    act.wait_ge(loaded[b], loads * 64)
                    if used is not None:
                        act.wait_ge(down_done, used * SUB + 2 * SUB)
                if part < 2:
                    nc.scalar.copy(gu_hi[b][:, 2 * part:2 * part + 2, :], raw_gu[b][:, 2 * part:2 * part + 2, :]).then_inc(w_hi_done, 1)
                else:
                    nc.scalar.copy(dn_hi[b][:, :, :], raw_dn[b][:, :, :]).then_inc(w_hi_done, 1)

            def body(it, final):
                for r in range(RUNS):
                    n, r2 = it * RUNS + r, r % 2
                    act.wait_ge(up_done, n + 1)
                    act.wait_ge(h_done, n + 2)
                    nc.scalar.activation(silu[:, 0, :], ps_g[r2][:, :], ACT.Silu)
                    nc.scalar.activation(silu[P - REST_E:, 1, :], ps_r[r2][:REST_E, :], ACT.Silu).then_inc(silu_done, 1)
                    act.wait_ge(h_done, n + 3)
                    act.wait_ge(down_done, n * SUB + SUB)
                    nc.scalar.copy(h_hi[r2][:, 0, :], h[:, 0, :])
                    nc.scalar.copy(h_hi[r2][:REST_E, 1, :], h[:REST_E, 1, :]).then_inc(hi_done, 1)
                    if r % GROUPS < PARTS and not (final and r >= GROUPS):
                        split_hi(it + 1 + r // GROUPS, it * RUNS + r // GROUPS * GROUPS, 1 - r // GROUPS, r % GROUPS)

            for part in range(PARTS):
                split_hi(1, None, 0, part)
            with act.Fori(0, BODIES - 1) as it:
                body(it, False)
            body(BODIES - 1, True)

        @block.vector
        def _(dve):
            dve.sem_inc(h_done, 2)
            dve.sem_inc(added, 2)
            dve.sem_inc(w_lo_done, 2)
            dve.sem_inc(lo_done, 1)
            dve.wait_ge(lut_loaded, 16)

            def split_lo(e, b, part):
                dve.wait_ge(w_hi_done, e * PARTS + part + 1)
                if part < 2:
                    ks = slice(2 * part, 2 * part + 2)
                    nc.vector.tensor_tensor(gu_lo[b][:, ks, :], raw_gu[b][:, ks, :], gu_hi[b][:, ks, :].bitcast(F32), ALU.subtract)
                else:
                    nc.vector.tensor_tensor(dn_lo[b][:, :, :], raw_dn[b][:, :, :], dn_hi[b][:, :, :].bitcast(F32), ALU.subtract).then_inc(w_lo_done, 1)

            def add_run(it, r):
                n = it * RUNS + r
                for s in range(SUB):
                    i = (r % GROUPS) * SUB + s
                    dve.wait_ge(down_done, n * SUB + s + 1 + 2 * SUB)
                    nc.vector.scalar_tensor_tensor(x_res[:, i, :], ps_o[s % 2][:, :], routing[:, i, bass.ds(it * 2 + r // GROUPS, 1)],
                                                   x_res[:, i, :], ALU.mult, ALU.add).then_inc(added, 1)

            def lookup_terms(it, r):
                c, half = it * (RUNS // 2) + r // 2, r % 2
                if half == 0:
                    dve.wait_ge(idx_loaded[r // 2 % 2], (it * (RUNS // 4) + r // 4 + 1) * 16)
                dve.wait_ge(summed, c * (LUT - 1) + half * (TERMS - 1) + 1)
                for q in range(TERMS):
                    e = half * TERMS + q
                    last = nc.vector.tensor_scalar(entry[:, q, :], idx_st[r // 2 % 2][:, :], float(e), lut_all[:, e:e + 1], ALU.is_equal, ALU.mult)
                last.then_inc(terms_ready, 1)

            def body(it, final):
                for r in range(RUNS):
                    n, r2 = it * RUNS + r, r % 2
                    if r > 0:
                        add_run(it, r - 1)
                    dve.wait_ge(silu_done, n + 2)
                    dve.wait_ge(lo_done, n + 1)
                    nc.vector.tensor_tensor(h[:, 0, :], ps_u[r2][:, :], silu[:, 0, :], ALU.mult)
                    nc.vector.tensor_tensor(h[:REST_E, 1, :], ps_r[r2][P - REST_E:, :], silu[P - REST_E:, 1, :], ALU.mult).then_inc(h_done, 1)
                    dve.wait_ge(hi_done, n + 1)
                    nc.vector.tensor_tensor(h_lo[r2][:, 0, :], h[:, 0, :], h_hi[r2][:, 0, :].bitcast(F32), ALU.subtract)
                    nc.vector.tensor_tensor(h_hi[r2][P - REST_E:, 1, :], h[:REST_E, 1, :], h_hi[r2][:REST_E, 1, :].bitcast(F32),
                                            ALU.subtract).then_inc(lo_done, 1)
                    if r % GROUPS < PARTS and not (final and r >= GROUPS):
                        split_lo(it * 2 + 1 + r // GROUPS, 1 - r // GROUPS, r % GROUPS)
                    lookup_terms(it, r)
                add_run(it, RUNS - 1)

            for part in range(PARTS):
                split_lo(0, 0, part)
            with dve.Fori(0, BODIES - 1) as it:
                body(it, False)
            body(BODIES - 1, True)


STATE = 64
DHEAD = 64
S_HEADS = 16
D_INNER = S_HEADS * DHEAD
M_TILES = S_HEADS + S_HEADS // 2 + D_INNER // P
CHUNK_TOK = P // S_HEADS
CHUNKS = N_TOK // CHUNK_TOK
SEQ_TOK = N_TOK // 2 // S_HEADS
STEPS = SEQ_TOK // CHUNK_TOK
SEQS = 4
S_TOK = SEQS * SEQ_TOK
S_GROUPS = N_TOK // S_TOK


def state_space(nc, x_res, ident, w_proj, w_dt, w_out):
    proj = nc.dram_tensor("proj", (M_TILES, P, N_TOK), F32).ap()
    z_dram = nc.dram_tensor("z_dt", (N_TOK, S_HEADS), F32).ap()
    cs_dram = nc.dram_tensor("log_decay", (CHUNKS, P), F32).ap()
    with ExitStack() as ctx:
        csT = ctx.enter_context(nc.sbuf_tensor("csT", [P, CHUNKS], F32))
        decay = ctx.enter_context(nc.sbuf_tensor("decay", [P, CHUNKS], F32))
        a_chunk = ctx.enter_context(nc.sbuf_tensor("a_chunk", [P, CHUNKS], F32))
        mask = ctx.enter_context(nc.sbuf_tensor("scan_mask", [P, P], F32))
        with ExitStack() as inner:
            x_hi = inner.enter_context(nc.sbuf_tensor("s_x_hi", [P, KD, N_TOK], F32R))
            x_lo = inner.enter_context(nc.sbuf_tensor("s_x_lo", [P, KD, N_TOK], F32R))
            layernorm_transposed(nc, "s_ln", x_res, x_hi, x_lo, ident)
            dt_hi = inner.enter_context(nc.sbuf_tensor("dt_hi", [P, KD, S_HEADS], F32R))
            dt_lo = inner.enter_context(nc.sbuf_tensor("dt_lo", [P, KD, S_HEADS], F32R))
            split_weights(nc, "dt", [(w_dt.rearrange("(k p) h -> p k h", p=P), dt_hi[:, :, :], dt_lo[:, :, :])])
            project_dt(nc, x_hi, x_lo, dt_hi, dt_lo, z_dram)
            project_tiles(nc, x_hi, x_lo, w_proj, proj, ident, z_dram, cs_dram, csT, decay, a_chunk, mask)
        scan(nc, x_res, ident, proj, cs_dram, csT, decay, a_chunk, mask, w_out)


def project_dt(nc, x_hi, x_lo, dt_hi, dt_lo, z_dram):
    with ExitStack() as ctx:
        z = ctx.enter_context(nc.sbuf_tensor("z_sb", [P, TILES, S_HEADS], F32))
        ps = ctx.enter_context(nc.psum_tensor("ps_z", [P, TILES, S_HEADS], F32))
        sem = nc.alloc_semaphore
        product, copied, stored = sem("z_product"), sem("z_copied"), sem("z_stored")
        block = ctx.enter_context(nc.Block())

        @block.tensor
        def _(pe):
            for i in range(TILES):
                toks = slice(i * P, (i + 1) * P)
                terms = [(x_hi, dt_hi), (x_lo, dt_hi), (x_hi, dt_lo)]
                for n, (k, (x, w)) in enumerate([(k, t) for k in range(KD) for t in terms]):
                    last = nc.tensor.matmul(ps[:, i, :], x[:, k, toks], w[:, k, :], start=(n == 0), stop=(n == 3 * KD - 1))
            last.then_inc(product, 1)

        @block.scalar
        def _(act):
            act.wait_ge(product, 1)
            nc.scalar.copy(z[:, :, :], ps[:, :, :]).then_inc(copied, 1)

        @block.sync
        def _(sp):
            sp.wait_ge(copied, 1)
            sp.dma_start(z_dram.rearrange("(n p) h -> p n h", p=P), z[:, :, :]).then_inc(stored, 16)
            sp.wait_ge(stored, 16)


def project_tiles(nc, x_hi, x_lo, w_proj, proj, ident, z_dram, cs_dram, csT, decay, a_chunk, mask):
    H = CHUNKS // P
    with ExitStack() as ctx:
        sb = lambda n, s, dt=F32: ctx.enter_context(nc.sbuf_tensor(n, s, dt))
        raw = [sb(f"s_raw{b}", [P, KD, P]) for b in range(2)]
        w_hi, w_lo = [sb(f"s_w_hi{b}", [P, KD, P], F32R) for b in range(2)], [sb(f"s_w_lo{b}", [P, KD, P], F32R) for b in range(2)]
        out = [sb(f"s_out{b}", [P, N_TOK]) for b in range(2)]
        ps = [[ctx.enter_context(nc.psum_tensor(f"s_ps{b}{g}", [P, GROUP], F32)) for g in range(GROUPS)] for b in range(2)]
        sem = nc.alloc_semaphore
        loaded, stored = [sem(f"s_loaded{b}") for b in range(2)], [sem(f"s_stored{b}") for b in range(2)]
        hi_done, lo_done, product, even_out, odd_out = sem("s_hi_done"), sem("s_lo_done"), sem("s_product"), sem("s_even_out"), sem("s_odd_out")
        HALF = GROUPS // 2
        stores_begun, splits_begun = sem("s_stores_begun"), sem("s_splits_begun")
        z, neg_abs, e, l, pos, la, cs, ones, cs_p = [sb("ld_" + n, [P, H, P]) for n in ("z", "neg_abs", "e", "l", "pos", "la", "cs", "ones", "cs_p")]
        order_int, order, order_col = sb("order_int", [P, P], I32), sb("order", [P, P]), sb("order_col", [P, 1])
        z_loaded, step, act_step, turned, cs_stored, numbered = [
            sem(n) for n in ("z_loaded", "decay_step", "decay_act_step", "decay_turned", "cs_stored", "positions_numbered")]
        ps_t, ps_l, ps_n = ps[0][0], ps[0][1], ps[0][2]
        block = ctx.enter_context(nc.Block())

        @block.sync
        def _(sp):
            def load(m, b):
                sp.dma_start(raw[b][:, :, :], w_proj[bass.ds(m, 1), :, :].rearrange("m (k p) c -> p (m k) c", p=P)).then_inc(loaded[b], 16)

            def store(m, b):
                sp.dma_start(proj[bass.ds(m, 1), :, :].rearrange("m p t -> p (m t)"), out[b][:, :]).then_inc(stored[b], 16)

            def body(it, final):
                for b in range(2):
                    m = it * 2 + b
                    if not final:
                        sp.wait_ge(lo_done, m + 1)
                        load(m + 2, b)
                    sp.wait_ge(even_out, (m + 3) * HALF)
                    sp.sem_inc(stores_begun, 1)
                    sp.wait_ge(odd_out, (m + 3) * HALF)
                    store(m, b)

            sp.dma_start(z[:, :, :], z_dram.rearrange("(a c t) h -> c a (t h)", a=H, t=CHUNK_TOK)).then_inc(z_loaded, 16)
            for b in range(2):
                load(b, b)
            sp.wait_ge(step, 8)
            sp.dma_start(cs_dram.rearrange("(a c) i -> c a i", a=H), cs_p[:, :, :]).then_inc(cs_stored, 16)
            with sp.Fori(0, M_TILES // 2 - 1) as it:
                body(it, False)
            body(M_TILES // 2 - 1, True)
            sp.wait_ge(cs_stored, 16)
            for b in range(2):
                sp.wait_ge(stored[b], 16 * (M_TILES // 2 + 1))

        @block.gpsimd
        def _(pool):
            pool.iota(order_int[:, :], pattern=[[1, S_HEADS], [S_HEADS, CHUNK_TOK]], base=0, channel_multiplier=0).then_inc(numbered, 1)
            with pool.Fori(0, M_TILES // 2) as it:
                for b in range(2):
                    m = it * 2 + b
                    pool.wait_ge(loaded[b], it * 16 + 16)
                    pool.sem_inc(splits_begun, 1)
                    pool.wait_ge(product, m * GROUPS + GROUPS)
                    pool.sem_inc(splits_begun, 1)
                    nc.gpsimd.tensor_copy(w_hi[b][:, :, :], raw[b][:, :, :]).then_inc(hi_done, 1)
                    pool.wait_ge(hi_done, m + 1)
                    nc.gpsimd.tensor_tensor(w_lo[b][:, :, :], raw[b][:, :, :], w_hi[b][:, :, :].bitcast(F32), ALU.subtract).then_inc(lo_done, 1)

        @block.tensor
        def _(pe):
            pe.sem_inc(product, 2 * GROUPS)
            with pe.Fori(0, M_TILES // 2) as it:
                for b in range(2):
                    m = it * 2 + b
                    pe.wait_ge(lo_done, m + 1)
                    for g in range(GROUPS):
                        pe.wait_ge(even_out if g % 2 == 0 else odd_out, m * HALF + g // 2 + 1)
                        terms = [(w_hi[b], x_hi), (w_lo[b], x_hi), (w_hi[b], x_lo)]
                        for n, (k, (w, x)) in enumerate([(k, t) for k in range(KD) for t in terms]):
                            last = nc.tensor.matmul(ps[b][g][:, :], w[:, k, :], x[:, k, g * GROUP:(g + 1) * GROUP],
                                                    start=(n == 0), stop=(n == 3 * KD - 1))
                        last.then_inc(product, 1)
            pe.wait_ge(even_out, (M_TILES + 2) * HALF)
            pe.wait_ge(odd_out, (M_TILES + 2) * HALF)
            pe.wait_ge(step, 8)
            for a in range(H):
                nc.tensor.transpose(ps_t[:, a * P:(a + 1) * P], cs_p[:, a, :], ident[:, :])
                nc.tensor.matmul(ps_l[:, a * P:(a + 1) * P], cs_p[:, a, P - 1:P].to_broadcast([P, P]), ident[:, :], start=True, stop=True)
            nc.tensor.transpose(ps_n[:, 0:P], order[:, :], ident[:, :]).then_inc(turned, 1)

        @block.scalar
        def _(act):
            for b in range(2):
                act.sem_inc(stored[b], 16)
            act.sem_inc(even_out, 2 * HALF)
            act.wait_ge(step, 2)
            nc.scalar.activation(e[:, :, :], neg_abs[:, :, :], ACT.Exp).then_inc(act_step, 1)
            act.wait_ge(act_step, 1)
            nc.scalar.activation(l[:, :, :], e[:, :, :], ACT.Ln, bias=1.0).then_inc(act_step, 1)
            with act.Fori(0, M_TILES // 2) as it:
                for b in range(2):
                    m = it * 2 + b
                    act.wait_ge(stored[b], it * 16 + 16)
                    for g in range(0, GROUPS, 2):
                        act.wait_ge(product, m * GROUPS + g + 1 + 2 * GROUPS)
                        nc.scalar.copy(out[b][:, g * GROUP:(g + 1) * GROUP], ps[b][g][:, :]).then_inc(even_out, 1)
            act.wait_ge(step, 11)
            nc.scalar.activation(a_chunk[:, :], ps_l[:, :CHUNKS], ACT.Exp)
            nc.scalar.activation(decay[:, :], decay[:, :], ACT.Exp)

        @block.vector
        def _(dve):
            dve.sem_inc(odd_out, 2 * HALF)
            nc.vector.memset(ones[:, :, :], 1.0).then_inc(step, 1)
            dve.wait_ge(z_loaded, 16)
            nc.vector.scalar_tensor_tensor(neg_abs[:, :, :], z[:, :, :], -1.0, z[:, :, :], ALU.mult, ALU.min).then_inc(step, 1)
            nc.vector.tensor_scalar_max(pos[:, :, :], z[:, :, :], 0.0).then_inc(step, 1)
            dve.wait_ge(numbered, 1)
            nc.vector.tensor_copy(order[:, :], order_int[:, :]).then_inc(step, 1)
            dve.wait_ge(act_step, 2)
            dve.wait_ge(step, 4)
            nc.vector.scalar_tensor_tensor(la[:, :, :], pos[:, :, :], -1.0, l[:, :, :], ALU.mult, ALU.subtract).then_inc(step, 1)
            dve.wait_ge(step, 5)
            for a in range(H):
                nc.vector.tensor_tensor_scan(cs[:, a, :], ones[:, a, :], la[:, a, :], 0.0, ALU.mult, ALU.add).then_inc(step, 1)
            dve.wait_ge(step, 7)
            nc.vector.tensor_copy(cs_p[:, :, :].rearrange("c a (h t) -> c a h t", t=CHUNK_TOK),
                                  cs[:, :, :].rearrange("c a (t h) -> c a h t", t=CHUNK_TOK)).then_inc(step, 1)
            with dve.Fori(0, M_TILES // 2) as it:
                for b in range(2):
                    m = it * 2 + b
                    dve.wait_ge(stored[b], it * 16 + 16)
                    for g in range(1, GROUPS, 2):
                        dve.wait_ge(product, m * GROUPS + g + 1 + 2 * GROUPS)
                        nc.vector.tensor_copy(out[b][:, g * GROUP:(g + 1) * GROUP], ps[b][g][:, :]).then_inc(odd_out, 1)
            dve.wait_ge(turned, 1)
            nc.vector.tensor_copy(csT[:, :], ps_t[:, :CHUNKS]).then_inc(step, 1)
            nc.vector.tensor_copy(order_col[:, :], ps_n[:, 0:1]).then_inc(step, 1)
            dve.wait_ge(step, 10)
            nc.vector.tensor_tensor(decay[:, :], ps_l[:, :CHUNKS], csT[:, :], ALU.subtract).then_inc(step, 1)
            nc.vector.tensor_scalar(mask[:, :], order[:, :], order_col[:, :], NEG, ALU.is_lt, ALU.mult)


def scan(nc, x_res, ident, proj, cs_dram, csT, decay, a_chunk, mask, w_out):
    N_POS = S_TOK * S_HEADS
    TT = S_TOK // P
    KO = D_INNER // P
    NC = SEQS * STEPS
    PAIRS = S_HEADS // 2
    with ExitStack() as ctx:
        sb = lambda n, s: ctx.enter_context(nc.sbuf_tensor(n, s, F32))
        bx_raw = sb("bx_raw", [P, S_HEADS, S_TOK])
        bx = [sb(f"bx{b}", [P, N_POS]) for b in range(2)]
        c_st = [sb(f"c_st{b}", [STATE, S_HEADS, S_TOK]) for b in range(2)]
        gate = [sb(f"gate{b}", [P, KO, S_TOK]) for b in range(2)]
        cs_all = sb("cs_all", [P, N_POS])
        c_dec = sb("c_dec", [STATE, N_POS])
        att = [sb(f"s_att{b}", [P, SEQS, P]) for b in range(2)]
        b_dec = [sb(f"b_dec{b}", [P, SEQS, STATE]) for b in range(2)]
        x_nat = [sb(f"x_nat{b}", [P, SEQS, DHEAD]) for b in range(2)]
        state = [sb(f"state{b}", [STATE, SEQS, DHEAD]) for b in range(2)]
        state_dec = sb("state_dec", [STATE, SEQS, DHEAD])
        gated = [sb(f"gated{b}", [P, KO, S_TOK]) for b in range(2)]
        w_o = sb("s_w_out_sb", [P, KO, D])
        pb = lambda n: ctx.enter_context(nc.psum_tensor(n, [P, 512], F32))
        ps_sc, ps_bx, ps_o = [[pb(f"s_ps_{c}{b}") for b in range(2)] for c in ("sc", "bx", "o")]
        ps_st, ps_y = pb("s_ps_st"), pb("s_ps_y")
        sem = nc.alloc_semaphore
        w_loaded, cs_loaded = sem("s_w_loaded"), sem("cs_loaded")
        loads_begun, turns_begun = sem("s_loads_begun"), sem("s_turns_begun")
        bx_loaded, bx_ready = sem("bx_loaded"), sem("bx_ready")
        c_loaded, gate_loaded = [[sem(f"{n}_loaded{b}") for b in range(2)] for n in ("c", "gate")]
        bx_done, sc_done, expo_done, exp_done, cdec_exp, cdec_done, silu_done = [
            sem(n) for n in ("bx_done", "sc_done", "expo_done", "s_exp_done", "cdec_exp", "cdec_done", "gate_silu_done")]
        x_out, b_out, att_done, st_done, dec_done, state_done, y_done, gated_done, o_done, o_added = [
            sem(n) for n in ("x_out", "b_out", "att_done", "st_done", "dec_done", "state_done", "y_mm_done", "gated_done", "o_done", "o_added_s")]
        block = ctx.enter_context(nc.Block())

        def chunk(buf, s, k):
            t0 = s * SEQ_TOK + k * CHUNK_TOK
            return buf[:, :, t0:t0 + CHUNK_TOK]

        last_group = lambda it, b: (it, 0) if b == 1 else (it - 1, 1)

        @block.sync
        def _(sp):
            sp.dma_start(w_o[:, :, :], w_out.rearrange("(k p) d -> p k d", p=P)).then_inc(w_loaded, 16)
            with sp.Fori(0, S_GROUPS // 2) as it:
                for b in range(2):
                    g = it * 2 + b
                    toks = bass.ds(g * S_TOK, S_TOK)
                    sp.wait_ge(bx_ready, g + 1)
                    sp.sem_inc(loads_begun, 1)
                    sp.dma_start(bx_raw[:, :, :], proj[0:S_HEADS, :, toks].rearrange("h p t -> p h t")).then_inc(bx_loaded, 16)
                    sp.wait_ge(sc_done, g * STEPS + STEPS)
                    sp.sem_inc(loads_begun, 1)
                    sp.dma_start(c_st[b][:, :, :], proj[S_HEADS:S_HEADS + PAIRS, :, toks].rearrange("m (two p) t -> p (m two) t", two=2)).then_inc(c_loaded[b], 16)
                    sp.wait_ge(gated_done, g * STEPS + STEPS)
                    sp.sem_inc(loads_begun, 1)
                    sp.dma_start(gate[b][:, :, :], proj[S_HEADS + PAIRS:M_TILES, :, toks].rearrange("m p t -> p m t")).then_inc(gate_loaded[b], 16)
                    sp.wait_ge(expo_done, g * STEPS + 1)
                    sp.sem_inc(loads_begun, 1)
                    sp.wait_ge(cdec_exp, g + 1)
                    sp.sem_inc(loads_begun, 1)
                    rows = cs_dram[bass.ds(g * NC, NC), :].rearrange("c i -> (c i)")
                    sp.dma_start(cs_all[:, :], rows.partition_broadcast(P)).then_inc(cs_loaded, 16)

        @block.gpsimd
        def _(pool):
            pool.sem_inc(bx_ready, 1)

            def lay_out(it, b):
                g = it * 2 + b
                pool.wait_ge(bx_loaded, g * 16 + 16)
                pool.sem_inc(turns_begun, 1)
                pool.wait_ge(sc_done, g * STEPS + STEPS)
                pool.sem_inc(turns_begun, 1)
                nc.gpsimd.tensor_copy(bx[b][:, :].rearrange("p (c h t) -> p c h t", h=S_HEADS, t=CHUNK_TOK),
                                      bx_raw[:, :, :].rearrange("p h (c t) -> p c h t", t=CHUNK_TOK)).then_inc(bx_ready, 1)

            def decay_c(it, b):
                pool.wait_ge(cdec_exp, it * 2 + b + 2)
                pool.sem_inc(turns_begun, 1)
                pool.wait_ge(c_loaded[b], it * 16 + 16)
                pool.sem_inc(turns_begun, 1)
                by_head = c_dec[:, :].rearrange("p (c h t) -> p h c t", h=S_HEADS, t=CHUNK_TOK)
                nc.gpsimd.tensor_tensor(by_head, by_head, c_st[b][:, :, :].rearrange("p h (c t) -> p h c t", t=CHUNK_TOK), ALU.mult).then_inc(cdec_done, 1)

            def body(it, final):
                decay_c(it, 0)
                lay_out(it, 1)
                decay_c(it, 1)
                if not final:
                    lay_out(it + 1, 0)

            lay_out(0, 0)
            with pool.Fori(0, S_GROUPS // 2 - 1) as it:
                body(it, False)
            body(S_GROUPS // 2 - 1, True)

        @block.tensor
        def _(pe):
            pe.sem_inc(sc_done, 2 * STEPS)
            pe.sem_inc(y_done, 2)
            pe.sem_inc(o_done, 2 * TT)
            pe.wait_ge(w_loaded, 16)

            def prepare(it, b, k):
                g = it * 2 + b
                n = g * STEPS + k
                if k == 0:
                    pe.wait_ge(bx_ready, g + 2)
                pe.wait_ge(b_out, n + 1)
                for s in range(SEQS):
                    last = nc.tensor.transpose(ps_bx[k % 2][:, s * P:(s + 1) * P], bx[b][:, (s * STEPS + k) * P:(s * STEPS + k + 1) * P], ident[:, :])
                last.then_inc(bx_done, 1)
                if k == 0:
                    pe.wait_ge(c_loaded[b], it * 16 + 16)
                pe.wait_ge(att_done, n + 1)
                for s in range(SEQS):
                    last = nc.tensor.matmul(ps_sc[k % 2][:, s * P:(s + 1) * P], bx[b][:STATE, (s * STEPS + k) * P:(s * STEPS + k + 1) * P], chunk(c_st[b], s, k), start=True, stop=True)
                last.then_inc(sc_done, 1)

            def new_states(it, b, k):
                g = it * 2 + b
                n = g * STEPS + k
                pe.wait_ge(b_out, n + 3)
                pe.wait_ge(state_done, g * (STEPS - 1) + k + 1)
                for s in range(SEQS):
                    last = nc.tensor.matmul(ps_st[:STATE, s * DHEAD:(s + 1) * DHEAD], b_dec[k % 2][:, s, :], x_nat[k % 2][:, s, :], start=True, stop=True)
                last.then_inc(st_done, 1)

            def outputs(it, b, k):
                g = it * 2 + b
                n = g * STEPS + k
                if k == 1:
                    pe.wait_ge(cdec_done, g + 1)
                if k > 0:
                    pe.wait_ge(state_done, g * (STEPS - 1) + k + 1)
                pe.wait_ge(gated_done, n + 2 * STEPS)
                pe.wait_ge(att_done, n + 3)
                pe.wait_ge(b_out, n + 3)
                for s in range(SEQS):
                    c0 = (s * STEPS + k) * P
                    dst = ps_y[:DHEAD, s * P:(s + 1) * P]
                    last = nc.tensor.matmul(dst, x_nat[k % 2][:, s, :], att[k % 2][:, s, :], start=True, stop=(k == 0))
                    if k > 0:
                        last = nc.tensor.matmul(dst, state[k % 2][:, s, :], c_dec[:, c0:c0 + P], start=False, stop=True)
                last.then_inc(y_done, 1)

            def project_out(it, b, part):
                g = it * 2 + b
                per = TT * KO // STEPS
                tt, k0 = divmod(part * per, KO)
                if part == 0:
                    pe.wait_ge(gated_done, g * STEPS + 3 * STEPS)
                if k0 == 0:
                    pe.wait_ge(o_added, g * TT + tt + 1)
                for k in range(k0, k0 + per):
                    last = nc.tensor.matmul(ps_o[tt][:, :], gated[b][:, k, tt * P:(tt + 1) * P], w_o[:, k, :], start=(k == 0), stop=(k == KO - 1))
                if k0 + per == KO:
                    last.then_inc(o_done, 1)

            def body(it, first):
                for b in range(2):
                    prepare(it, b, 0)
                    for k in range(STEPS):
                        if k + 1 < STEPS:
                            prepare(it, b, k + 1)
                            new_states(it, b, k)
                        if not (first and b == 0):
                            project_out(*last_group(it, b), k)
                        outputs(it, b, k)

            body(0, True)
            with pe.Fori(1, S_GROUPS // 2) as it:
                body(it, False)
            for k in range(STEPS):
                project_out(S_GROUPS // 2 - 1, 1, k)

        @block.scalar
        def _(act):
            act.sem_inc(cdec_exp, 1)
            act.sem_inc(x_out, 2)
            with act.Fori(0, S_GROUPS // 2) as it:
                for b in range(2):
                    g = it * 2 + b
                    act.wait_ge(cs_loaded, g * 16 + 16)
                    act.wait_ge(y_done, g * STEPS + 2)
                    nc.scalar.activation(c_dec[:, :], cs_all[:STATE, :], ACT.Exp).then_inc(cdec_exp, 1)
                    for k in range(STEPS):
                        n = g * STEPS + k
                        act.wait_ge(bx_done, n + 1)
                        act.wait_ge(y_done, n + 1)
                        nc.scalar.copy(x_nat[k % 2][:, :, :], ps_bx[k % 2][:, :].rearrange("p (s c) -> p s c", s=SEQS)[:, :, STATE:]).then_inc(x_out, 1)
                        act.wait_ge(expo_done, n + 2)
                        nc.scalar.activation(att[k % 2][:, :, :], att[k % 2][:, :, :], ACT.Exp).then_inc(exp_done, 1)
                        if k == 0:
                            act.wait_ge(gate_loaded[b], it * 16 + 16)
                            nc.scalar.activation(gate[b][:, :, :], gate[b][:, :, :], ACT.Silu).then_inc(silu_done, 1)

        @block.vector
        def _(dve):
            dve.sem_inc(expo_done, 1)
            dve.sem_inc(b_out, 2)
            dve.sem_inc(att_done, 2)
            dve.sem_inc(state_done, 1)
            dve.sem_inc(gated_done, 2 * STEPS)
            dve.sem_inc(o_added, 2)

            def add_out(it, b, tt):
                g = it * 2 + b
                dve.wait_ge(o_done, g * TT + tt + 1 + 2 * TT)
                row = x_res[:, bass.ds(g * TT + tt, 1), :]
                nc.vector.tensor_tensor(row, ps_o[tt][:, :], row, ALU.add).then_inc(o_added, 1)

            def weigh(it, b, k):
                g = it * 2 + b
                n = g * STEPS + k
                if k == 0:
                    dve.wait_ge(cs_loaded, g * 16 + 16)
                dve.wait_ge(y_done, n + 1)
                for s in range(SEQS):
                    c = s * STEPS + k
                    last = nc.vector.scalar_tensor_tensor(att[k % 2][:, s, :], cs_all[:, c * P:(c + 1) * P], csT[:, bass.ds(g * NC + c, 1)],
                                                          mask[:, :], ALU.subtract, ALU.add)
                last.then_inc(expo_done, 1)
                dve.wait_ge(x_out, n + 3)
                dec = decay[:, bass.ds(g * NC, NC)].rearrange("p (s k) -> p s k", s=SEQS)[:, :, k:k + 1]
                nc.vector.tensor_tensor(b_dec[k % 2][:, :, :], ps_bx[k % 2][:, :].rearrange("p (s c) -> p s c", s=SEQS)[:, :, :STATE],
                                        dec.to_broadcast([P, SEQS, STATE]), ALU.mult).then_inc(b_out, 1)
                dve.wait_ge(sc_done, n + 1 + 2 * STEPS)
                dve.wait_ge(exp_done, n + 1)
                nc.vector.tensor_tensor(att[k % 2][:, :, :], ps_sc[k % 2][:, :].rearrange("p (s c) -> p s c", s=SEQS), att[k % 2][:, :, :],
                                        ALU.mult).then_inc(att_done, 1)

            def update_state(it, b, k):
                g = it * 2 + b
                n = g * STEPS + k
                new = ps_st[:STATE, :SEQS * DHEAD].rearrange("p (s c) -> p s c", s=SEQS)
                if k > 0:
                    a = a_chunk[:STATE, bass.ds(g * NC, NC)].rearrange("p (s k) -> p s k", s=SEQS)[:, :, k:k + 1]
                    dve.wait_ge(state_done, g * (STEPS - 1) + k + 1)
                    nc.vector.tensor_tensor(state_dec[:, :, :], state[k % 2][:, :, :], a.to_broadcast([STATE, SEQS, DHEAD]), ALU.mult).then_inc(dec_done, 1)
                dve.wait_ge(y_done, n + 2)
                dve.wait_ge(st_done, g * (STEPS - 1) + k + 1)
                if k > 0:
                    dve.wait_ge(dec_done, g * (STEPS - 2) + k)
                    nc.vector.tensor_tensor(state[(k + 1) % 2][:, :, :], new, state_dec[:, :, :], ALU.add).then_inc(state_done, 1)
                else:
                    nc.vector.tensor_copy(state[1][:, :, :], new).then_inc(state_done, 1)

            def gate_outputs(it, b, k):
                g = it * 2 + b
                n = g * STEPS + k
                if k == 0:
                    dve.wait_ge(silu_done, g + 1)
                    dve.wait_ge(o_done, g * TT)
                dve.wait_ge(y_done, n + 3)
                y = ps_y[:DHEAD, :].rearrange("p (s h two t) -> p s h two t", s=SEQS, two=2, t=CHUNK_TOK)
                for parity in range(2):
                    half = slice(parity * DHEAD, (parity + 1) * DHEAD)
                    of_chunk = lambda buf: buf[half, :, :].rearrange("p h (s c t) -> p s c h t", s=SEQS, t=CHUNK_TOK)[:, :, k, :, :]
                    last = nc.vector.tensor_tensor(of_chunk(gated[b]), y[:, :, :, parity, :], of_chunk(gate[b]), ALU.mult)
                last.then_inc(gated_done, 1)

            def body(it, first):
                for b in range(2):
                    g = it * 2 + b
                    weigh(it, b, 0)
                    for k in range(STEPS):
                        if k + 1 < STEPS:
                            weigh(it, b, k + 1)
                            update_state(it, b, k)
                        gate_outputs(it, b, k)
                        if (k + 1) % (STEPS // TT) == 0 and not (first and b == 0):
                            add_out(*last_group(it, b), k // (STEPS // TT))

            body(0, True)
            with dve.Fori(1, S_GROUPS // 2) as it:
                body(it, False)
            for tt in range(TT):
                add_out(S_GROUPS // 2 - 1, 1, tt)


def lut_feed_forward(nc, x_res, ident, w_ffn):
    RUNS = 2 * GROUPS
    SUB = GROUP // P
    BODIES = (JT - 1) // 2
    PARTS = 3
    LAST_ROWS = INTER - (JT - 1) * P
    assert JT % 2 == 1
    flat = w_ffn.rearrange("c p j -> (c p j)")
    size = D * INTER
    gate, up = [flat[n * size:(n + 1) * size].rearrange("(k p i) -> p k i", p=P, i=INTER) for n in range(2)]
    down = flat[2 * size:3 * size].rearrange("(i d) -> i d", d=D)
    with ExitStack() as ctx:
        sb = lambda n, s, dt=F32: ctx.enter_context(nc.sbuf_tensor(n, s, dt))
        x_hi, x_lo = sb("f_x_hi", [P, KD, N_TOK], F32R), sb("f_x_lo", [P, KD, N_TOK], F32R)
        raw = [sb(f"f_raw{b}", [P, PARTS, 512]) for b in range(2)]
        w_hi, w_lo = [sb(f"f_w_hi{b}", [P, PARTS, 512], F32R) for b in range(2)], [sb(f"f_w_lo{b}", [P, PARTS, 512], F32R) for b in range(2)]
        silu, h = [sb(f"f_silu{b}", [P, GROUP]) for b in range(2)], [sb(f"f_h{b}", [P, GROUP]) for b in range(2)]
        h_hi, h_lo = [sb(f"f_h_hi{b}", [P, GROUP], F32R) for b in range(2)], [sb(f"f_h_lo{b}", [P, GROUP], F32R) for b in range(2)]
        layernorm_transposed(nc, "f_ln", x_res, x_hi, x_lo, ident)
        ps_g, ps_u = [[ctx.enter_context(nc.psum_tensor(f"f_ps_{c}{b}", [P, GROUP], F32)) for b in range(2)] for c in "gu"]
        ps_o = [ctx.enter_context(nc.psum_tensor(f"f_ps_o{s}", [P, D], F32)) for s in range(SUB)]
        sem = nc.alloc_semaphore
        loaded = [sem(f"f_loaded{b}") for b in range(2)]
        w_hi_done, w_lo_done, up_done, silu_done, h_done, hi_done, lo_done, down_done, added = [
            sem("f_" + n) for n in ("w_hi_done", "w_lo_done", "up_done", "silu_done", "h_done", "hi_done", "lo_done", "down_done", "added")]
        block = ctx.enter_context(nc.Block())
        runs_of = lambda final: GROUPS if final else RUNS
        rows_of = lambda it: LAST_ROWS if isinstance(it, int) and it == BODIES else P

        @block.sync
        def _(sp):
            def load(j, b, rows):
                sp.wait_ge(w_lo_done, j + 1)
                for part, w in ((0, gate), (1, up)):
                    dst = raw[b][:, part, :].rearrange("p (k i) -> p k i", i=P)[:, :, :rows]
                    sp.dma_start(dst, w[:, :, bass.ds(j * P, rows)]).then_inc(loaded[b], 16)
                sp.dma_start(raw[b][:rows, 2, :], down[bass.ds(j * P, rows), :]).then_inc(loaded[b], 16)

            with sp.Fori(0, BODIES) as it:
                for b in range(2):
                    load(it * 2 + b, b, P)
            load(2 * BODIES, 0, LAST_ROWS)

        @block.tensor
        def _(pe):
            pe.sem_inc(down_done, 2)

            def up_product(it, r):
                n, b, g, r2, rows = it * RUNS + r, r // GROUPS % 2, r % GROUPS, r % 2, rows_of(it)
                if g == 0:
                    pe.wait_ge(w_lo_done, it * 2 + r // GROUPS + 3)
                pe.wait_ge(h_done, n + 1)
                for ps, part in ((ps_g, 0), (ps_u, 1)):
                    terms = [(w_hi[b], x_hi), (w_lo[b], x_hi), (w_hi[b], x_lo)]
                    for m, (k, (w, x)) in enumerate([(k, t) for k in range(KD) for t in terms]):
                        last = nc.tensor.matmul(ps[r2][:rows, :], w[:, part, k * P:k * P + rows], x[:, k, g * GROUP:(g + 1) * GROUP],
                                                start=(m == 0), stop=(m == 3 * KD - 1))
                last.then_inc(up_done, 1)

            def down_product(it, r):
                n, b, r2, rows = it * RUNS + r, r // GROUPS, r % 2, rows_of(it)
                pe.wait_ge(lo_done, n + 1)
                for s in range(SUB):
                    pe.wait_ge(added, n * SUB + s + 1)
                    toks = slice(s * P, (s + 1) * P)
                    terms = [(h_hi[r2], w_hi[b]), (h_lo[r2], w_hi[b]), (h_hi[r2], w_lo[b])]
                    for m, (a, w) in enumerate(terms):
                        last = nc.tensor.matmul(ps_o[s][:, :], a[:rows, toks], w[:rows, 2, :], start=(m == 0), stop=(m == 2))
                last.then_inc(down_done, 1)

            def body(it, final):
                runs = runs_of(final)
                for r in range(runs):
                    if r + 1 < runs:
                        up_product(it, r + 1)
                    elif not final:
                        up_product(it + 1, 0)
                    down_product(it, r)

            up_product(0, 0)
            with pe.Fori(0, BODIES - 1) as it:
                body(it, False)
            body(BODIES - 1, False)
            body(BODIES, True)

        def split_next(split, it, r):
            j = it * 2 + r // GROUPS + 1
            last_tile = isinstance(it, int) and it == BODIES - 1 and r >= GROUPS
            split(j, it + 1 + r // GROUPS, (r // GROUPS + 1) % 2, r % GROUPS, LAST_ROWS if last_tile and r % GROUPS == 2 else P)

        @block.scalar
        def _(act):
            def split_hi(j, loads, b, part, rows):
                if part == 0:
                    act.wait_ge(loaded[b], loads * 48)
                    if not (isinstance(j, int) and j == 0):
                        act.wait_ge(down_done, (j - 1) * GROUPS + 2)
                nc.scalar.copy(w_hi[b][:rows, part, :], raw[b][:rows, part, :]).then_inc(w_hi_done, 1)

            def body(it, final):
                rows = rows_of(it)
                for r in range(runs_of(final)):
                    n, r2 = it * RUNS + r, r % 2
                    act.wait_ge(up_done, n + 1)
                    nc.scalar.activation(silu[r2][:rows, :], ps_g[r2][:rows, :], ACT.Silu).then_inc(silu_done, 1)
                    act.wait_ge(h_done, n + 3)
                    act.wait_ge(down_done, n + 1)
                    nc.scalar.copy(h_hi[r2][:rows, :], h[r2][:rows, :]).then_inc(hi_done, 1)
                    if r % GROUPS < PARTS and not final:
                        split_next(split_hi, it, r)

            for part in range(PARTS):
                split_hi(0, 1, 0, part, P)
            with act.Fori(0, BODIES - 1) as it:
                body(it, False)
            body(BODIES - 1, False)
            body(BODIES, True)

        @block.vector
        def _(dve):
            dve.sem_inc(h_done, 2)
            dve.sem_inc(added, SUB)
            dve.sem_inc(w_lo_done, 2)

            def split_lo(j, loads, b, part, rows):
                dve.wait_ge(w_hi_done, j * PARTS + part + 1)
                last = nc.vector.tensor_tensor(w_lo[b][:rows, part, :], raw[b][:rows, part, :], w_hi[b][:rows, part, :].bitcast(F32), ALU.subtract)
                if part == PARTS - 1:
                    last.then_inc(w_lo_done, 1)

            def add_run(it, r):
                n = it * RUNS + r
                dve.wait_ge(down_done, n + 3)
                for s in range(SUB):
                    i = (r % GROUPS) * SUB + s
                    nc.vector.tensor_tensor(x_res[:, i, :], ps_o[s][:, :], x_res[:, i, :], ALU.add).then_inc(added, 1)

            def body(it, final):
                rows = rows_of(it)
                runs = runs_of(final)
                for r in range(runs):
                    n, r2 = it * RUNS + r, r % 2
                    if r > 0:
                        add_run(it, r - 1)
                    dve.wait_ge(silu_done, n + 1)
                    nc.vector.tensor_tensor(h[r2][:rows, :], ps_u[r2][:rows, :], silu[r2][:rows, :], ALU.mult).then_inc(h_done, 1)
                    dve.wait_ge(hi_done, n + 1)
                    nc.vector.tensor_tensor(h_lo[r2][:rows, :], h[r2][:rows, :], h_hi[r2][:rows, :].bitcast(F32), ALU.subtract).then_inc(lo_done, 1)
                    if r % GROUPS < PARTS and not final:
                        split_next(split_lo, it, r)
                add_run(it, runs - 1)

            for part in range(PARTS):
                split_lo(0, 1, 0, part, P)
            with dve.Fori(0, BODIES - 1) as it:
                body(it, False)
            body(BODIES - 1, False)
            body(BODIES, True)


def build_program(nc, t, out):
    with ExitStack() as ctx:
        x_res = ctx.enter_context(nc.sbuf_tensor("x_res", [P, TILES, D], F32))
        ident = ctx.enter_context(nc.sbuf_tensor("ident", [P, P], F32))
        w_ffn = nc.dram_tensor("w_ffn", (LOOKUPS, P, LOOKUP), F32).ap()
        load_tokens(nc, t["x"], x_res, ident)
        if '1' in STAGES:
            attention(nc, x_res, ident, t["w_qkv"], t["b_qk"], t["b_v"], t["wo"], t["bo"])
        if '2' in STAGES:
            mixture_of_experts(nc, x_res, ident, t["gate_wT"], t["w_gu"], t["w_dn"], t["lut"], t["idx"], w_ffn)
        if '3' in STAGES:
            state_space(nc, x_res, ident, t["w_proj"], t["w_dt"], t["s_w_out"])
        if '4' in STAGES:
            lut_feed_forward(nc, x_res, ident, w_ffn)
        store_tokens(nc, x_res, out)


def scan_columns(w_in, w_param):
    import numpy as np
    param = w_param.reshape(S_HEADS, 1 + 2 * STATE, D)
    b_x = np.concatenate([param[:, 1:1 + STATE], w_in[:D_INNER].reshape(S_HEADS, DHEAD, D)], axis=1)
    c_pairs = param[:, 1 + STATE:].reshape(S_HEADS // 2, P, D)
    gate = w_in[D_INNER:].reshape(-1, P, D)
    return {
        "w_proj": np.ascontiguousarray(np.concatenate([b_x, c_pairs, gate]).transpose(0, 2, 1)),
        "w_dt": np.ascontiguousarray(param[:, 0].T),
    }


def expert_columns(gate, up):
    import numpy as np
    return np.ascontiguousarray(np.concatenate([gate[:, :P], up[:, :P], gate[:, P:], up[:, P:]], axis=1).transpose(0, 2, 1))


def lay_out(inputs):
    import numpy as np
    c = np.ascontiguousarray
    a = {k: np.asarray(v) for k, v in inputs.items()}
    return {
        "x": c(a["L0_attn_x"].reshape(N_TOK, D)),
        "w_qkv": c(np.concatenate([a["L0_attn_" + n].transpose(1, 0, 2).reshape(D, D) for n in ("Wq", "Wk", "Wv")], axis=1)),
        "b_qk": c(np.concatenate([a["L0_attn_" + n].reshape(D) for n in ("bq", "bk")]).reshape(-1, P).T),
        "b_v": c(a["L0_attn_bv"].reshape(D)),
        "wo": c(a["L0_attn_Wo"]),
        "bo": c(a["L0_attn_bo"]),
        "gate_wT": c(a["L0_ffn_gate_w"].T),
        "w_gu": expert_columns(a["L0_ffn_w_gate_proj"], a["L0_ffn_w_up_proj"]),
        "w_dn": c(a["L0_ffn_w_down_proj"].transpose(0, 2, 1)),
        **scan_columns(a["L1_attn_w_in"], a["L1_attn_w_param"]),
        "s_w_out": c(a["L1_attn_w_out"].T),
        "lut": c(a["L1_ffn_lut"]),
        "idx": c(np.concatenate([a["L1_ffn_" + n].T.reshape(-1) for n in ("gate_idx", "up_idx", "down_idx")]).reshape(LOOKUPS, P, LOOKUP)),
    }


def kernel(**inputs):
    import concourse.bacc as bacc
    from concourse.bass_utils import run_bass_kernel_spmd

    arrays = lay_out(inputs)
    nc = bacc.Bacc("TRN2", target_bir_lowering=False, num_devices=1)
    t = {n: nc.dram_tensor(n, a.shape, mybir.dt.from_np(a.dtype), kind="ExternalInput").ap() for n, a in arrays.items()}
    out = nc.dram_tensor("out", (N_TOK, D), F32, kind="ExternalOutput").ap()
    build_program(nc, t, out)
    r = run_bass_kernel_spmd(nc, [arrays], core_ids=[0])
    return r.results[0]["out"].reshape(2, N_TOK // 2, D)
```
